# Optimizing a Trainium2 kernel written in Bass

```python
import numpy as np
import jax
import jax.numpy as jnp

def _softmax(x, axis=-1):
    return jax.nn.softmax(x, axis=axis)

def _gelu(x):
    return jax.nn.gelu(x, approximate=True)

def _silu(x):
    return jax.nn.silu(x)

def _sigmoid(x):
    return jax.nn.sigmoid(x)

def _layernorm(x, axis=-1, eps=1e-05):
    m = jnp.mean(x, axis=axis, keepdims=True)
    v = jnp.var(x, axis=axis, keepdims=True)
    return (x - m) / jnp.sqrt(v + eps)

def _scatter_add(tgt, idx, src, axis=0):
    return tgt.at[idx].add(src)

def _segment_sum(src, seg, n):
    return jax.ops.segment_sum(src, seg, n)
kernel_name = 'mk_decoder_postln_d1_seqx_r8_f8d048'

def setup_inputs(seed: int=0):
    np.random.seed(seed)
    _w = jnp.asarray

    def _rec_inputs():
        import jax
        import jax.numpy as jnp
        _rk = jax.random.key(seed)
        x = 7.22e-05 + 1 * jax.random.normal(jax.random.fold_in(_rk, 1), (32, 56, 128), jnp.float32)
        _lenS = 56 - jax.random.randint(jax.random.fold_in(_rk, 7), (32,), 0, max(1, 56 // 4) + 1, jnp.int32)
        _lenS2 = 1500 - jax.random.randint(jax.random.fold_in(_rk, 8), (32,), 0, max(1, 1500 // 4) + 1, jnp.int32)
        _ctx_1024P = jax.random.normal(jax.random.fold_in(_rk, 11), (32, 16, 128), jnp.float32)
        _ctx_1024c = jax.random.dirichlet(jax.random.fold_in(_rk, 511), 0.3 * jnp.ones((16,), jnp.float32), (32, 1500))
        _ctx_1024t = jnp.einsum('bsk,bkd->bsd', _ctx_1024c, _ctx_1024P)
        _ctx_1024t = _ctx_1024t * jax.lax.rsqrt(jnp.mean(jnp.square(_ctx_1024t)) + 1e-12) * 0.953939
        ctx_1024 = 4.13588e-05 + 0.999923 * (_ctx_1024t + 0.3 * jax.random.normal(jax.random.fold_in(_rk, 611), (32, 1500, 128), jnp.float32))
        return (x, ctx_1024)
    x, ctx_1024 = _rec_inputs()

    def _L0_attn_setup():
        import jax, jax.numpy as jnp
        import numpy as np
        import math
        key = jax.random.key(seed)
        ks = jax.random.split(key, 10)
        b, n, d, h = (2, 128, 128, 16)
        hd = d // h
        std = 0.02
        x = jax.random.normal(ks[0], (b, n, d), jnp.float32)
        Wq = jax.random.normal(ks[1], (d, d), jnp.float32) * std
        Wk = jax.random.normal(ks[2], (d, d), jnp.float32) * std
        Wv = jax.random.normal(ks[3], (d, d), jnp.float32) * std
        Wo = jax.random.normal(ks[4], (d, d), jnp.float32) * std
        Ww1 = jax.random.normal(ks[5], (d, hd), jnp.float32) * std
        Ww2 = jax.random.normal(ks[6], (hd, d), jnp.float32) * std
        Wb = jax.random.normal(ks[7], (d, h), jnp.float32) * std
        Wf = jax.random.normal(ks[8], (d, h), jnp.float32) * std
        delta = jnp.full((h,), math.log(0.99 / (1.0 - 0.99)), jnp.float32)
        return dict(x=x, Wq=Wq, Wk=Wk, Wv=Wv, Wo=Wo, Ww1=Ww1, Ww2=Ww2, Wb=Wb, Wf=Wf, delta=delta)
    _L0_attn_all = _L0_attn_setup()
    _L0_attn_in = {k: v for k, v in _L0_attn_all.items() if k in ('Wq', 'Wk', 'Wv', 'Wo', 'Ww1', 'Ww2', 'Wb', 'Wf', 'delta')}
    del _L0_attn_all

    def _L0_xattn_setup():
        import jax, jax.numpy as jnp
        import numpy as np
        D = 128
        key = jax.random.key(seed)
        ks = jax.random.split(key, 9)
        B, S = (4, 256)
        s = 1.0 / np.sqrt(D)
        return {'query': jax.random.normal(ks[0], (B, S, D), jnp.float32), 'key': jax.random.normal(ks[1], (B, S, D), jnp.float32), 'value': jax.random.normal(ks[2], (B, S, D), jnp.float32), 'Wq': jax.random.normal(ks[3], (D, D), jnp.float32) * s, 'bq': jax.random.normal(ks[4], (D,), jnp.float32) * 0.01, 'Wk': jax.random.normal(ks[5], (D, D), jnp.float32) * s, 'bk': jax.random.normal(ks[6], (D,), jnp.float32) * 0.01, 'Wv': jax.random.normal(ks[7], (D, D), jnp.float32) * s, 'bv': jax.random.normal(ks[8], (D,), jnp.float32) * 0.01}
    _L0_xattn_all = _L0_xattn_setup()
    _L0_xattn_in = {k: v for k, v in _L0_xattn_all.items() if k in ('Wq', 'bq', 'Wk', 'bk', 'Wv', 'bv')}
    del _L0_xattn_all

    def _L0_ffn_setup():
        import jax, jax.numpy as jnp
        import numpy as np
        D = 128
        H = 16
        DK = D // H
        E = 8
        DFF = 4 * D
        TOPK = 2
        EPS = 1e-05

        def _layernorm(x, g, b):
            m = jnp.mean(x, axis=-1, keepdims=True)
            v = jnp.mean(jnp.square(x - m), axis=-1, keepdims=True)
            return (x - m) * jax.lax.rsqrt(v + EPS) * g + b
        key = jax.random.key(seed)
        ks = jax.random.split(key, 16)
        s_in = 1.0 / np.sqrt(D)
        s_ff = 1.0 / np.sqrt(DFF)
        return {'x': jax.random.normal(ks[0], (2, 256, D), dtype=jnp.float32), 'ln1_g': jnp.ones((D,), jnp.float32), 'ln1_b': jnp.zeros((D,), jnp.float32), 'w_qkv': jax.random.normal(ks[1], (D, 3 * D), jnp.float32) * s_in, 'b_qkv': jnp.zeros((3 * D,), jnp.float32), 'w_o': jax.random.normal(ks[2], (D, D), jnp.float32) * s_in, 'b_o': jnp.zeros((D,), jnp.float32), 'ln2_g': jnp.ones((D,), jnp.float32), 'ln2_b': jnp.zeros((D,), jnp.float32), 'gate_w': jax.random.normal(ks[3], (D, E), jnp.float32) * s_in, 'gate_b': jnp.zeros((E,), jnp.float32), 'W1': jax.random.normal(ks[4], (E, D, DFF), jnp.float32) * s_in, 'b1': jnp.zeros((E, DFF), jnp.float32), 'W2': jax.random.normal(ks[5], (E, DFF, D), jnp.float32) * s_ff, 'b2': jnp.zeros((E, D), jnp.float32)}
    _L0_ffn_all = _L0_ffn_setup()
    _L0_ffn_in = {k: v for k, v in _L0_ffn_all.items() if k in ('ln1_g', 'ln1_b', 'w_qkv', 'b_qkv', 'w_o', 'b_o', 'ln2_g', 'ln2_b', 'gate_w', 'gate_b', 'W1', 'b1', 'W2', 'b2')}
    del _L0_ffn_all
    return {'x': x, 'ctx_1024': ctx_1024, 'L0_attn_Wq': _L0_attn_in['Wq'], 'L0_attn_Wk': _L0_attn_in['Wk'], 'L0_attn_Wv': _L0_attn_in['Wv'], 'L0_attn_Wo': _L0_attn_in['Wo'], 'L0_attn_Ww1': _L0_attn_in['Ww1'], 'L0_attn_Ww2': _L0_attn_in['Ww2'], 'L0_attn_Wb': _L0_attn_in['Wb'], 'L0_attn_Wf': _L0_attn_in['Wf'], 'L0_attn_delta': _L0_attn_in['delta'], 'L0_xattn_Wq': _L0_xattn_in['Wq'], 'L0_xattn_bq': _L0_xattn_in['bq'], 'L0_xattn_Wk': _L0_xattn_in['Wk'], 'L0_xattn_bk': _L0_xattn_in['bk'], 'L0_xattn_Wv': _L0_xattn_in['Wv'], 'L0_xattn_bv': _L0_xattn_in['bv'], 'L0_ffn_ln1_g': _L0_ffn_in['ln1_g'], 'L0_ffn_ln1_b': _L0_ffn_in['ln1_b'], 'L0_ffn_w_qkv': _L0_ffn_in['w_qkv'], 'L0_ffn_b_qkv': _L0_ffn_in['b_qkv'], 'L0_ffn_w_o': _L0_ffn_in['w_o'], 'L0_ffn_b_o': _L0_ffn_in['b_o'], 'L0_ffn_ln2_g': _L0_ffn_in['ln2_g'], 'L0_ffn_ln2_b': _L0_ffn_in['ln2_b'], 'L0_ffn_gate_w': _L0_ffn_in['gate_w'], 'L0_ffn_gate_b': _L0_ffn_in['gate_b'], 'L0_ffn_W1': _L0_ffn_in['W1'], 'L0_ffn_b1': _L0_ffn_in['b1'], 'L0_ffn_W2': _L0_ffn_in['W2'], 'L0_ffn_b2': _L0_ffn_in['b2']}

def reference(x, ctx_1024, L0_attn_Wq, L0_attn_Wk, L0_attn_Wv, L0_attn_Wo, L0_attn_Ww1, L0_attn_Ww2, L0_attn_Wb, L0_attn_Wf, L0_attn_delta, L0_xattn_Wq, L0_xattn_bq, L0_xattn_Wk, L0_xattn_bk, L0_xattn_Wv, L0_xattn_bv, L0_ffn_ln1_g, L0_ffn_ln1_b, L0_ffn_w_qkv, L0_ffn_b_qkv, L0_ffn_w_o, L0_ffn_b_o, L0_ffn_ln2_g, L0_ffn_ln2_b, L0_ffn_gate_w, L0_ffn_gate_b, L0_ffn_W1, L0_ffn_b1, L0_ffn_W2, L0_ffn_b2):
    import jax
    import jax.numpy as jnp

    def _L0_attn_ref(x, Wq, Wk, Wv, Wo, Ww1, Ww2, Wb, Wf, delta):
        import jax, jax.numpy as jnp
        import numpy as np
        import math
        b, n, d = x.shape
        h = delta.shape[0]
        hd = d // h
        scale = hd ** (-0.5)
        q = (x @ Wq).reshape(b, n, h, hd)
        k = (x @ Wk).reshape(b, n, h, hd)
        v = (x @ Wv).reshape(b, n, h, hd)
        w = (x @ Ww1 @ Ww2).reshape(b, n, h, hd)
        w = w * jax.lax.rsqrt(jnp.sum(w * w, axis=-1, keepdims=True) + 1e-06)
        beta = 2.0 * jax.nn.sigmoid(x @ Wb)
        log_f = jax.nn.log_sigmoid((x @ Wf + delta).astype(jnp.float32))
        bt = jnp.transpose(beta, (0, 2, 1))
        A = jnp.einsum('bshd,brhd->bhsr', w, w)
        L = jnp.tril(A, -1) * bt[:, :, None, :]
        Mlow = jnp.tril(jnp.einsum('bshd,bjhd->bhsj', w, k), -1)
        C = jax.scipy.linalg.solve_triangular(L, Mlow, lower=True, unit_diagonal=True)
        G = jnp.tril(jnp.einsum('bthd,bshd->bhts', q, w) * bt[:, :, None, :])
        S = jnp.einsum('bthd,bjhd->bhtj', q, k) - G @ C
        Fc = jnp.cumsum(jnp.transpose(log_f, (0, 2, 1)), axis=-1)
        logits = S * scale + Fc[..., :, None] - Fc[..., None, :]
        mask = jnp.tril(jnp.ones((n, n), bool))
        logits = jnp.where(mask, logits, -jnp.inf)
        P = jax.nn.softmax(logits, axis=-1)
        o = jnp.einsum('bhtj,bjhd->bthd', P, v).reshape(b, n, d)
        return o @ Wo

    def _L0_xattn_ref(query, key, value, Wq, bq, Wk, bk, Wv, bv):
        import jax, jax.numpy as jnp
        import numpy as np
        D = 128
        scale = 1.0 / query.shape[-1] ** 0.5
        q = jnp.einsum('bsd,ed->bse', query, Wq) + bq
        k = jnp.einsum('bsd,ed->bse', key, Wk) + bk
        v = jnp.einsum('bsd,ed->bse', value, Wv) + bv
        scores = jnp.einsum('bqd,bkd->bqk', q, k) * scale
        w = jax.nn.softmax(scores, axis=-1)
        return jnp.einsum('bqk,bkd->bqd', w, v)

    def _L0_ffn_ref(x, ln1_g, ln1_b, w_qkv, b_qkv, w_o, b_o, ln2_g, ln2_b, gate_w, gate_b, W1, b1, W2, b2):
        import jax, jax.numpy as jnp
        import numpy as np
        D = 128
        H = 16
        DK = D // H
        E = 8
        DFF = 4 * D
        TOPK = 2
        EPS = 1e-05

        def _layernorm(x, g, b):
            m = jnp.mean(x, axis=-1, keepdims=True)
            v = jnp.mean(jnp.square(x - m), axis=-1, keepdims=True)
            return (x - m) * jax.lax.rsqrt(v + EPS) * g + b
        B, S, _ = x.shape
        h = _layernorm(x, ln1_g, ln1_b)
        qkv = h @ w_qkv + b_qkv
        q, k, v = jnp.split(qkv, 3, axis=-1)
        q = q.reshape(B, S, H, DK)
        k = k.reshape(B, S, H, DK)
        v = v.reshape(B, S, H, DK)
        scores = jnp.einsum('bqhd,bkhd->bhqk', q, k) / np.sqrt(DK)
        attn = jax.nn.softmax(scores, axis=-1)
        o = jnp.einsum('bhqk,bkhd->bqhd', attn, v).reshape(B, S, D)
        x = x + o @ w_o + b_o
        h = _layernorm(x, ln2_g, ln2_b).reshape(B * S, D)
        logits = h @ gate_w + gate_b
        topv, topi = jax.lax.top_k(logits, TOPK)
        gw = jax.nn.softmax(topv, axis=-1)
        ew = jnp.sum(jax.nn.one_hot(topi, E, dtype=h.dtype) * gw[..., None], axis=1)
        hid = jax.nn.relu(jnp.einsum('td,edf->etf', h, W1) + b1[:, None, :])
        out_e = jnp.einsum('etf,efd->etd', hid, W2) + b2[:, None, :]
        moe = jnp.einsum('etd,te->td', out_e, ew)
        return x + moe.reshape(B, S, D)
    x = _layernorm(x + _L0_attn_ref(x, L0_attn_Wq, L0_attn_Wk, L0_attn_Wv, L0_attn_Wo, L0_attn_Ww1, L0_attn_Ww2, L0_attn_Wb, L0_attn_Wf, L0_attn_delta), axis=-1)
    x = _layernorm(x + _L0_xattn_ref(x, ctx_1024, ctx_1024, L0_xattn_Wq, L0_xattn_bq, L0_xattn_Wk, L0_xattn_bk, L0_xattn_Wv, L0_xattn_bv), axis=-1)
    x = _layernorm(x + _L0_ffn_ref(x, L0_ffn_ln1_g, L0_ffn_ln1_b, L0_ffn_w_qkv, L0_ffn_b_qkv, L0_ffn_w_o, L0_ffn_b_o, L0_ffn_ln2_g, L0_ffn_ln2_b, L0_ffn_gate_w, L0_ffn_gate_b, L0_ffn_W1, L0_ffn_b1, L0_ffn_W2, L0_ffn_b2), axis=-1)
    return x

_drawn_inputs = setup_inputs


def setup_inputs(seed=0):
    import zlib

    import numpy as np

    out = dict(_drawn_inputs(seed))
    spreads = {'L0_attn_delta': (4.595119953155518, 0.6),
     'L0_ffn_ln1_g': (1.0, 0.2),
     'L0_ffn_ln1_b': (0.0, 0.1),
     'L0_ffn_b_qkv': (0.0, 0.1),
     'L0_ffn_b_o': (0.0, 0.1),
     'L0_ffn_ln2_g': (1.0, 0.2),
     'L0_ffn_ln2_b': (0.0, 0.1),
     'L0_ffn_gate_b': (0.0, 0.1),
     'L0_ffn_b1': (0.0, 0.333),
     'L0_ffn_b2': (0.0, 0.1)}
    factors = {'L0_attn_Wq': 8.0,
     'L0_attn_Wk': 8.0,
     'L0_attn_Ww1': 8.0,
     'L0_attn_Ww2': 8.0,
     'L0_attn_Wb': 21.503,
     'L0_attn_Wf': 46.564,
     'L0_xattn_bq': 8.0,
     'L0_xattn_bk': 64.0}
    for name, (base, spread) in spreads.items():
        noise = np.random.default_rng([zlib.crc32(name.encode()), seed]).standard_normal(out[name].shape)
        drawn = base * np.exp(spread * noise) if base else spread * noise
        out[name] = jnp.asarray(drawn.astype(out[name].dtype))
    for name, factor in factors.items():
        out[name] = (out[name] * factor).astype(out[name].dtype)
    return out
```

```python
from contextlib import ExitStack

import concourse.bass as bass
from concourse import mybir

F32 = mybir.dt.float32
ALU = mybir.AluOpType
ACT = mybir.ActivationFunctionType
AX = mybir.AxisListType

NB, NS, D, H = 32, 56, 128, 16
HD = D // H
NT = NB // 2
TP = 2 * NS
NTOK = NB * NS
CH = 4
CW = NTOK // CH
T8 = 8
NK = NS // T8
GB = NB // CH
HB = NB // 2
NCTX = 1500
NCC = 12
CR = NCTX // NCC
QP = 120
NE, FF = 8, 4 * D
FC = FF // 128
NEG = -1.0e30
EPS = 1e-05
SCALE_HD = float(HD) ** -0.5
SCALE_D = float(D) ** -0.5


def live(j, n):
    return not isinstance(j, int) or 0 <= j < n


def past(j, r):
    return not isinstance(j, int) or j >= r


def pipeline(eng, n, skew, lo, unroll, body):
    for i in range(lo):
        body(i, i % unroll)
    with eng.Fori(lo // unroll, n // unroll, 1) as r:
        for u in range(unroll):
            body(r * unroll + u, u)
    for i in range(n, n + skew):
        body(i, i % unroll)


def build(nc, a, out):
    ctx = ExitStack()
    with ctx:
        def sb(name, shape):
            return ctx.enter_context(nc.sbuf_tensor(name, shape, F32))

        def sem(name):
            return ctx.enter_context(nc.semaphore(name))

        ps = ctx.enter_context(nc.psum_tensor("ps", [128, 8, 512], F32))

        ident = sb("ident", [128, 128])
        blockones = sb("blockones", [128, 128])
        head_win = sb("head_win", [128, 15 * H])
        fc_win = sb("fc_win", [128, 15 * H])
        fc_neg = sb("fc_neg", [128, T8 * H])
        causal8 = sb("causal8", [128, T8])
        half_mask = sb("half_mask", [TP, 2 * HD])
        quad_mask = sb("quad_mask", [128, 4])
        ones_row = sb("ones_row", [1, TP])

        wq = sb("wq", [D, D]); wk = sb("wk", [D, D]); wv = sb("wv", [D, D]); wo = sb("wo", [D, D])
        ww1 = sb("ww1", [D, HD]); ww2 = sb("ww2", [HD, D])
        wbf = sb("wbf", [D, 2 * H]); wb_rep = sb("wb_rep", [D, D]); wf_rep = sb("wf_rep", [D, D])
        delta = sb("delta", [D, 1])
        eps_ww = sb("eps_ww", [128, 1]); eps_ln = sb("eps_ln", [128, 1]); minus_half = sb("minus_half", [128, 1])
        xw = sb("xw", [D, 3, D])
        xwqT = sb("xwqT", [D, D]); xwvT = sb("xwvT", [D, D])
        wqkv = sb("wqkv", [D, 3 * D]); w_o = sb("w_o", [D, D]); gate_w = sb("gate_w", [D, NE])
        cols = sb("cols", [D, 9])
        BQ, BK, G1, B1, FQ, FK, FV, G2, B2 = (cols[:, i:i + 1] for i in range(9))
        rows = sb("rows", [1, 2 * D + NE])
        rows_b = sb("rows_b", [TP, 2 * D + NE])
        BVR, BOR, GBR = rows_b[:, 0:D], rows_b[:, D:2 * D], rows_b[:, 2 * D:]
        b1_nat = sb("b1_nat", [NE * FC, 128]); b1T = sb("b1T", [128, NE * FC]); b1e = sb("b1e", [128, 2, FC])
        b2_nat = sb("b2_nat", [NE, D])
        w1r = sb("w1r", [D, 2, FF]); w2r = sb("w2r", [128, 2, FC, D])

        res = sb("res", [TP, NT, D])
        xT = sb("xT", [D, NTOK])
        v_nat = sb("v_nat", [TP, NT, D])
        acc = v_nat
        x2n = sb("x2n", [TP, NT, D])
        small = sb("small", [128, 4, 80])
        stage = sb("stage", [128, 4, 3, D])
        lg = sb("lg", [TP, NT, NE]); ew = sb("ew", [TP, NT, NE]); gt = sb("gt", [TP, 6, NT, NE])
        gs = sb("gs", [TP, 6, NT]); iota8 = sb("iota8", [TP, NE])

        class Region:
            def __init__(self, name, size):
                self.t, self.size = sb(name, [128, size]), size
                self.at = 0

            def take(self, n):
                self.at += n
                assert self.at <= self.size, (self.at, self.size)
                return self.t[:, self.at - n:self.at]

            def restart(self, at=0):
                self.at = at

        R1 = Region("R1", 7 * NTOK + 4 * NTOK)
        R2 = Region("R2", NK * NB * NS)
        qT, kT, wT, bwT, fcT, tmpA, tmpB = (R1.take(NTOK) for _ in range(7))
        halves = R1.at
        Tw = R1.take(2 * HB * NS).rearrange("p (h n) -> p h n", h=2)
        Xw = R1.take(2 * HB * NS).rearrange("p (h n) -> p h n", h=2)
        Tq = R1.take(4 * HB * NS).rearrange("p (h r n) -> p h r n", h=2, r=2)
        E = R2.take(NK * NB * NS).rearrange("p (k n) -> p k n", k=NK)
        R1.restart(halves)
        pa = R1.take(2 * NK * TP).rearrange("p (r n) -> p r n", r=2)
        paT = R1.take(2 * NK * 128).rearrange("p (r n) -> p r n", r=2)
        vpa = R1.take(4 * 640).rearrange("p (r b n) -> p r b n", r=2, b=2)
        oTa = R1.take(2 * TP).rearrange("p (r n) -> p r n", r=2)
        R1.restart(); R2.restart()
        ctxr = R1.take(4 * 2 * NCC * D).rearrange("p (r b n) -> p r b n", r=4, b=2)
        ctx_end = R1.at
        cT = R2.take(2 * 2 * NCTX).rearrange("p (r n) -> p r n", r=2)
        px = R2.take(2 * NCTX).rearrange("p (r n) -> p r n", r=2)
        pxT = R2.take(2 * NCC * QP).rearrange("p (r n) -> p r n", r=2)
        qx = sb("qx", [D, NTOK]); onx = sb("onx", [QP, 2, D])
        ewT = qx[0:NE, :]
        qxs = sb("qxs", [D, 2, TP]); qts = sb("qts", [D, 2, TP]); oxT = sb("oxT", [D, 2, TP])
        R1.restart()
        hs = R1.take(4 * 2 * TP).rearrange("p (r b n) -> p r b n", r=4, b=2)
        qs = R1.take(2 * TP).rearrange("p (r n) -> p r n", r=2)
        km = R1.take(2 * 4 * TP).rearrange("p (r f n) -> p r f n", r=2, f=4)
        pf = R1.take(2 * H * NS).rearrange("p (r n) -> p r n", r=2)
        pfT = R1.take(2 * 8 * QP).rearrange("p (r n) -> p r n", r=2)
        vpf = R1.take(4 * 2 * 384).rearrange("p (r b n) -> p r b n", r=4, b=2)
        ofT = R1.take(2 * TP).rearrange("p (r n) -> p r n", r=2)
        h2s = R1.take(4 * TP).rearrange("p (r n) -> p r n", r=4)
        R2.restart()
        hid = R2.take(2 * FC * CW).rearrange("p (r f n) -> p r f n", r=2, f=FC)

        fct8 = sb("fct8", [128, NB, NK])
        rowmax = sb("rowmax", [128, 2, NB]); rowsum = sb("rowsum", [128, NK, NB]); rinv = sb("rinv", [128, NK, NB])

        s_const = sem("s_const"); s_link = sem("s_link")
        s_x = sem("s_x"); s_w1 = sem("s_w1")
        s_rep = sem("s_rep")
        s_pe0 = sem("s_pe0"); s_ev0 = sem("s_ev0"); s_act0 = sem("s_act0"); s_dve0 = sem("s_dve0")
        s_T = sem("s_T"); s_U = sem("s_U"); s_X = sem("s_X"); s_K = sem("s_K"); s_Tq = sem("s_Tq"); s_S = sem("s_S")
        s_Sev = sem("s_Sev"); s_msk = sem("s_msk"); s_max = sem("s_max"); s_sub = sem("s_sub"); s_exp = sem("s_exp")
        s_sum = sem("s_sum"); s_rinv = sem("s_rinv"); s_fct = sem("s_fct"); s_fct8 = sem("s_fct8")
        s_zero = sem("s_zero"); s_v = sem("s_v"); s_vev = sem("s_vev")
        s_out = sem("s_out"); s_w2 = sem("s_w2"); s_prep = sem("s_prep"); s_prep_ev = sem("s_prep_ev")
        a_zero = sem("a_zero"); a_ps = sem("a_ps"); a_tr = sem("a_tr"); a_pt = sem("a_pt"); a_vp = sem("a_vp")
        a_pv = sem("a_pv"); a_o = sem("a_o"); a_wo = sem("a_wo"); a_y = sem("a_y"); a_st = sem("a_st"); a_mv = sem("a_mv")
        a_ln = sem("a_ln"); a_rs = sem("a_rs"); a_x1 = sem("a_x1"); a_xt = sem("a_xt"); a_xe = sem("a_xe"); a_rb = sem("a_rb")
        b_ctx = [sem(f"b_ctx{u}") for u in range(4)]
        b_qx = sem("b_qx"); b_qxe = sem("b_qxe"); b_qxs = sem("b_qxs"); b_qt = sem("b_qt"); b_qte = sem("b_qte"); b_qb = sem("b_qb")
        b_ct = sem("b_ct"); b_cta = sem("b_cta"); b_ctd = sem("b_ctd"); b_sc = sem("b_sc"); b_mx = sem("b_mx"); b_m2 = sem("b_m2")
        b_nb = sem("b_nb"); b_exp = sem("b_exp"); b_ptr = sem("b_ptr"); b_pte = sem("b_pte"); b_pv = sem("b_pv")
        b_rd = sem("b_rd"); b_on = sem("b_on"); b_ont = sem("b_ont"); b_one = sem("b_one"); b_wv = sem("b_wv"); b_y = sem("b_y")
        b_st = sem("b_st"); b_mv = sem("b_mv"); b_ln = sem("b_ln"); b_rs = sem("b_rs"); b_x2 = sem("b_x2"); b_st2 = sem("b_st2")
        b_mv2 = sem("b_mv2"); b_ln2 = sem("b_ln2"); b_rs2 = sem("b_rs2"); b_h = sem("b_h"); b_ht = sem("b_ht"); b_hte = sem("b_hte")
        b_rb = sem("b_rb")
        c_zero = sem("c_zero"); c_hs = sem("c_hs"); c_qkv = sem("c_qkv"); c_q = sem("c_q"); c_km = sem("c_km"); c_vp = sem("c_vp")
        c_sc = sem("c_sc"); c_mx = sem("c_mx"); c_sub = sem("c_sub"); c_exp = sem("c_exp"); c_sum = sem("c_sum"); c_ri = sem("c_ri")
        c_nrm = sem("c_nrm"); c_ptr = sem("c_ptr"); c_pte = sem("c_pte"); c_pv = sem("c_pv"); c_o = sem("c_o"); c_wo = sem("c_wo")
        c_y = sem("c_y"); c_st = sem("c_st"); c_mv = sem("c_mv"); c_ln = sem("c_ln"); c_rs = sem("c_rs"); c_h = sem("c_h")
        c_ht = sem("c_ht"); c_hte = sem("c_hte"); c_hx = sem("c_hx"); c_gt = sem("c_gt"); c_lg = sem("c_lg"); c_acc = sem("c_acc")
        m_link = sem("m_link"); m_e = sem("m_e"); m_ew = sem("m_ew"); m_ewt = sem("m_ewt"); m_ewe = sem("m_ewe"); m_b2 = sem("m_b2")
        m_b1 = sem("m_b1"); m_acc0 = sem("m_acc0"); m_w = [sem(f"m_w{u}") for u in range(2)]; m_hid = sem("m_hid"); m_relu = sem("m_relu")
        m_out = sem("m_out"); m_acc = sem("m_acc"); f_st = sem("f_st"); f_mv = sem("f_mv"); f_ln = sem("f_ln"); f_rs = sem("f_rs")
        f_y = sem("f_y")

        xflat = a["x"].rearrange("b n d -> (b n) d").rearrange("(i p) d -> p i d", p=TP)

        def tok(t):
            return t[:, :].rearrange("p (b n) -> p b n", n=NS)

        block = ctx.enter_context(nc.Block())

        @block.sync
        def _(sp):
            sp.dma_start(res[:, :, :], xflat).then_inc(s_x, 16)
            for t, n in ((wq, "Wq"), (wk, "Wk"), (ww1, "Ww1"), (ww2, "Ww2"), (wv, "Wv"), (wo, "Wo")):
                sp.dma_start(t[:, :], a["L0_attn_" + n]).then_inc(s_w1, 16)
            sp.dma_start(wbf[:, 0:H], a["L0_attn_Wb"]).then_inc(s_w1, 16)
            sp.dma_start(wbf[:, H:2 * H], a["L0_attn_Wf"]).then_inc(s_w1, 16)
            sp.dma_start(delta[:, :], a["L0_attn_delta"].rearrange("(h o) -> h o", o=1).broadcast_to([H, HD]).rearrange("h (d o) -> h d o", o=1)).then_inc(s_w1, 16)
            X, F = "L0_xattn_", "L0_ffn_"
            for t, n in ((xw[:, 0, :], X + "Wq"), (xw[:, 1, :], X + "Wv"), (xw[:, 2, :], X + "Wk"), (wqkv[:, :], F + "w_qkv"),
                         (w_o[:, :], F + "w_o"), (gate_w[:, :], F + "gate_w"), (b2_nat[:, :], F + "b2")):
                sp.dma_start(t, a[n]).then_inc(s_w2, 16)
            sp.dma_start(b1_nat[:, :], a[F + "b1"].rearrange("e (c f) -> (e c) f", f=128)).then_inc(s_w2, 16)
            bqkv = a[F + "b_qkv"].rearrange("(s d o) -> s d o", s=3, o=1)
            for t, v in ((BQ, a[X + "bq"]), (BK, a[X + "bk"]), (G1, a[F + "ln1_g"]), (B1, a[F + "ln1_b"]), (FQ, bqkv[0]),
                         (FK, bqkv[1]), (FV, bqkv[2]), (G2, a[F + "ln2_g"]), (B2, a[F + "ln2_b"])):
                sp.dma_start(t, v if len(v.shape) == 2 else v.rearrange("(d o) -> d o", o=1)).then_inc(s_w2, 16)
            for lo, v in ((0, a[X + "bv"]), (D, a[F + "b_o"]), (2 * D, a[F + "gate_b"])):
                sp.dma_start(rows[:, lo:lo + v.shape[0]], v.rearrange("(o d) -> o d", o=1)).then_inc(s_w2, 16)
            ctx_v = a["ctx_1024"].rearrange("(i two) (p c) d -> i p two (c d)", two=2, c=NCC)
            sp.wait_ge(s_S, 2 * NS)
            sp.wait_ge(s_K, 2 * (NS - 1))
            for i in range(4):
                sp.dma_start(ctxr[0:CR, i], ctx_v[i]).then_inc(b_ctx[i], 16)
            with sp.Fori(1, NT // 4, 1) as r:
                for u in range(4):
                    sp.wait_ge(b_pv, r * 4 + u - 3)
                    sp.wait_ge(s_S, 2 * NS)
                    sp.dma_start(ctxr[0:CR, u], ctx_v[r * 4 + u]).then_inc(b_ctx[u], 16)

            w1_v = a[F + "W1"]
            w2_v = a[F + "W2"].rearrange("e (c f) d -> e f c d", f=128)

            def expert(e, u):
                sp.dma_start(w1r[:, u, :], w1_v[e]).then_inc(m_w[u], 16)
                sp.dma_start(w2r[:, u], w2_v[e]).then_inc(m_w[u], 16)

            expert(0, 0)
            expert(1, 1)
            with sp.Fori(1, NE // 2, 1) as r:
                for u in range(2):
                    e = r * 2 + u
                    sp.wait_ge(m_w[u], 32)
                    sp.wait_ge(m_out, (e - 1) * CH)
                    expert(e, u)
            oflat = out.rearrange("b n d -> (b n) d").rearrange("(i p) d -> p i d", p=TP)
            sp.wait_ge(f_y, NT)
            sp.dma_start(oflat, acc[:, :, :]).then_inc(s_out, 16)
            sp.wait_ge(s_out, 16)

        NW1 = 9 * 16
        NW2 = 20 * 16

        def stat(u, lo, n=1, rows=TP):
            return small[0:rows, u % 4, lo:lo + n]

        ST1, MV1, LN1, RS1, ST2, MV2, LN2, RS2 = 0, 6, 8, 9, 10, 16, 18, 19
        MX, QB, M2, NBI, DEN, RDN, HMX, HSM, HRI = 20, 21, 22, 23, 24, 25, 26, 42, 58

        @block.gpsimd
        def _(pool):
            links = [0]

            def link(ins):
                links[0] += 1
                ins.then_inc(s_link, 1)
                pool.wait_ge(s_link, links[0])

            pool.memset(eps_ww[:, :], 1e-6)
            pool.memset(eps_ln[:, :], EPS)
            pool.memset(minus_half[:, :], -0.5)
            link(pool.memset(ident[:, :], 0.0))
            pool.affine_select(out=ident[:, :], in_=ident[:, :], compare_op=ALU.not_equal, fill=1.0,
                               base=0, pattern=[[-1, 128]], channel_multiplier=1).then_inc(s_const, 1)
            bo = blockones[:, :].rearrange("p (g d) -> p g d", d=HD)
            link(pool.memset(blockones[:, :], 1.0))
            link(pool.affine_select(out=bo, in_=bo, compare_op=ALU.is_ge, fill=0.0,
                                    base=0, pattern=[[-HD, H], [0, HD]], channel_multiplier=1))
            link(pool.affine_select(out=bo, in_=bo, compare_op=ALU.is_ge, fill=0.0,
                                    base=HD - 1, pattern=[[HD, H], [0, HD]], channel_multiplier=-1))
            link(pool.memset(head_win[:, :], 0.0))
            mid = slice(7 * H, 8 * H)
            link(pool.tensor_copy(head_win[:, mid], blockones[:, 0:D:HD]))
            link(pool.memset(fc_win[:, :], 0.0))
            link(pool.affine_select(out=fc_win[:, mid], in_=fc_win[:, mid], compare_op=ALU.not_equal, fill=1.0,
                                    base=0, pattern=[[-HD, H]], channel_multiplier=1))
            fn = fc_neg[:, :].rearrange("p (t h) -> p t h", t=T8)
            link(pool.memset(fc_neg[:, :], 0.0))
            link(pool.affine_select(out=fn, in_=fn, compare_op=ALU.not_equal, fill=-1.0,
                                    base=0, pattern=[[0, T8], [-HD, H]], channel_multiplier=1))
            link(pool.memset(causal8[:, :], 0.0))
            link(pool.affine_select(out=causal8[:, :], in_=causal8[:, :], compare_op=ALU.is_ge, fill=NEG,
                                    base=0, pattern=[[-H, T8]], channel_multiplier=1))
            link(pool.memset(half_mask[:, :], 1.0))
            link(pool.affine_select(out=half_mask[:, 0:HD], in_=half_mask[:, 0:HD], compare_op=ALU.is_ge, fill=0.0,
                                    base=NS - 1, pattern=[[0, HD]], channel_multiplier=-1))
            link(pool.affine_select(out=half_mask[:, HD:], in_=half_mask[:, HD:], compare_op=ALU.is_ge, fill=0.0,
                                    base=-NS, pattern=[[0, HD]], channel_multiplier=1))
            link(pool.tensor_copy(quad_mask[:, :], blockones[:, 0:4 * HD:HD]))
            for g in range(1, 4):
                link(pool.tensor_tensor(quad_mask[:, :], quad_mask[:, :], blockones[:, 4 * HD * g:4 * HD * (g + 1):HD], ALU.add))
            link(pool.iota(iota8[:, :], pattern=[[1, NE]], base=0, channel_multiplier=0, allow_small_or_imprecise_dtypes=True))
            pool.memset(ones_row[:, :], 1.0).then_inc(s_const, 1)
            pool.memset(E[:, :, :], 0.0).then_inc(s_const, 1)
            K, Q = tok(kT), tok(qT)
            pool.wait_ge(s_dve0, 4)
            for t in range(NS):
                W = T8 * (t // T8 + 1)
                for half in range(2):
                    bs = slice(half * HB, (half + 1) * HB)
                    if t > 0:
                        pool.wait_ge(s_K, 2 * (t - 1) + half + 1)
                    if t >= 2:
                        pool.wait_ge(s_S, 2 * (t - 2) + half + 1)
                    o = Tq[:, half, t % 2, 0:HB * W].rearrange("p (b j) -> p b j", j=W)
                    nc.gpsimd.tensor_tensor(o, K[:, bs, 0:W], Q[:, bs, t:t + 1].broadcast_to([128, HB, W]),
                                            ALU.mult).then_inc(s_Tq, 1)

            def rstd(var, eps_sum, out, mv, ln, rs, j):
                pool.wait_ge(mv, j + 1)
                nc.gpsimd.tensor_tensor(eps_sum, var, eps_ln[0:TP, :], ALU.add).then_inc(ln, 1)
                pool.wait_ge(ln, j + 1)
                nc.gpsimd.tensor_tensor(out, eps_sum, minus_half[0:TP, :], ALU.pow).then_inc(rs, 1)

            pool.wait_ge(s_S, 2 * NS)
            pool.wait_ge(s_K, 2 * (NS - 1))
            pool.memset(vpa, 0.0).then_inc(a_zero, 1)
            pool.wait_ge(a_zero, 1)
            pool.wait_ge(s_vev, 2)
            pool.wait_ge(s_prep_ev, 4)

            def body_a(i, u):
                if live(i, NT):
                    if past(i, 2):
                        pool.wait_ge(a_pv, i - 1)
                    for b in range(2):
                        nc.gpsimd.tensor_tensor(
                            vpa[0:TP, u % 2, b, :].rearrange("p (h c) -> p h c", c=5 * HD)[:, :, 0:HD],
                            v_nat[:, bass.ds(i, 1), :].rearrange("p i (h d) -> p (i h) d", d=HD),
                            half_mask[:, b * HD:(b + 1) * HD].unsqueeze(1).broadcast_to([TP, H, HD]),
                            ALU.mult).then_inc(a_vp, 1)
                j = i - 2
                if live(j, NT):
                    rstd(stat(u - 2, MV1 + 1), stat(u - 2, LN1), stat(u - 2, RS1), a_mv, a_ln, a_rs, j)
                    pool.wait_ge(a_x1, j + 1)
                    nc.gpsimd.tensor_tensor(res[:, bass.ds(j, 1), :].rearrange("p i d -> p (i d)"), stage[0:TP, (u - 2) % 4, 1, :], BVR,
                                            ALU.add).then_inc(a_rb, 1)

            pipeline(pool, NT, 3, 8, 4, body_a)

            def body_b(i, u):
                if live(i, NT):
                    pool.wait_ge(b_qxe, CH)
                    if past(i, 2):
                        pool.wait_ge(b_qt, i - 1)
                    nc.gpsimd.tensor_copy(qxs[:, u % 2, :], qx[:, bass.ts(i, TP)]).then_inc(b_qxs, 1)
                j = i - 4
                if live(j, NT):
                    x2 = stage[0:TP, u % 4, 1, :]
                    rstd(stat(u, MV1 + 1), stat(u, LN1), stat(u, RS1), b_mv, b_ln, b_rs, j)
                    rstd(stat(u, MV2 + 1), stat(u, LN2), stat(u, RS2), b_mv2, b_ln2, b_rs2, j)
                    pool.wait_ge(b_x2, j + 1)
                    nc.gpsimd.tensor_tensor(res[:, bass.ds(j, 1), :].rearrange("p i d -> p (i d)"), x2, BOR, ALU.add).then_inc(b_rb, 1)
                    nc.gpsimd.tensor_copy(x2n[:, bass.ds(j, 1), :].rearrange("p i d -> p (i d)"), x2).then_inc(b_rb, 1)

            pipeline(pool, NT, 5, 8, 4, body_b)

            pool.wait_ge(b_pv, NT)
            pool.memset(vpf, 0.0).then_inc(c_zero, 1)

            def body_c(i, u):
                if live(i, NT):
                    pool.wait_ge(b_hte, NT)
                    if past(i, 4):
                        pool.wait_ge(c_qkv, i - 3)
                    nc.gpsimd.tensor_copy(hs[:, u % 4, :, :].rearrange("p b (r n) -> p b r n", r=2),
                                          xT[:, bass.ts(i, TP)].rearrange("p (b n) -> p b n", b=2).unsqueeze(2)
                                          .broadcast_to([128, 2, 2, NS])).then_inc(c_hs, 1)
                j = i - 4
                if live(j, NT):
                    rstd(stat(u, MV1 + 1), stat(u, LN1), stat(u, RS1), c_mv, c_ln, c_rs, j)
                    pool.wait_ge(c_y, j + 1)
                    pool.wait_ge(b_rb, 2 * NT)
                    nc.gpsimd.tensor_tensor(acc[:, bass.ds(j, 1), :].rearrange("p i d -> p (i d)"), stage[0:TP, u % 4, 0, :],
                                            x2n[:, bass.ds(j, 1), :].rearrange("p i d -> p (i d)"), ALU.add).then_inc(c_acc, 1)
                j = i - 1
                if live(j, NT):
                    pool.wait_ge(c_ri, j + 1)
                    p = pf[0:QP, (u - 1) % 2, :].rearrange("p (h j) -> p h j", h=H)
                    nc.gpsimd.tensor_tensor(p, p, stat(u - 1, HRI, H, QP).unsqueeze(2).broadcast_to([QP, H, NS]),
                                            ALU.mult).then_inc(c_nrm, 1)
                j = i - 5
                if live(j, NT):
                    pool.wait_ge(c_hte, j + 1)
                    nc.gpsimd.tensor_copy(xT[:, bass.ts(j, TP)], h2s[:, (u - 5) % 4, :]).then_inc(c_hx, 1)

            pipeline(pool, NT, 6, 8, 4, body_c)
            pool.wait_ge(f_mv, NT)
            nc.gpsimd.tensor_tensor(gs[:, 1, :], gt[:, 1, :, 1], eps_ln[0:TP, :].broadcast_to([TP, NT]), ALU.add).then_inc(f_ln, 1)
            pool.wait_ge(f_ln, 1)
            nc.gpsimd.tensor_tensor(gs[:, 2, :], gs[:, 1, :], minus_half[0:TP, :].broadcast_to([TP, NT]), ALU.pow).then_inc(f_rs, 1)

        @block.scalar
        def _(act):
            def chunk(t, c):
                return t[:, c * CW:(c + 1) * CW]

            for c in range(CH):
                act.wait_ge(s_pe0, 1 + c)
                nc.scalar.copy(chunk(xT, c), ps[:, c, 0:CW]).then_inc(s_ev0, 1)
            for c in range(CH):
                act.wait_ge(s_pe0, 5 + c)
                nc.scalar.mul(chunk(qT, c), ps[:, 4 + c, 0:CW], SCALE_HD).then_inc(s_ev0, 1)
            for c in range(CH):
                act.wait_ge(s_pe0, 9 + c)
                nc.scalar.copy(chunk(kT, c), ps[:, c, 0:CW]).then_inc(s_ev0, 1)
            for c in range(CH):
                act.wait_ge(s_pe0, 13 + c)
                nc.scalar.copy(tmpA[0:HD, c * CW:(c + 1) * CW], ps[0:HD, 4 + c, 0:CW]).then_inc(s_ev0, 1)
            for c in range(CH):
                act.wait_ge(s_pe0, 17 + c)
                nc.scalar.copy(chunk(wT, c), ps[:, c, 0:CW])
                nc.scalar.activation(chunk(tmpB, c), ps[:, c, 0:CW], ACT.Square).then_inc(s_ev0, 1)
            for c in range(CH):
                act.wait_ge(s_pe0, 21 + c)
                nc.scalar.activation(chunk(bwT, c), ps[:, 4 + c, 0:CW], ACT.Exp, scale=-1.0).then_inc(s_ev0, 1)
            act.wait_ge(s_const, 1)
            for c in range(CH):
                act.wait_ge(s_pe0, 25 + c)
                nc.scalar.activation(chunk(tmpB, c), ps[:, c, 0:CW], ACT.Ln, bias=eps_ww[:, :]).then_inc(s_ev0, 1)
            act.wait_ge(s_ev0, 28)
            nc.scalar.activation(tmpB[:, :], tmpB[:, :], ACT.Exp, scale=-0.5).then_inc(s_act0, 1)
            act.wait_ge(s_dve0, 4)
            act.wait_ge(s_w1, NW1)
            for c in range(CH):
                act.wait_ge(s_pe0, 29 + c)
                nc.scalar.activation(chunk(fcT, c), ps[:, 4 + c, 0:CW], ACT.Identity, bias=delta[:, :]).then_inc(s_ev0, 1)
            act.wait_ge(s_ev0, 32)
            nc.scalar.activation(tmpA[:, :], fcT[:, :], ACT.Abs).then_inc(s_act0, 1)
            act.wait_ge(s_act0, 2)
            nc.scalar.activation(tmpA[:, :], tmpA[:, :], ACT.Exp, scale=-1.0).then_inc(s_act0, 1)
            act.wait_ge(s_act0, 3)
            nc.scalar.activation(tmpA[:, :], tmpA[:, :], ACT.Ln, bias=1.0).then_inc(s_act0, 1)

            for k in range(NK):
                W = T8 * (k + 1)
                act.wait_ge(s_sub, k + 1)
                e = E[:, k, :].rearrange("p (b j) -> p b j", j=NS)[:, :, 0:W]
                nc.scalar.activation(e, e, ACT.Exp).then_inc(s_exp, 1)

            def body_a(i, u):
                if live(i, NT):
                    act.wait_ge(a_tr, i + 1)
                    if past(i, 2):
                        act.wait_ge(a_pv, i - 1)
                    nc.scalar.copy(paT[0:TP, u % 2, :],
                                   ps[0:TP, 2 * (u % 2):2 * (u % 2) + 2, :].rearrange("p b n -> p (b n)")[:, 0:NK * 128])\
                        .then_inc(a_pt, 1)
                j = i - 1
                if live(j, NT):
                    act.wait_ge(a_pv, j + 1)
                    if past(j, 2):
                        act.wait_ge(a_wo, j - 1)
                    nc.scalar.copy(oTa[:, (u - 1) % 2, :], ps[:, 4 + (u - 1) % 2, 0:TP]).then_inc(a_o, 1)
                j = i - 3
                if live(j, NT):
                    act.wait_ge(a_xt, j + 1)
                    nc.scalar.copy(xT[:, bass.ts(j, TP)], ps[:, 7, 0:TP]).then_inc(a_xe, 1)

            pipeline(act, NT, 3, 8, 4, body_a)

            for c in range(CH):
                act.wait_ge(b_qx, c + 1)
                nc.scalar.activation(chunk(qx, c), ps[:, c, 0:CW], ACT.Identity, bias=BQ).then_inc(b_qxe, 1)

            def body_b(i, u):
                if live(i, NT):
                    act.wait_ge(b_qt, i + 1)
                    if past(i, 2):
                        act.wait_ge(b_sc, i - 1)
                    nc.scalar.copy(qts[:, u % 2, :], ps[:, 7, 0:TP]).then_inc(b_qte, 1)
                for q in (0, 2, 4):
                    if live(i, NT):
                        act.wait_ge(b_ct, 6 * i + q + 1)
                        b, t = q // 3, q % 3
                        nc.scalar.copy(cT[:, u % 2, b * NCTX + t * 4 * CR:b * NCTX + (t + 1) * 4 * CR],
                                       ps[:, 3, 0:4 * CR]).then_inc(b_cta, 1)
                    j = i - 4
                    if q == 2 and live(j, NT):
                        act.wait_ge(b_ont, j + 1)
                        if past(j, 2):
                            act.wait_ge(b_wv, j - 1)
                        nc.scalar.copy(oxT[:, u % 2, :].rearrange("p (b n) -> p b n", b=2),
                                       ps[:, 7, 128:256].rearrange("p (b n) -> p b n", b=2)[:, :, 0:NS]).then_inc(b_one, 1)
                j = i - 1
                if live(j, NT):
                    act.wait_ge(b_nb, j + 1)
                    if past(j, 2):
                        act.wait_ge(b_ptr, 3 * (j - 1))
                    nc.scalar.activation(px[0:QP, (u - 1) % 2, :].rearrange("p (t n) -> p t n", t=3), ps[0:QP, 0:3, 0:4 * CR],
                                         ACT.Exp, bias=stat(u - 1, NBI, 1, QP), scale=SCALE_D,
                                         accum_out=stat(u - 1, DEN, 1, QP)).then_inc(b_exp, 1)
                j = i - 5
                if live(j, NT):
                    act.wait_ge(s_w2, NW2)
                    act.wait_ge(b_ht, j + 1)
                    nc.scalar.activation(xT[:, bass.ts(j, TP)], ps[:, 7, 384:384 + TP], ACT.Identity, bias=B1,
                                         scale=G1).then_inc(b_hte, 1)

            pipeline(act, NT, 5, 8, 4, body_b)

            def body_c(i, u):
                if live(i, NT):
                    act.wait_ge(c_qkv, i + 1)
                    if past(i, 2):
                        act.wait_ge(c_sc, i - 1)
                    nc.scalar.activation(qs[:, u % 2, :], ps[:, 0, 0:TP], ACT.Identity, bias=FQ).then_inc(c_q, 1)
                j = i - 2
                if live(j, NT):
                    act.wait_ge(c_ptr, j + 1)
                    if past(j, 2):
                        act.wait_ge(c_pv, j - 1)
                    nc.scalar.copy(pfT[0:TP, u % 2, :].rearrange("p (k n) -> p k n", k=2), ps[0:TP, 5:7, 0:4 * QP]).then_inc(c_pte, 1)
                j = i - 1
                if live(j, NT):
                    act.wait_ge(c_sub, j + 1)
                    p = pf[0:QP, (u - 1) % 2, :]
                    nc.scalar.activation(p, p, ACT.Exp, scale=SCALE_HD).then_inc(c_exp, 1)
                j = i - 5
                if live(j, NT):
                    act.wait_ge(c_ht, j + 1)
                    if past(j, 4):
                        act.wait_ge(c_gt, j - 3)
                        act.wait_ge(c_hx, j - 3)
                    nc.scalar.activation(h2s[:, (u - 5) % 4, :], ps[:, 7, 256:256 + TP], ACT.Identity, bias=B2,
                                         scale=G2).then_inc(c_hte, 1)
                j = i - 3
                if live(j, NT):
                    act.wait_ge(c_pv, j + 1)
                    if past(j, 2):
                        act.wait_ge(c_wo, j - 1)
                    nc.scalar.activation(ofT[:, (u - 3) % 2, :], ps[:, 7, 0:TP], ACT.Identity, bias=FV).then_inc(c_o, 1)

            pipeline(act, NT, 6, 8, 4, body_c)

            act.wait_ge(m_link, 12)
            nc.scalar.activation(gs[:, 4, :], gs[:, 4, :], ACT.Exp).then_inc(m_e, 1)

            def relu(e, u):
                act.wait_ge(s_prep_ev, 4)
                if past(e, 2):
                    act.wait_ge(m_relu, CH * FC * (e - 1))
                nc.scalar.copy(b1e[:, u, :], b1T[:, bass.ds(e * FC, FC)]).then_inc(m_b1, 1)
                for c in range(CH):
                    n = e * CH + c
                    for f in range(FC):
                        if c == 0 and f == 0:
                            act.wait_ge(m_b1, e + 1)
                        if f == 0 and past(n, 2):
                            act.wait_ge(m_out, n - 1)
                        act.wait_ge(m_hid, n * FC + f + 1)
                        nc.scalar.activation(hid[:, c % 2, f, :], ps[:, f, 0:CW], ACT.Relu,
                                             bias=b1e[:, u, f:f + 1]).then_inc(m_relu, 1)

            pipeline(act, NE, 0, 2, 2, relu)

        @block.vector
        def _(dve):
            K, Wv, BW = tok(kT), tok(wT), tok(bwT)
            dve.wait_ge(s_w1, NW1)
            dve.tensor_copy(wb_rep[:, :].rearrange("p (h d) -> p h d", d=HD),
                            wbf[:, 0:H].unsqueeze(2).broadcast_to([D, H, HD])).then_inc(s_rep, 1)
            dve.tensor_copy(wf_rep[:, :].rearrange("p (h d) -> p h d", d=HD),
                            wbf[:, H:].unsqueeze(2).broadcast_to([D, H, HD])).then_inc(s_rep, 1)
            dve.wait_ge(s_ev0, 24)
            dve.tensor_scalar(bwT[:, :], bwT[:, :], 1.0, None, ALU.add).then_inc(s_dve0, 1)
            dve.wait_ge(s_dve0, 1)
            dve.reciprocal(bwT[:, :], bwT[:, :]).then_inc(s_dve0, 1)
            dve.wait_ge(s_act0, 1)
            dve.tensor_tensor(wT[:, :], wT[:, :], tmpB[:, :], ALU.mult).then_inc(s_dve0, 1)
            dve.wait_ge(s_dve0, 3)
            dve.scalar_tensor_tensor(bwT[:, :], bwT[:, :], 2.0, wT[:, :], ALU.mult, ALU.mult).then_inc(s_dve0, 1)
            dve.wait_ge(s_dve0, 4)
            dve.memset(tmpB[:, :], 1.0).then_inc(s_dve0, 1)
            dve.wait_ge(s_dve0, 5)
            dve.memset(tmpB[:, 0:NTOK:NS], 0.0).then_inc(s_dve0, 1)
            dve.wait_ge(s_act0, 4)
            dve.scalar_tensor_tensor(tmpA[:, :], fcT[:, :], 0.0, tmpA[:, :], ALU.min, ALU.subtract).then_inc(s_dve0, 1)
            dve.wait_ge(s_dve0, 7)
            dve.tensor_tensor_scan(fcT[:, :], tmpB[:, :], tmpA[:, :], 0.0, ALU.mult, ALU.add).then_inc(s_dve0, 1)
            for j in range(2):
                dve.wait_ge(s_v, j + 1)
                dve.tensor_copy(v_nat[:, 8 * j:8 * j + 8, :].rearrange("p (c i) d -> p c (i d)", c=2),
                                ps[0:TP, 2 * j:2 * j + 2, :]).then_inc(s_vev, 1)
            dve.wait_ge(s_prep, 1)
            dve.tensor_copy(xwqT[:, :], ps[:, 4, 0:D]).then_inc(s_prep_ev, 1)
            dve.tensor_copy(xwvT[:, :], ps[:, 4, D:2 * D]).then_inc(s_prep_ev, 1)
            dve.tensor_copy(b1T[:, :], ps[:, 4, 2 * D:2 * D + NE * FC]).then_inc(s_prep_ev, 1)
            dve.tensor_copy(rows_b[:, :], ps[0:TP, 5, 0:2 * D + NE]).then_inc(s_prep_ev, 1)
            dve.wait_ge(s_fct, 1)
            dve.tensor_copy(fct8[:, :, :], ps[:, 7, 0:NB * NK].rearrange("p (b k) -> p b k", k=NK)).then_inc(s_fct8, 1)

            def step_T(t, half):
                bs = slice(half * HB, (half + 1) * HB)
                if t >= 2:
                    dve.wait_ge(s_K, 2 * (t - 2) + half + 1)
                dve.tensor_tensor(Tw[:, half, 0:HB * t].rearrange("p (b j) -> p b j", j=t), K[:, bs, 0:t],
                                  Wv[:, bs, t:t + 1].broadcast_to([128, HB, t]), ALU.mult).then_inc(s_T, 1)

            def softmax_logits(k):
                W = T8 * (k + 1)
                e = E[:, k, :].rearrange("p (b j) -> p b j", j=NS)
                if k == 0:
                    dve.wait_ge(s_const, 3)
                    dve.wait_ge(s_fct8, 1)
                dve.wait_ge(s_S, 2 * T8 * (k + 1))
                dve.tensor_tensor(e[:, :, 0:W].rearrange("p (c b) j -> p c b j", c=CH),
                                  ps[:, 4:8, 0:GB * W].rearrange("p c (b j) -> p c b j", j=W),
                                  fct8[:, :, k:k + 1].rearrange("p (c b) k -> p c b k", c=CH).broadcast_to([128, CH, GB, W]),
                                  ALU.add).then_inc(s_Sev, 1)
                dve.wait_ge(s_Sev, k + 1)
                d = e[:, :, T8 * k:W]
                dve.tensor_tensor(d, d, causal8[:, :].unsqueeze(1).broadcast_to([128, NB, T8]), ALU.add).then_inc(s_msk, 1)
                dve.wait_ge(s_msk, k + 1)
                dve.tensor_reduce(rowmax[:, k % 2, :], e[:, :, 0:W], AX.X, ALU.max).then_inc(s_max, 1)
                dve.wait_ge(s_max, k + 1)
                dve.tensor_tensor(e[:, :, 0:W], e[:, :, 0:W],
                                  rowmax[:, k % 2, :].unsqueeze(2).broadcast_to([128, NB, W]), ALU.subtract).then_inc(s_sub, 1)

            def softmax_sum(k):
                W = T8 * (k + 1)
                e = E[:, k, :].rearrange("p (b j) -> p b j", j=NS)
                dve.wait_ge(s_exp, k + 1)
                dve.tensor_reduce(rowsum[:, k, :], e[:, :, 0:W], AX.X, ALU.add).then_inc(s_sum, 1)
                dve.wait_ge(s_sum, k + 1)
                dve.reciprocal(rinv[:, k, :], rowsum[:, k, :]).then_inc(s_rinv, 1)

            for half in range(2):
                step_T(1, half)
            for t in range(1, NS):
                for half in range(2):
                    bs = slice(half * HB, (half + 1) * HB)
                    x = Xw[:, half, 0:HB * t]
                    dve.wait_ge(s_U, 2 * (t - 1) + half + 1)
                    dve.tensor_tensor(x.rearrange("p (c b j) -> p c b j", c=2, j=t),
                                      ps[:, 2 * half:2 * half + 2, 0:GB * t].rearrange("p c (b j) -> p c b j", j=t),
                                      BW[:, bs, t:t + 1].rearrange("p (c b) n -> p c b n", c=2).broadcast_to([128, 2, GB, t]),
                                      ALU.mult).then_inc(s_X, 1)
                    dve.wait_ge(s_X, 2 * (t - 1) + half + 1)
                    dve.wait_ge(s_Tq, 2 * (t - 1) + half + 1)
                    dve.tensor_tensor(K[:, bs, 0:t], K[:, bs, 0:t], x.rearrange("p (b j) -> p b j", j=t),
                                      ALU.subtract).then_inc(s_K, 1)
                    if t + 1 < NS:
                        step_T(t + 1, half)
                if t % T8 == 0:
                    softmax_logits(t // T8 - 1)
                if t % T8 == 2 and t > T8:
                    softmax_sum(t // T8 - 1)
            softmax_logits(NK - 1)
            softmax_sum(NK - 1)

            dve.wait_ge(s_S, 2 * NS)
            dve.wait_ge(s_rinv, NK)

            def body_a(i, u):
                if live(i, NT):
                    if past(i, 2):
                        dve.wait_ge(a_tr, i - 1)
                    dve.tensor_tensor(pa[:, u % 2, :].rearrange("p (k b j) -> p k b j", k=NK, b=2),
                                      E[:, :, bass.ts(i, TP)].rearrange("p k (b j) -> p k b j", b=2),
                                      rinv[:, :, bass.ts(i, 2)].unsqueeze(3).broadcast_to([128, NK, 2, NS]),
                                      ALU.mult).then_inc(a_ps, 1)
                j = i - 2
                if live(j, NT):
                    y, x1 = stage[0:TP, (u - 2) % 4, 0, :], stage[0:TP, (u - 2) % 4, 1, :]
                    dve.wait_ge(a_wo, j + 1)
                    dve.tensor_tensor(y, ps[0:TP, 6, 0:D], res[:, bass.ds(j, 1), :].rearrange("p i d -> p (i d)"), ALU.add).then_inc(a_y, 1)
                    dve.wait_ge(a_y, j + 1)
                    dve.bn_stats(stat(u - 2, ST1, 6), y).then_inc(a_st, 1)
                    dve.wait_ge(s_vev, 2)
                    dve.wait_ge(a_st, j + 1)
                    dve.bn_aggr(stat(u - 2, MV1, 2), stat(u - 2, ST1, 6)).then_inc(a_mv, 1)
                    dve.wait_ge(a_rs, j + 1)
                    if past(j, 4):
                        dve.wait_ge(a_rb, j - 3)
                    dve.tensor_scalar(x1, y, stat(u - 2, MV1), stat(u - 2, RS1), ALU.subtract, ALU.mult).then_inc(a_x1, 1)

            pipeline(dve, NT, 3, 8, 4, body_a)

            def body_b(i, u):
                if live(i, NT):
                    dve.wait_ge(b_qte, i + 1)
                    dve.tensor_copy(stat(u, QB, 1, QP), ps[0:QP, 7, TP:TP + 1]).then_inc(b_qb, 1)
                    for q in (1, 3, 5):
                        dve.wait_ge(b_ct, 6 * i + q + 1)
                        if q == 1 and past(i, 2):
                            dve.wait_ge(b_sc, i - 1)
                        b, t = q // 3, q % 3
                        dve.tensor_copy(cT[:, u % 2, b * NCTX + t * 4 * CR:b * NCTX + (t + 1) * 4 * CR],
                                        ps[:, 4, 0:4 * CR]).then_inc(b_ctd, 1)
                j = i - 1
                if live(j, NT):
                    dve.wait_ge(b_sc, j + 1)
                    dve.tensor_reduce(stat(u - 1, MX, 1, QP), ps[0:QP, 0:3, 0:4 * CR], AX.XY, ALU.max).then_inc(b_mx, 1)
                    dve.wait_ge(b_mx, j + 1)
                    dve.tensor_scalar(stat(u - 1, M2, 1, QP), stat(u - 1, MX, 1, QP), stat(u - 1, QB, 1, QP), None,
                                      ALU.add).then_inc(b_m2, 1)
                    dve.wait_ge(b_m2, j + 1)
                    dve.tensor_scalar(stat(u - 1, NBI, 1, QP), stat(u - 1, M2, 1, QP), stat(u - 1, QB, 1, QP), -SCALE_D,
                                      ALU.subtract, ALU.mult).then_inc(b_nb, 1)
                y, x2, h = (stage[0:TP, u % 4, k, :] for k in range(3))
                for r in range(3):
                    j = i - 2
                    if live(j, NT):
                        dve.wait_ge(b_ptr, 3 * j + r + 1)
                        if r == 0 and past(j, 2):
                            dve.wait_ge(b_pv, j - 1)
                        dve.tensor_copy(pxT[0:CR, u % 2, r * 4 * QP:(r + 1) * 4 * QP], ps[0:CR, 5, 0:4 * QP]).then_inc(b_pte, 1)
                    j = i - 3
                    if r == 0 and live(j, NT):
                        dve.wait_ge(b_exp, j + 1)
                        dve.reciprocal(stat(u - 3, RDN, 1, QP), stat(u - 3, DEN, 1, QP)).then_inc(b_rd, 1)
                        dve.wait_ge(b_rd, j + 1)
                        dve.wait_ge(b_pv, j + 1)
                        if past(j, 2):
                            dve.wait_ge(b_ont, j - 1)
                        dve.tensor_scalar(onx[:, (u - 3) % 2, :], ps[0:QP, 6, 0:D], stat(u - 3, RDN, 1, QP), None,
                                          ALU.mult).then_inc(b_on, 1)
                    j = i - 4
                    if r == 0 and live(j, NT):
                        dve.wait_ge(b_wv, j + 1)
                        dve.tensor_tensor(y, ps[0:TP, 7, 256:384], res[:, bass.ds(j, 1), :].rearrange("p i d -> p (i d)"), ALU.add).then_inc(b_y, 1)
                        dve.wait_ge(b_y, j + 1)
                        dve.bn_stats(stat(u, ST1, 6), y).then_inc(b_st, 1)
                        dve.wait_ge(s_vev, 2)
                        dve.wait_ge(b_st, j + 1)
                        dve.bn_aggr(stat(u, MV1, 2), stat(u, ST1, 6)).then_inc(b_mv, 1)
                    if r == 1 and live(j, NT):
                        dve.wait_ge(b_rs, j + 1)
                        if past(j, 4):
                            dve.wait_ge(b_rb, 2 * (j - 3))
                        dve.tensor_scalar(x2, y, stat(u, MV1), stat(u, RS1), ALU.subtract, ALU.mult).then_inc(b_x2, 1)
                        dve.wait_ge(b_x2, j + 1)
                        dve.bn_stats(stat(u, ST2, 6), x2).then_inc(b_st2, 1)
                        dve.wait_ge(s_vev, 2)
                        dve.wait_ge(b_st2, j + 1)
                        dve.bn_aggr(stat(u, MV2, 2), stat(u, ST2, 6)).then_inc(b_mv2, 1)
                    if r == 2 and live(j, NT):
                        dve.wait_ge(b_rs2, j + 1)
                        if past(j, 4):
                            dve.wait_ge(b_ht, j - 3)
                        dve.tensor_scalar(h, x2, stat(u, MV2), stat(u, RS2), ALU.subtract, ALU.mult).then_inc(b_h, 1)

            pipeline(dve, NT, 5, 8, 4, body_b)

            dve.wait_ge(c_zero, 1)
            dve.wait_ge(b_rb, 2 * NT)

            def body_c(i, u):
                if live(i, NT):
                    dve.wait_ge(c_q, i + 1)
                    if past(i, 2):
                        dve.wait_ge(c_sc, i - 1)
                    dve.scalar_tensor_tensor(km[:, u % 2, :, :], ps[:, 0, TP:2 * TP].unsqueeze(1).broadcast_to([128, 4, TP]), FK,
                                             quad_mask[:, :].unsqueeze(2).broadcast_to([128, 4, TP]), ALU.add, ALU.mult)\
                        .then_inc(c_km, 1)
                    if past(i, 4):
                        dve.wait_ge(c_pv, i - 3)
                    dve.tensor_tensor(vpf[0:TP, u % 4, :, :].rearrange("p b (k c) -> p b k c", c=48)[:, :, :, 0:2 * HD],
                                      ps[0:TP, 0, 2 * TP:2 * TP + 2 * D].rearrange("p (b k c) -> p b k c", b=2, c=2 * HD),
                                      half_mask[:, :].unsqueeze(1).unsqueeze(1).broadcast_to([TP, 2, 8, 2 * HD]),
                                      ALU.mult).then_inc(c_vp, 1)
                j = i - 4
                y, h = stage[0:TP, u % 4, 0, :], stage[0:TP, u % 4, 2, :]
                if live(j, NT):
                    dve.wait_ge(c_wo, j + 1)
                    if past(j, 4):
                        dve.wait_ge(c_acc, j - 3)
                    dve.tensor_tensor(y, ps[0:TP, 7, 128:256], res[:, bass.ds(j, 1), :].rearrange("p i d -> p (i d)"), ALU.add).then_inc(c_y, 1)
                    dve.wait_ge(c_y, j + 1)
                    dve.bn_stats(stat(u, ST1, 6), y).then_inc(c_st, 1)
                    dve.wait_ge(s_vev, 2)
                    dve.wait_ge(c_st, j + 1)
                    dve.bn_aggr(stat(u, MV1, 2), stat(u, ST1, 6)).then_inc(c_mv, 1)
                j = i - 1
                p = pf[0:QP, (u - 1) % 2, :]
                if live(j, NT):
                    sc = ps[0:QP, 1:5, 0:4 * NS].rearrange("p g (h j) -> p g h j", j=NS)
                    dve.wait_ge(c_sc, j + 1)
                    dve.tensor_reduce(stat(u - 1, HMX, H, QP).rearrange("p (g h) -> p g h", g=4), sc, AX.X, ALU.max).then_inc(c_mx, 1)
                    dve.wait_ge(c_mx, j + 1)
                    if past(j, 2):
                        dve.wait_ge(c_ptr, j - 1)
                    dve.tensor_tensor(p.rearrange("p (g h j) -> p g h j", g=4, j=NS), sc,
                                      stat(u - 1, HMX, H, QP).rearrange("p (g h) -> p g h", g=4).unsqueeze(3)
                                      .broadcast_to([QP, 4, 4, NS]), ALU.subtract).then_inc(c_sub, 1)
                j = i - 4
                if live(j, NT):
                    dve.wait_ge(c_rs, j + 1)
                    if past(j, 4):
                        dve.wait_ge(c_ht, j - 3)
                    dve.tensor_scalar(h, y, stat(u, MV1), stat(u, RS1), ALU.subtract, ALU.mult).then_inc(c_h, 1)
                j = i - 1
                if live(j, NT):
                    dve.wait_ge(c_exp, j + 1)
                    dve.tensor_reduce(stat(u - 1, HSM, H, QP), p.rearrange("p (h j) -> p h j", j=NS), AX.X, ALU.add).then_inc(c_sum, 1)
                    dve.wait_ge(c_sum, j + 1)
                    dve.reciprocal(stat(u - 1, HRI, H, QP), stat(u - 1, HSM, H, QP)).then_inc(c_ri, 1)
                j = i - 6
                if live(j, NT):
                    dve.wait_ge(c_gt, j + 1)
                    dve.tensor_tensor(lg[:, bass.ds(j, 1), :].rearrange("p i d -> p (i d)"), ps[0:TP, 7, 384:384 + NE], GBR, ALU.add).then_inc(c_lg, 1)

            pipeline(dve, NT, 6, 8, 4, body_c)

            links = [0]

            def link(ins):
                links[0] += 1
                ins.then_inc(m_link, 1)
                dve.wait_ge(m_link, links[0])

            dve.wait_ge(c_lg, NT)

            def wide(x):
                return x.unsqueeze(2).broadcast_to([TP, NT, NE])

            iota_w = iota8[:, :].unsqueeze(1).broadcast_to([TP, NT, NE])
            eq, val, one1, l2, one2 = (gt[:, k, :, :] for k in range(5))

            def largest(logits, top, one):
                link(dve.tensor_reduce(top, logits, AX.X, ALU.max))
                link(dve.tensor_tensor(eq, logits, wide(top), ALU.is_equal))
                link(dve.scalar_tensor_tensor(val, eq, -float(NE), iota_w, ALU.mult, ALU.add))
                link(dve.tensor_reduce(gs[:, 5, :], val, AX.X, ALU.min))
                link(dve.tensor_tensor(one, val, wide(gs[:, 5, :]), ALU.is_equal))

            largest(lg[:, :, :], gs[:, 0, :], one1)
            link(dve.scalar_tensor_tensor(l2, one1, NEG, lg[:, :, :], ALU.mult, ALU.add))
            largest(l2, gs[:, 1, :], one2)
            link(dve.tensor_tensor(gs[:, 4, :], gs[:, 1, :], gs[:, 0, :], ALU.subtract))
            dve.wait_ge(m_e, 1)
            link(dve.tensor_scalar(gs[:, 2, :], gs[:, 4, :], 1.0, None, ALU.add))
            link(dve.reciprocal(gs[:, 3, :], gs[:, 2, :]))
            link(dve.tensor_tensor(gs[:, 2, :], gs[:, 4, :], gs[:, 3, :], ALU.mult))
            link(dve.tensor_tensor(one1, one1, wide(gs[:, 3, :]), ALU.mult))
            link(dve.tensor_tensor(one2, one2, wide(gs[:, 2, :]), ALU.mult))
            dve.tensor_tensor(ew[:, :, :], one1, one2, ALU.add).then_inc(m_ew, 1)
            for c in range(CH):
                dve.wait_ge(m_ewt, c + 1)
                dve.tensor_copy(ewT[:, c * CW:(c + 1) * CW], ps[0:NE, c, 0:CW]).then_inc(m_ewe, 1)
            dve.wait_ge(c_acc, NT)
            for c in range(CH):
                dve.wait_ge(m_b2, c + 1)
                t = acc[:, 4 * c:4 * c + 4, :]
                dve.tensor_tensor(t, t, ps[0:TP, 4 + c, :].rearrange("p (i d) -> p i d", d=D), ALU.add).then_inc(m_acc0, 1)

            dve.wait_ge(m_acc0, CH)
            dve.wait_ge(m_ew, 1)

            def weigh(e, u):
                for c in range(CH):
                    n = e * CH + c
                    dve.wait_ge(m_out, n + 1)
                    if past(n, CH):
                        dve.wait_ge(m_acc, 4 * (n - 3))
                    for k in range(4):
                        t = acc[:, 4 * c + k, :]
                        dve.scalar_tensor_tensor(t, ps[0:TP, 4 + c % 2, k * D:(k + 1) * D],
                                                 ew[:, 4 * c + k, bass.ds(e, 1)], t, ALU.mult, ALU.add).then_inc(m_acc, 1)

            pipeline(dve, NE, 0, 2, 2, weigh)

            dve.wait_ge(m_acc, NE * CH * 4)
            with dve.Fori(0, NT, 1) as i:
                dve.bn_stats(gt[:, 2:4, :, :].rearrange("p k i e -> p (k i e)")[:, bass.ts(i, 6)],
                             acc[:, bass.ds(i, 1), :].rearrange("p i d -> p (i d)")).then_inc(f_st, 1)
            dve.wait_ge(f_st, NT)
            for i in range(NT):
                dve.bn_aggr(gt[:, 1, i, 0:2],
                            gt[:, 2:4, :, :].rearrange("p k i e -> p (k i e)")[:, 6 * i:6 * i + 6]).then_inc(f_mv, 1)
            dve.wait_ge(f_mv, NT)
            dve.wait_ge(f_rs, 1)
            with dve.Fori(0, NT, 1) as i:
                t = acc[:, bass.ds(i, 1), :].rearrange("p i d -> p (i d)")
                dve.tensor_scalar(t, t, gt[:, 1, :, :].rearrange("p i e -> p (i e)")[:, bass.ds(i * NE, 1)],
                                  gs[:, 2, bass.ds(i, 1)], ALU.subtract, ALU.mult).then_inc(f_y, 1)

        @block.tensor
        def _(pe):
            pe.wait_ge(s_const, 1)
            pe.wait_ge(s_x, 16)
            for c in range(CH):
                for i in range(4):
                    last = pe.transpose(ps[:, c, i * TP:(i + 1) * TP], res[:, 4 * c + i, :], ident[0:TP, 0:TP])
                last.then_inc(s_pe0, 1)

            def project(first, w, src, bank, need):
                for c in range(CH):
                    pe.wait_ge(s_ev0, need + c)
                    pe.matmul(ps[0:w.shape[1], bank + c, 0:CW], w, src[0:w.shape[0], c * CW:(c + 1) * CW],
                              start=True, stop=True).then_inc(s_pe0, 1)

            pe.wait_ge(s_w1, NW1)
            pe.wait_ge(s_rep, 2)
            project(5, wq[:, :], xT, 4, 1)
            project(9, wk[:, :], xT, 0, 1)
            project(13, ww1[:, :], xT, 4, 5)
            project(17, ww2[:, :], tmpA, 0, 13)
            project(21, wb_rep[:, :], xT, 4, 13)
            pe.wait_ge(s_const, 2)
            project(25, blockones[:, :], tmpB, 0, 17)
            project(29, wf_rep[:, :], xT, 4, 21)
            pe.wait_ge(s_ev0, 28)
            for i in range(NT):
                mm = pe.matmul(ps[0:TP, i // 4, (i % 4) * D:(i % 4 + 1) * D], xT[:, i * TP:(i + 1) * TP], wv[:, :],
                               start=True, stop=True)
                if i % 8 == 7:
                    mm.then_inc(s_v, 1)
            pe.wait_ge(s_dve0, 8)
            pe.wait_ge(s_ev0, 32)
            pe.wait_ge(s_w2, NW2)
            pe.transpose(ps[:, 4, 0:D], xw[:, 0, :], ident[:, :])
            pe.transpose(ps[:, 4, D:2 * D], xw[:, 1, :], ident[:, :])
            pe.transpose(ps[:, 4, 2 * D:2 * D + NE * FC], b1_nat[:, :], ident[0:NE * FC, 0:NE * FC])
            pe.matmul(ps[0:TP, 5, 0:2 * D + NE], ones_row[:, :], rows[:, :], start=True, stop=True).then_inc(s_prep, 1)
            F = fcT[:, :].rearrange("p (b k t) -> p b k t", k=NK, t=T8)
            for t in range(T8):
                mm = pe.matmul(ps[:, 7, 0:NB * NK], fc_win[:, (7 - t) * H:(15 - t) * H], F[:, :, :, t],
                               start=(t == 0), stop=(t == T8 - 1))
            mm.then_inc(s_fct, 1)
            pe.wait_ge(s_fct8, 1)
            pe.wait_ge(s_prep_ev, 4)
            pe.wait_ge(s_vev, 2)

            def reduce_U(t, half):
                pe.wait_ge(s_T, 2 * (t - 1) + half + 1)
                for c in range(2):
                    mm = pe.matmul(ps[:, 2 * half + c, 0:GB * t], blockones[:, :],
                                   Tw[:, half, c * GB * t:(c + 1) * GB * t], start=True, stop=True)
                mm.then_inc(s_U, 1)

            def reduce_S(t, half):
                k, W = t // T8, T8 * (t // T8 + 1)
                if t % T8 == 0:
                    if k > 0:
                        pe.wait_ge(s_Sev, k)
                    for c in range(2 * half, 2 * half + 2):
                        pe.matmul(ps[:, 4 + c, 0:GB * W], fc_neg[:, :], tok(fcT)[:, c * GB:(c + 1) * GB, 0:W],
                                  start=True, stop=False)
                pe.wait_ge(s_Tq, 2 * t + half + 1)
                for c in range(2):
                    mm = pe.matmul(ps[:, 4 + 2 * half + c, 0:GB * W], head_win[:, (7 - t % T8) * H:(15 - t % T8) * H],
                                   Tq[:, half, t % 2, c * GB * W:(c + 1) * GB * W],
                                   start=False, stop=(t % T8 == T8 - 1))
                mm.then_inc(s_S, 1)

            for t in range(NS):
                for half in range(2):
                    if t + 1 < NS:
                        reduce_U(t + 1, half)
                    reduce_S(t, half)

            def body_a(i, u):
                if live(i, NT):
                    pe.wait_ge(a_ps, i + 1)
                    if past(i, 2):
                        pe.wait_ge(a_pt, i - 1)
                    for k in range(NK):
                        mm = pe.transpose(ps[0:TP, 2 * (u % 2) + k // 4, (k % 4) * 128:(k % 4 + 1) * 128],
                                          pa[:, u % 2, k * TP:(k + 1) * TP], ident[:, :])
                    mm.then_inc(a_tr, 1)
                j = i - 2
                if live(j, NT):
                    pe.wait_ge(a_o, j + 1)
                    if past(j, 1):
                        pe.wait_ge(a_y, j)
                    pe.matmul(ps[0:TP, 6, 0:D], oTa[:, u % 2, :], wo[:, :], start=True, stop=True).then_inc(a_wo, 1)
                j = i - 3
                if live(j, NT):
                    pe.wait_ge(a_x1, j + 1)
                    if past(j, 1):
                        pe.wait_ge(a_xe, j)
                    pe.transpose(ps[:, 7, 0:TP], stage[0:TP, (u - 3) % 4, 1, :], ident[0:TP, 0:TP]).then_inc(a_xt, 1)
                j = i - 1
                if live(j, NT):
                    v = (u - 1) % 2
                    pe.wait_ge(a_pt, j + 1)
                    pe.wait_ge(a_vp, 2 * (j + 1))
                    if past(j, 2):
                        pe.wait_ge(a_o, j - 1)
                    for b in range(2):
                        for hh in range(4):
                            for g in range(4):
                                h = 4 * g + hh
                                mm = pe.matmul(ps[32 * g:32 * g + 32, 4 + v, b * NS:(b + 1) * NS],
                                               vpa[0:TP, v, b, g * 160 + hh * 32:g * 160 + hh * 32 + 32],
                                               paT[0:TP, v, h:NK * 128:H], start=(hh == 0), stop=(hh == 3),
                                               tile_position=(0, 32 * g))
                    mm.then_inc(a_pv, 1)

            pipeline(pe, NT, 3, 8, 4, body_a)

            pe.wait_ge(a_xe, NT)
            pe.wait_ge(a_pt, NT)
            for c in range(CH):
                pe.matmul(ps[:, c, 0:CW], xwqT[:, :], xT[:, c * CW:(c + 1) * CW], start=True, stop=True).then_inc(b_qx, 1)
            pe.wait_ge(b_qxe, CH)

            def body_b(i, u):
                v = u % 2
                if live(i, NT):
                    pe.wait_ge(b_qxs, i + 1)
                    if not isinstance(i, int) or i >= 6:
                        pe.wait_ge(b_hte, i - 5)
                    pe.matmul(ps[:, 7, 0:TP], xw[:, 2, :], qxs[:, v, :], start=True, stop=True)
                    for b in range(2):
                        mm = pe.matmul(ps[64 * b:64 * b + NS, 7, TP:TP + 1], qxs[:, v, b * NS:(b + 1) * NS], BK,
                                       start=True, stop=True)
                    mm.then_inc(b_qt, 1)
                for q in range(6):
                    b, t = q // 3, q % 3
                    if live(i, NT):
                        if q == 0:
                            pe.wait_ge(b_ctx[u], 4 * (i - u) + 16)
                        evacuated = b_ctd if q % 2 else b_cta
                        if q >= 2 or past(i, 1):
                            pe.wait_ge(evacuated, 3 * i + q // 2)
                        for k in range(4):
                            c = 4 * t + k
                            mm = pe.transpose(ps[:, 3 + q % 2, k * CR:(k + 1) * CR], ctxr[0:CR, u, b, c * D:(c + 1) * D],
                                              ident[0:CR, 0:CR])
                        mm.then_inc(b_ct, 1)
                    j = i - 1
                    if live(j, NT):
                        if q == 0:
                            pe.wait_ge(b_cta, 3 * (j + 1))
                            pe.wait_ge(b_ctd, 3 * (j + 1))
                            pe.wait_ge(b_qte, j + 1)
                            if past(j, 1):
                                pe.wait_ge(b_exp, j)
                        w = (u - 1) % 2
                        mm = pe.matmul(ps[64 * b:64 * b + NS, t, 0:4 * CR], qts[:, w, b * NS:(b + 1) * NS],
                                       cT[:, w, b * NCTX + t * 4 * CR:b * NCTX + (t + 1) * 4 * CR], start=True, stop=True)
                        if q == 5:
                            mm.then_inc(b_sc, 1)
                    j = i - 4
                    if q == 2 and live(j, NT):
                        pe.wait_ge(b_on, j + 1)
                        if live(i, NT):
                            pe.wait_ge(b_qte, i + 1)
                            pe.wait_ge(b_qb, i + 1)
                        else:
                            pe.wait_ge(b_hte, i - 5)
                        pe.transpose(ps[:, 7, 128:128 + QP], onx[:, v, :], ident[0:QP, 0:QP]).then_inc(b_ont, 1)
                for r in range(3):
                    j = i - 2
                    if live(j, NT):
                        pe.wait_ge(b_exp, j + 1)
                        if r > 0 or past(j, 1):
                            pe.wait_ge(b_pte, 3 * j + r)
                        for k in range(4):
                            c = 4 * r + k
                            mm = pe.transpose(ps[0:CR, 5, k * QP:(k + 1) * QP], px[0:QP, v, c * CR:(c + 1) * CR],
                                              ident[0:QP, 0:QP])
                        mm.then_inc(b_ptr, 1)
                    j, uj, q = (i - 3, u - 3, 2) if r == 0 else (i - 2, u - 2, r - 1)
                    if live(j, NT):
                        w = uj % 2
                        pe.wait_ge(b_pte, 3 * j + q + 1)
                        if q == 0 and past(j, 1):
                            pe.wait_ge(b_on, j)
                        for c in range(4 * q, 4 * q + 4):
                            for b in range(2):
                                mm = pe.matmul(ps[64 * b:64 * b + NS, 6, 0:D], pxT[0:CR, w, c * QP + 64 * b:c * QP + 64 * b + NS],
                                               ctxr[0:CR, uj % 4, b, c * D:(c + 1) * D],
                                               start=(c == 0), stop=(c == NCC - 1))
                        if q == 2:
                            mm.then_inc(b_pv, 1)
                    j = i - 4
                    if r == 0 and live(j, NT):
                        pe.wait_ge(b_one, j + 1)
                        pe.matmul(ps[0:TP, 7, 256:384], oxT[:, v, :], xwvT[:, :], start=True, stop=True).then_inc(b_wv, 1)
                    j = i - 5
                    if r == 1 and live(j, NT):
                        pe.wait_ge(b_h, j + 1)
                        if live(i - 4, NT):
                            pe.wait_ge(b_y, i - 3)
                        elif past(j, 1):
                            pe.wait_ge(b_hte, j)
                        pe.transpose(ps[:, 7, 384:384 + TP], stage[0:TP, (u - 5) % 4, 2, :], ident[0:TP, 0:TP]).then_inc(b_ht, 1)

            pipeline(pe, NT, 5, 8, 4, body_b)

            def body_c(i, u):
                v = u % 2
                if live(i, NT):
                    pe.wait_ge(c_hs, i + 1)
                    if past(i, 1):
                        pe.wait_ge(c_q, i)
                        pe.wait_ge(c_km, i)
                        pe.wait_ge(c_vp, i)
                    h1 = hs[:, u % 4, :, 0:NS]
                    pe.matmul(ps[:, 0, 0:TP], wqkv[:, 0:D], h1, start=True, stop=True)
                    pe.matmul(ps[:, 0, TP:2 * TP], wqkv[:, D:2 * D], h1, start=True, stop=True)
                    for b in range(2):
                        mm = pe.matmul(ps[0:TP, 0, 2 * TP + b * D:2 * TP + (b + 1) * D], hs[:, u % 4, b, :], wqkv[:, 2 * D:3 * D],
                                       start=True, stop=True)
                    mm.then_inc(c_qkv, 1)
                j = i - 4
                if live(j, NT):
                    pe.wait_ge(c_o, j + 1)
                    pe.matmul(ps[0:TP, 7, 128:256], ofT[:, v, :], w_o[:, :], start=True, stop=True).then_inc(c_wo, 1)
                j = i - 1
                if live(j, NT):
                    w = (u - 1) % 2
                    pe.wait_ge(c_q, j + 1)
                    pe.wait_ge(c_km, j + 1)
                    if past(j, 1):
                        pe.wait_ge(c_sub, j)
                    for b in range(2):
                        for g in range(4):
                            rs = slice(32 * g, 32 * g + 32)
                            mm = pe.matmul(ps[64 * b:64 * b + NS, 1 + g, 0:4 * NS], qs[rs, w, b * NS:(b + 1) * NS],
                                           km[rs, w, :, b * NS:(b + 1) * NS], start=True, stop=True,
                                           tile_position=(32 * g, 64 * b))
                    mm.then_inc(c_sc, 1)
                j = i - 6
                if live(j, NT):
                    pe.wait_ge(c_hte, j + 1)
                    if live(i - 4, NT):
                        pe.wait_ge(c_y, i - 3)
                    elif live(i - 5, NT):
                        pe.wait_ge(c_hte, i - 5)
                    pe.matmul(ps[0:TP, 7, 384:384 + NE], h2s[:, (u - 6) % 4, :], gate_w[:, :], start=True, stop=True).then_inc(c_gt, 1)
                j = i - 2
                if live(j, NT):
                    pe.wait_ge(c_nrm, j + 1)
                    if past(j, 1):
                        pe.wait_ge(c_pte, j)
                    for k in range(8):
                        mm = pe.transpose(ps[0:TP, 5 + k // 4, (k % 4) * QP:(k % 4 + 1) * QP], pf[0:QP, v, k * TP:(k + 1) * TP],
                                          ident[0:QP, 0:QP])
                    mm.then_inc(c_ptr, 1)
                j = i - 5
                if live(j, NT):
                    pe.wait_ge(c_h, j + 1)
                    if live(i - 4, NT):
                        pe.wait_ge(c_y, i - 3)
                    if live(i - 6, NT):
                        pe.wait_ge(c_lg, i - 5)
                    pe.transpose(ps[:, 7, 256:256 + TP], stage[0:TP, (u - 5) % 4, 2, :], ident[0:TP, 0:TP]).then_inc(c_ht, 1)
                j = i - 3
                if live(j, NT):
                    w = (u - 3) % 2
                    pe.wait_ge(c_pte, j + 1)
                    pe.wait_ge(c_vp, j + 1)
                    if live(i - 4, NT):
                        pe.wait_ge(c_y, i - 3)
                    if live(i - 5, NT):
                        pe.wait_ge(c_hte, i - 4)
                    for b in range(2):
                        for s in range(2):
                            for g in range(4):
                                k = 2 * g + s
                                mm = pe.matmul(ps[32 * g:32 * g + 32, 7, b * NS:(b + 1) * NS],
                                               vpf[0:TP, (u - 3) % 4, b, g * 96 + s * 32:g * 96 + s * 32 + 32],
                                               pfT[0:TP, w, k * QP + 64 * b:k * QP + 64 * b + NS],
                                               start=(s == 0), stop=(s == 1), tile_position=(0, 32 * g))
                    mm.then_inc(c_pv, 1)

            pipeline(pe, NT, 6, 8, 4, body_c)

            pe.wait_ge(m_ew, 1)
            for c in range(CH):
                for i in range(4):
                    mm = pe.transpose(ps[0:NE, c, i * TP:(i + 1) * TP], ew[:, 4 * c + i, :], ident[0:TP, 0:TP])
                mm.then_inc(m_ewt, 1)
            for c in range(CH):
                pe.wait_ge(m_ewe, c + 1)
                for i in range(4):
                    t = 4 * c + i
                    mm = pe.matmul(ps[0:TP, 4 + c, i * D:(i + 1) * D], ewT[:, t * TP:(t + 1) * TP], b2_nat[:, :],
                                   start=True, stop=True)
                mm.then_inc(m_b2, 1)
            pe.wait_ge(c_hx, NT)
            pe.wait_ge(m_acc0, 2)

            def second(n, c, w):
                pe.wait_ge(m_relu, FC * n)
                if past(n, 3):
                    pe.wait_ge(m_acc, 4 * (n - 2))
                for k in range(4):
                    for f in range(FC):
                        mm = pe.matmul(ps[0:TP, 4 + c % 2, k * D:(k + 1) * D], hid[:, c % 2, f, k * TP:(k + 1) * TP],
                                       w2r[:, w, f, :], start=(f == 0), stop=(f == FC - 1))
                mm.then_inc(m_out, 1)

            def experts(e, u):
                for c in range(CH):
                    n = e * CH + c
                    if c == 0:
                        pe.wait_ge(m_w[u], 16 * (e - u) + 32)
                    for f in range(FC):
                        if past(n, 1):
                            pe.wait_ge(m_relu, FC * (n - 1) + f + 1)
                        pe.matmul(ps[:, f, 0:CW], w1r[:, u, f * 128:(f + 1) * 128], xT[:, c * CW:(c + 1) * CW],
                                  start=True, stop=True).then_inc(m_hid, 1)
                    if past(n, 1):
                        second(n, (c - 1) % CH, u if c else 1 - u)

            pipeline(pe, NE, 0, 2, 2, experts)
            second(NE * CH, CH - 1, 1)


_INS = ["x", "ctx_1024"] + ["L0_attn_" + n for n in ("Wq", "Wk", "Wv", "Wo", "Ww1", "Ww2", "Wb", "Wf", "delta")] + \
    ["L0_xattn_" + n for n in ("Wq", "bq", "Wk", "bk", "Wv", "bv")] + \
    ["L0_ffn_" + n for n in ("ln1_g", "ln1_b", "w_qkv", "b_qkv", "w_o", "b_o", "ln2_g", "ln2_b", "gate_w", "gate_b",
                             "W1", "b1", "W2", "b2")]


def kernel(**inputs):
    import numpy as _np
    import concourse.bacc as _bacc
    from concourse import mybir as _mybir
    from concourse.bass_utils import run_bass_kernel_spmd as _run

    nc = _bacc.Bacc("TRN2", target_bir_lowering=False, num_devices=1)
    arrays, args = {}, {}
    for name in _INS:
        v = _np.ascontiguousarray(inputs[name])
        arrays["in_" + name] = v
        args[name] = nc.dram_tensor("in_" + name, v.shape, _mybir.dt.from_np(v.dtype), kind="ExternalInput").ap()
    o = nc.dram_tensor("out_0", (NB, NS, D), _mybir.dt.float32, kind="ExternalOutput").ap()
    build(nc, args, o)
    r = _run(nc, [arrays], core_ids=[0])
    return r.results[0]["out_0"]
```

```python
from contextlib import ExitStack

import concourse.bass as bass
from concourse import mybir

F32 = mybir.dt.float32
F32R = mybir.dt.float32r
I32 = mybir.dt.int32
ALU = mybir.AluOpType
ACT = mybir.ActivationFunctionType
AX = mybir.AxisListType

NB, NS, D, H = 32, 56, 128, 16
HD = D // H
NT = NB // 2
TP = 2 * NS
NTOK = NB * NS
CH = 4
CW = NTOK // CH
T8 = 8
NK = NS // T8
GB = NB // CH
HB = NB // 2
NCTX = 1500
NCC = 12
CR = NCTX // NCC
QP = 120
NE, FF = 8, 4 * D
FC = FF // 128
NEG = -1.0e30
EPS = 1e-05
UPPER = -(1 << 12)
SCALE_HD = float(HD) ** -0.5
SCALE_D = float(D) ** -0.5


def live(j, n):
    return not isinstance(j, int) or 0 <= j < n


def past(j, r):
    return not isinstance(j, int) or j >= r


def at(i, n):
    return isinstance(i, int) and i == n


def pipeline(eng, n, skew, lo, unroll, body):
    for i in range(lo):
        body(i, i % unroll)
    with eng.Fori(lo // unroll, n // unroll, 1) as r:
        for u in range(unroll):
            body(r * unroll + u, u)
    for i in range(n, n + skew):
        body(i, i % unroll)


def build(nc, a, out):
    ctx = ExitStack()
    with ctx:
        def sb(name, shape, dtype=F32):
            return ctx.enter_context(nc.sbuf_tensor(name, shape, dtype))

        def sem(name):
            return ctx.enter_context(nc.semaphore(name))

        ps = ctx.enter_context(nc.psum_tensor("ps", [128, 8, 512], F32))

        ident = sb("ident", [128, 128])
        blockones = sb("blockones", [128, 128])
        head_win = sb("head_win", [128, 15 * H])
        fc_win = sb("fc_win", [128, 15 * H])
        fc_neg = sb("fc_neg", [128, T8 * H])
        causal8 = sb("causal8", [128, T8])
        half_mask = sb("half_mask", [TP, 2 * HD])
        quad_mask = sb("quad_mask", [128, 4])
        ones_row = sb("ones_row", [1, TP])

        wq = sb("wq", [D, D]); wk = sb("wk", [D, D]); wv = sb("wv", [D, D]); wo = sb("wo", [D, D])
        ww1 = sb("ww1", [D, HD]); ww2 = sb("ww2", [HD, D])
        wbf = sb("wbf", [D, 2 * H]); wb_rep = sb("wb_rep", [D, D]); wf_rep = sb("wf_rep", [D, D])
        delta = sb("delta", [D, 1])
        eps_ww = sb("eps_ww", [128, 1]); eps_ln = sb("eps_ln", [128, 1]); minus_half = sb("minus_half", [128, 1])
        xw = sb("xw", [D, 3, D])
        xwqT = sb("xwqT", [D, D]); xwvT = sb("xwvT", [D, D])
        wqkv = sb("wqkv", [D, 3 * D]); w_o = sb("w_o", [D, D]); gate_w = sb("gate_w", [D, NE])
        cols = sb("cols", [D, 9])
        BQ, BK, G1, B1, FQ, FK, FV, G2, B2 = (cols[:, i:i + 1] for i in range(9))
        rows = sb("rows", [1, 2 * D + NE])
        rows_b = sb("rows_b", [TP, 2 * D + NE])
        BVR, BOR, GBR = rows_b[:, 0:D], rows_b[:, D:2 * D], rows_b[:, 2 * D:]
        b1_nat = sb("b1_nat", [NE * FC, 128]); b1T = sb("b1T", [128, NE * FC]); b1e = sb("b1e", [128, 2, FC])
        b2_nat = sb("b2_nat", [NE, D])
        w1r = sb("w1r", [D, 2, FF]); w2r = sb("w2r", [128, 2, FC, D])

        with nc.sbuf_tensor("early", [128, 2 * NTOK], F32) as early:
            pass
        xh = sb("xh", [D, NTOK], F32R); xl = sb("xl", [D, NTOK], F32R)
        with nc.sbuf_tensor("xT", [D, 4 * FF], F32) as xT:
            pass
        w1h = sb("w1h", [D, 2, FF], F32R); w1l = sb("w1l", [D, 2, FF], F32R)

        res = sb("res", [TP, NT, D])
        v_nat = sb("v_nat", [TP, NT, D])
        acc = v_nat
        x2n = sb("x2n", [TP, NT, D])
        small = sb("small", [128, 4, 80])
        stage = sb("stage", [128, 4, 3, D])
        lg = sb("lg", [TP, NT, NE]); ew = sb("ew", [TP, NT, NE]); gt = sb("gt", [TP, 6, NT, NE])
        gs = sb("gs", [TP, 6, NT]); iota8 = sb("iota8", [TP, NE])

        class Region:
            def __init__(self, name, size):
                self.t, self.size = sb(name, [128, size]), size
                self.at = 0

            def take(self, n):
                self.at += n
                assert self.at <= self.size, (self.at, self.size)
                return self.t[:, self.at - n:self.at]

            def restart(self, at=0):
                self.at = at

        R1 = Region("R1", 7 * NTOK + 2 * NTOK)
        R2 = Region("R2", NK * NB * NS)
        qT, kT, wT, bwT, fcT, tmpA, tmpB = (R1.take(NTOK) for _ in range(7))
        halves = R1.at
        Tw = R1.take(2 * HB * NS).rearrange("p (h n) -> p h n", h=2)
        Xw = R1.take(2 * HB * NS).rearrange("p (h n) -> p h n", h=2)
        Tq = early[:, :].rearrange("p (h r n) -> p h r n", h=2, r=2)
        E = R2.take(NK * NB * NS).rearrange("p (k n) -> p k n", k=NK)
        R1.restart(halves)
        pa = R1.take(2 * NK * TP).rearrange("p (r n) -> p r n", r=2)
        paT = R1.take(2 * NK * 128).rearrange("p (r n) -> p r n", r=2)
        vpa = early[:, 0:4 * 640].rearrange("p (r b n) -> p r b n", r=2, b=2)
        oTa = R1.take(2 * TP).rearrange("p (r n) -> p r n", r=2)
        R1.restart(); R2.restart()
        ctxr = R1.take(4 * 2 * NCC * D).rearrange("p (r b n) -> p r b n", r=4, b=2)
        ctx_end = R1.at
        cT = R2.take(2 * 2 * NCTX).rearrange("p (r n) -> p r n", r=2)
        px = R2.take(2 * NCTX).rearrange("p (r n) -> p r n", r=2)
        pxT = R2.take(2 * NCC * QP).rearrange("p (r n) -> p r n", r=2)
        qx = sb("qx", [D, NTOK]); onx = sb("onx", [QP, 2, D])
        ewT = qx[0:NE, :]
        qxs = sb("qxs", [D, 2, TP]); qts = sb("qts", [D, 2, TP]); oxT = sb("oxT", [D, 2, TP])
        R1.restart()
        hs = R1.take(4 * 2 * TP).rearrange("p (r b n) -> p r b n", r=4, b=2)
        qs = R1.take(2 * TP).rearrange("p (r n) -> p r n", r=2)
        km = R1.take(2 * 4 * TP).rearrange("p (r f n) -> p r f n", r=2, f=4)
        pf = R1.take(2 * H * NS).rearrange("p (r n) -> p r n", r=2)
        pfT = R1.take(2 * 8 * QP).rearrange("p (r n) -> p r n", r=2)
        vpf = R1.take(4 * 2 * 384).rearrange("p (r b n) -> p r b n", r=4, b=2)
        ofT = R1.take(2 * TP).rearrange("p (r n) -> p r n", r=2)
        h2s = R1.take(4 * TP).rearrange("p (r n) -> p r n", r=4)
        xm = R1.take(2 * TP).rearrange("p (r n) -> p r n", r=2)
        w1m = R1.take(2 * FF).rearrange("p (r n) -> p r n", r=2)
        R2.restart()
        hid = R2.take(2 * FC * CW).rearrange("p (r f n) -> p r f n", r=2, f=FC)

        fct8 = sb("fct8", [128, NB, NK])
        rowmax = sb("rowmax", [128, 2, NB]); rowsum = sb("rowsum", [128, NK, NB]); rinv = sb("rinv", [128, NK, NB])

        s_const = sem("s_const"); s_link = sem("s_link")
        s_x = sem("s_x"); s_w1 = sem("s_w1")
        s_rep = sem("s_rep")
        s_pe0 = sem("s_pe0"); s_ev0 = sem("s_ev0"); s_act0 = sem("s_act0"); s_dve0 = sem("s_dve0")
        s_T = sem("s_T"); s_U = sem("s_U"); s_X = sem("s_X"); s_K = sem("s_K"); s_Tq = sem("s_Tq"); s_S = sem("s_S")
        s_Sev = sem("s_Sev"); s_msk = sem("s_msk"); s_max = sem("s_max"); s_sub = sem("s_sub"); s_exp = sem("s_exp")
        s_sum = sem("s_sum"); s_rinv = sem("s_rinv"); s_fct = sem("s_fct"); s_fct8 = sem("s_fct8")
        s_zero = sem("s_zero"); s_v = sem("s_v"); s_vev = sem("s_vev")
        s_out = sem("s_out"); s_w2 = sem("s_w2"); s_prep = sem("s_prep"); s_prep_ev = sem("s_prep_ev")
        a_zero = sem("a_zero"); a_ps = sem("a_ps"); a_tr = sem("a_tr"); a_pt = sem("a_pt"); a_vp = sem("a_vp")
        a_pv = sem("a_pv"); a_o = sem("a_o"); a_wo = sem("a_wo"); a_y = sem("a_y"); a_st = sem("a_st"); a_mv = sem("a_mv")
        a_ln = sem("a_ln"); a_rs = sem("a_rs"); a_x1 = sem("a_x1"); a_xt = sem("a_xt"); a_xe = sem("a_xe"); a_rb = sem("a_rb")
        b_ctx = [sem(f"b_ctx{u}") for u in range(4)]
        b_qx = sem("b_qx"); b_qxe = sem("b_qxe"); b_qxs = sem("b_qxs"); b_qt = sem("b_qt"); b_qte = sem("b_qte"); b_qb = sem("b_qb")
        b_ct = sem("b_ct"); b_cta = sem("b_cta"); b_ctd = sem("b_ctd"); b_sc = sem("b_sc"); b_mx = sem("b_mx"); b_m2 = sem("b_m2")
        b_nb = sem("b_nb"); b_exp = sem("b_exp"); b_ptr = sem("b_ptr"); b_pta = sem("b_pta"); b_ptd = sem("b_ptd"); b_pv = sem("b_pv")
        b_rd = sem("b_rd"); b_on = sem("b_on"); b_ont = sem("b_ont"); b_one = sem("b_one"); b_wv = sem("b_wv"); b_y = sem("b_y")
        b_st = sem("b_st"); b_mv = sem("b_mv"); b_ln = sem("b_ln"); b_rs = sem("b_rs"); b_x2 = sem("b_x2"); b_st2 = sem("b_st2")
        b_mv2 = sem("b_mv2"); b_ln2 = sem("b_ln2"); b_rs2 = sem("b_rs2"); b_h = sem("b_h"); b_ht = sem("b_ht"); b_hte = sem("b_hte")
        b_rb = sem("b_rb")
        c_zero = sem("c_zero"); c_hs = sem("c_hs"); c_qkv = sem("c_qkv"); c_q = sem("c_q"); c_km = sem("c_km"); c_vp = sem("c_vp")
        c_sc = sem("c_sc"); c_mx = sem("c_mx"); c_sub = sem("c_sub"); c_exp = sem("c_exp"); c_sum = sem("c_sum"); c_ri = sem("c_ri")
        c_nrm = sem("c_nrm"); c_ptr = sem("c_ptr"); c_pte = sem("c_pte"); c_pv = sem("c_pv"); c_o = sem("c_o"); c_wo = sem("c_wo")
        c_y = sem("c_y"); c_st = sem("c_st"); c_mv = sem("c_mv"); c_ln = sem("c_ln"); c_rs = sem("c_rs"); c_h = sem("c_h")
        c_ht = sem("c_ht"); c_hte = sem("c_hte"); c_xm = sem("c_xm"); c_xh = sem("c_xh"); c_xl = sem("c_xl"); c_gt = sem("c_gt"); c_lg = sem("c_lg"); c_acc = sem("c_acc")
        m_link = sem("m_link"); m_e = sem("m_e"); m_ew = sem("m_ew"); m_ewt = sem("m_ewt"); m_ewe = sem("m_ewe"); m_b2 = sem("m_b2")
        m_b1 = sem("m_b1"); m_acc0 = sem("m_acc0"); m_w = [sem(f"m_w{u}") for u in range(2)]; m_hid = sem("m_hid"); m_relu = sem("m_relu")
        m_out = sem("m_out"); m_acc = sem("m_acc"); m_wm = sem("m_wm"); m_wh = sem("m_wh"); m_wl = sem("m_wl"); f_st = sem("f_st"); f_mv = sem("f_mv"); f_ln = sem("f_ln"); f_rs = sem("f_rs")
        f_y = sem("f_y")

        xflat = a["x"].rearrange("b n d -> (b n) d").rearrange("(i p) d -> p i d", p=TP)

        def tok(t):
            return t[:, 0:NTOK].rearrange("p (b n) -> p b n", n=NS)

        block = ctx.enter_context(nc.Block())

        @block.sync
        def _(sp):
            sp.dma_start(res[:, :, :], xflat).then_inc(s_x, 16)
            for t, n in ((wq, "Wq"), (wk, "Wk"), (ww1, "Ww1"), (ww2, "Ww2"), (wv, "Wv"), (wo, "Wo")):
                sp.dma_start(t[:, :], a["L0_attn_" + n]).then_inc(s_w1, 16)
            sp.dma_start(wbf[:, 0:H], a["L0_attn_Wb"]).then_inc(s_w1, 16)
            sp.dma_start(wbf[:, H:2 * H], a["L0_attn_Wf"]).then_inc(s_w1, 16)
            sp.dma_start(delta[:, :], a["L0_attn_delta"].rearrange("(h o) -> h o", o=1).broadcast_to([H, HD]).rearrange("h (d o) -> h d o", o=1)).then_inc(s_w1, 16)
            X, F = "L0_xattn_", "L0_ffn_"
            for t, n in ((xw[:, 0, :], X + "Wq"), (xw[:, 1, :], X + "Wv"), (xw[:, 2, :], X + "Wk"), (wqkv[:, :], F + "w_qkv"),
                         (w_o[:, :], F + "w_o"), (gate_w[:, :], F + "gate_w"), (b2_nat[:, :], F + "b2")):
                sp.dma_start(t, a[n]).then_inc(s_w2, 16)
            sp.dma_start(b1_nat[:, :], a[F + "b1"].rearrange("e (c f) -> (e c) f", f=128)).then_inc(s_w2, 16)
            bqkv = a[F + "b_qkv"].rearrange("(s d o) -> s d o", s=3, o=1)
            for t, v in ((BQ, a[X + "bq"]), (BK, a[X + "bk"]), (G1, a[F + "ln1_g"]), (B1, a[F + "ln1_b"]), (FQ, bqkv[0]),
                         (FK, bqkv[1]), (FV, bqkv[2]), (G2, a[F + "ln2_g"]), (B2, a[F + "ln2_b"])):
                sp.dma_start(t, v if len(v.shape) == 2 else v.rearrange("(d o) -> d o", o=1)).then_inc(s_w2, 16)
            for lo, v in ((0, a[X + "bv"]), (D, a[F + "b_o"]), (2 * D, a[F + "gate_b"])):
                sp.dma_start(rows[:, lo:lo + v.shape[0]], v.rearrange("(o d) -> o d", o=1)).then_inc(s_w2, 16)
            ctx_v = a["ctx_1024"].rearrange("(i two) (p c) d -> i p two (c d)", two=2, c=NCC)
            sp.wait_ge(s_S, 2 * NS)
            sp.wait_ge(s_K, 2 * (NS - 1))
            for i in range(4):
                sp.dma_start(ctxr[0:CR, i], ctx_v[i]).then_inc(b_ctx[i], 16)
            with sp.Fori(1, NT // 4, 1) as r:
                for u in range(4):
                    sp.wait_ge(b_pv, r * 4 + u - 3)
                    sp.wait_ge(s_S, 2 * NS)
                    sp.dma_start(ctxr[0:CR, u], ctx_v[r * 4 + u]).then_inc(b_ctx[u], 16)

            w1_v = a[F + "W1"]
            w2_v = a[F + "W2"].rearrange("e (c f) d -> e f c d", f=128)

            def expert(e, u):
                sp.dma_start(w1r[:, u, :], w1_v[e]).then_inc(m_w[u], 16)
                sp.dma_start(w2r[:, u], w2_v[e]).then_inc(m_w[u], 16)

            expert(0, 0)
            expert(1, 1)
            with sp.Fori(1, NE // 2, 1) as r:
                for u in range(2):
                    e = r * 2 + u
                    sp.wait_ge(m_w[u], 32)
                    sp.wait_ge(m_out, (e - 1) * CH)
                    expert(e, u)
            oflat = out.rearrange("b n d -> (b n) d").rearrange("(i p) d -> p i d", p=TP)
            for c in range(CH):
                sp.wait_ge(f_y, 4 * (c + 1))
                sp.dma_start(oflat[:, 4 * c:4 * c + 4, :], acc[:, 4 * c:4 * c + 4, :]).then_inc(s_out, 16)
            sp.wait_ge(s_out, 16 * CH)

        NW1 = 9 * 16
        NW2 = 20 * 16

        def stat(u, lo, n=1, rows=TP):
            return small[0:rows, u % 4, lo:lo + n]

        ST1, MV1, LN1, RS1, ST2, MV2, LN2, RS2 = 0, 6, 8, 9, 10, 16, 18, 19
        MX, QB, M2, NBI, DEN, RDN, HMX, HSM, HRI = 20, 21, 22, 23, 24, 25, 26, 42, 58

        @block.gpsimd
        def _(pool):
            links = [0]

            def link(ins):
                links[0] += 1
                ins.then_inc(s_link, 1)
                pool.wait_ge(s_link, links[0])

            pool.memset(eps_ww[:, :], 1e-6)
            pool.memset(eps_ln[:, :], EPS)
            pool.memset(minus_half[:, :], -0.5)
            link(pool.memset(ident[:, :], 0.0))
            pool.affine_select(out=ident[:, :], in_=ident[:, :], compare_op=ALU.not_equal, fill=1.0,
                               base=0, pattern=[[-1, 128]], channel_multiplier=1).then_inc(s_const, 1)
            bo = blockones[:, :].rearrange("p (g d) -> p g d", d=HD)
            link(pool.memset(blockones[:, :], 1.0))
            link(pool.affine_select(out=bo, in_=bo, compare_op=ALU.is_ge, fill=0.0,
                                    base=0, pattern=[[-HD, H], [0, HD]], channel_multiplier=1))
            link(pool.affine_select(out=bo, in_=bo, compare_op=ALU.is_ge, fill=0.0,
                                    base=HD - 1, pattern=[[HD, H], [0, HD]], channel_multiplier=-1))
            link(pool.memset(head_win[:, :], 0.0))
            mid = slice(7 * H, 8 * H)
            link(pool.tensor_copy(head_win[:, mid], blockones[:, 0:D:HD]))
            link(pool.memset(fc_win[:, :], 0.0))
            link(pool.affine_select(out=fc_win[:, mid], in_=fc_win[:, mid], compare_op=ALU.not_equal, fill=1.0,
                                    base=0, pattern=[[-HD, H]], channel_multiplier=1))
            fn = fc_neg[:, :].rearrange("p (t h) -> p t h", t=T8)
            link(pool.memset(fc_neg[:, :], 0.0))
            link(pool.affine_select(out=fn, in_=fn, compare_op=ALU.not_equal, fill=-1.0,
                                    base=0, pattern=[[0, T8], [-HD, H]], channel_multiplier=1))
            link(pool.memset(causal8[:, :], 0.0))
            link(pool.affine_select(out=causal8[:, :], in_=causal8[:, :], compare_op=ALU.is_ge, fill=NEG,
                                    base=0, pattern=[[-H, T8]], channel_multiplier=1))
            link(pool.memset(half_mask[:, :], 1.0))
            link(pool.affine_select(out=half_mask[:, 0:HD], in_=half_mask[:, 0:HD], compare_op=ALU.is_ge, fill=0.0,
                                    base=NS - 1, pattern=[[0, HD]], channel_multiplier=-1))
            link(pool.affine_select(out=half_mask[:, HD:], in_=half_mask[:, HD:], compare_op=ALU.is_ge, fill=0.0,
                                    base=-NS, pattern=[[0, HD]], channel_multiplier=1))
            link(pool.tensor_copy(quad_mask[:, :], blockones[:, 0:4 * HD:HD]))
            for g in range(1, 4):
                link(pool.tensor_tensor(quad_mask[:, :], quad_mask[:, :], blockones[:, 4 * HD * g:4 * HD * (g + 1):HD], ALU.add))
            link(pool.iota(iota8[:, :], pattern=[[1, NE]], base=0, channel_multiplier=0, allow_small_or_imprecise_dtypes=True))
            pool.memset(ones_row[:, :], 1.0).then_inc(s_const, 1)
            pool.memset(E[:, :, :], 0.0).then_inc(s_const, 1)
            K, Q = tok(kT), tok(qT)
            pool.wait_ge(s_dve0, 4)
            for t in range(NS):
                W = T8 * (t // T8 + 1)
                for half in range(2):
                    bs = slice(half * HB, (half + 1) * HB)
                    if t > 0:
                        pool.wait_ge(s_K, 2 * (t - 1) + half + 1)
                    if t >= 2:
                        pool.wait_ge(s_S, 2 * (t - 2) + half + 1)
                    o = Tq[:, half, t % 2, 0:HB * W].rearrange("p (b j) -> p b j", j=W)
                    nc.gpsimd.tensor_tensor(o, K[:, bs, 0:W], Q[:, bs, t:t + 1].broadcast_to([128, HB, W]),
                                            ALU.mult).then_inc(s_Tq, 1)

            def rstd(var, eps_sum, out, mv, ln, rs, j):
                pool.wait_ge(mv, j + 1)
                nc.gpsimd.tensor_tensor(eps_sum, var, eps_ln[0:TP, :], ALU.add).then_inc(ln, 1)
                pool.wait_ge(ln, j + 1)
                nc.gpsimd.tensor_tensor(out, eps_sum, minus_half[0:TP, :], ALU.pow).then_inc(rs, 1)

            pool.wait_ge(s_S, 2 * NS)
            pool.wait_ge(s_K, 2 * (NS - 1))
            pool.memset(vpa, 0.0).then_inc(a_zero, 1)
            pool.wait_ge(a_zero, 1)
            pool.wait_ge(s_vev, 2)
            pool.wait_ge(s_prep_ev, 4)

            def body_a(i, u):
                if live(i, NT):
                    if past(i, 2):
                        pool.wait_ge(a_pv, i - 1)
                    for b in range(2):
                        nc.gpsimd.tensor_tensor(
                            vpa[0:TP, u % 2, b, :].rearrange("p (h c) -> p h c", c=5 * HD)[:, :, 0:HD],
                            v_nat[:, bass.ds(i, 1), :].rearrange("p i (h d) -> p (i h) d", d=HD),
                            half_mask[:, b * HD:(b + 1) * HD].unsqueeze(1).broadcast_to([TP, H, HD]),
                            ALU.mult).then_inc(a_vp, 1)
                j = i - 2
                if live(j, NT):
                    rstd(stat(u - 2, MV1 + 1), stat(u - 2, LN1), stat(u - 2, RS1), a_mv, a_ln, a_rs, j)
                    pool.wait_ge(a_x1, j + 1)
                    nc.gpsimd.tensor_tensor(res[:, bass.ds(j, 1), :].rearrange("p i d -> p (i d)"), stage[0:TP, (u - 2) % 4, 1, :], BVR,
                                            ALU.add).then_inc(a_rb, 1)

            pipeline(pool, NT, 3, 8, 4, body_a)

            def body_b(i, u):
                if live(i, NT):
                    pool.wait_ge(b_qxe, CH)
                    if past(i, 2):
                        pool.wait_ge(b_qt, i - 1)
                    nc.gpsimd.tensor_copy(qxs[:, u % 2, :], qx[:, bass.ts(i, TP)]).then_inc(b_qxs, 1)
                j, v = i - 5, u - 5
                if live(j, NT):
                    x2 = stage[0:TP, v % 4, 1, :]
                    rstd(stat(v, MV1 + 1), stat(v, LN1), stat(v, RS1), b_mv, b_ln, b_rs, j)
                    rstd(stat(v, MV2 + 1), stat(v, LN2), stat(v, RS2), b_mv2, b_ln2, b_rs2, j)
                    pool.wait_ge(b_x2, j + 1)
                    nc.gpsimd.tensor_tensor(res[:, bass.ds(j, 1), :].rearrange("p i d -> p (i d)"), x2, BOR, ALU.add).then_inc(b_rb, 1)
                    nc.gpsimd.tensor_copy(x2n[:, bass.ds(j, 1), :].rearrange("p i d -> p (i d)"), x2).then_inc(b_rb, 1)

            pipeline(pool, NT, 6, 8, 4, body_b)

            pool.wait_ge(b_pv, NT)
            pool.memset(vpf, 0.0).then_inc(c_zero, 1)

            def lower(e, u):
                pool.wait_ge(m_wm, e + 1)
                if past(e, 2):
                    pool.wait_ge(m_hid, CH * FC * (e - 1))
                else:
                    pool.wait_ge(c_hs, NT)
                nc.gpsimd.tensor_tensor(w1l[:, u, :], w1r[:, u, :], w1m[:, u, :], ALU.subtract).then_inc(m_wl, 1)

            def body_c(i, u):
                if live(i, NT):
                    pool.wait_ge(b_hte, NT)
                    if past(i, 4):
                        pool.wait_ge(c_qkv, i - 3)
                    nc.gpsimd.tensor_copy(hs[:, u % 4, :, :].rearrange("p b (r n) -> p b r n", r=2),
                                          xT[:, bass.ts(i, TP)].rearrange("p (b n) -> p b n", b=2).unsqueeze(2)
                                          .broadcast_to([128, 2, 2, NS])).then_inc(c_hs, 1)
                j = i - 5
                if live(j, NT):
                    rstd(stat(u - 5, MV1 + 1), stat(u - 5, LN1), stat(u - 5, RS1), c_mv, c_ln, c_rs, j)
                    pool.wait_ge(c_y, j + 1)
                    pool.wait_ge(b_rb, 2 * NT)
                    nc.gpsimd.tensor_tensor(acc[:, bass.ds(j, 1), :].rearrange("p i d -> p (i d)"), stage[0:TP, (u - 5) % 4, 0, :],
                                            x2n[:, bass.ds(j, 1), :].rearrange("p i d -> p (i d)"), ALU.add).then_inc(c_acc, 1)
                j = i - 2
                if live(j, NT):
                    pool.wait_ge(c_ri, j + 1)
                    p = pf[0:QP, u % 2, :].rearrange("p (h j) -> p h j", h=H)
                    nc.gpsimd.tensor_tensor(p, p, stat(u - 2, HRI, H, QP).unsqueeze(2).broadcast_to([QP, H, NS]),
                                            ALU.mult).then_inc(c_nrm, 1)
                j = i - 6
                if live(j, NT):
                    pool.wait_ge(c_xm, j + 1)
                    nc.gpsimd.tensor_tensor(xl[:, bass.ts(j, TP)], h2s[:, (u - 6) % 4, :], xm[:, u % 2, :],
                                            ALU.subtract).then_inc(c_xl, 1)
                if at(i, NT):
                    lower(0, 0)
                if at(i, NT + 2):
                    lower(1, 1)

            pipeline(pool, NT, 7, 8, 4, body_c)

            with pool.Fori(1, NE // 2, 1) as r:
                for u in range(2):
                    lower(r * 2 + u, u)

            for c in range(CH):
                four = slice(4 * c, 4 * c + 4)
                pool.wait_ge(f_mv, 4 * (c + 1))
                nc.gpsimd.tensor_tensor(gs[:, 1, four], gt[:, 1, four, 1], eps_ln[0:TP, :].broadcast_to([TP, 4]), ALU.add).then_inc(f_ln, 1)
                pool.wait_ge(f_ln, c + 1)
                nc.gpsimd.tensor_tensor(gs[:, 2, four], gs[:, 1, four], minus_half[0:TP, :].broadcast_to([TP, 4]), ALU.pow).then_inc(f_rs, 1)

        @block.scalar
        def _(act):
            def chunk(t, c):
                return t[:, c * CW:(c + 1) * CW]

            for c in range(CH):
                act.wait_ge(s_pe0, 1 + c)
                nc.scalar.copy(chunk(xT, c), ps[:, c, 0:CW]).then_inc(s_ev0, 1)
            for c in range(CH):
                act.wait_ge(s_pe0, 5 + c)
                nc.scalar.mul(chunk(qT, c), ps[:, 4 + c, 0:CW], SCALE_HD).then_inc(s_ev0, 1)
            for c in range(CH):
                act.wait_ge(s_pe0, 9 + c)
                nc.scalar.copy(chunk(kT, c), ps[:, c, 0:CW]).then_inc(s_ev0, 1)
            for c in range(CH):
                act.wait_ge(s_pe0, 13 + c)
                nc.scalar.copy(tmpA[0:HD, c * CW:(c + 1) * CW], ps[0:HD, 4 + c, 0:CW]).then_inc(s_ev0, 1)
            for c in range(CH):
                act.wait_ge(s_pe0, 17 + c)
                nc.scalar.copy(chunk(wT, c), ps[:, c, 0:CW])
                nc.scalar.activation(chunk(tmpB, c), ps[:, c, 0:CW], ACT.Square).then_inc(s_ev0, 1)
            for c in range(CH):
                act.wait_ge(s_pe0, 21 + c)
                nc.scalar.activation(chunk(bwT, c), ps[:, 4 + c, 0:CW], ACT.Exp, scale=-1.0).then_inc(s_ev0, 1)
            act.wait_ge(s_const, 1)
            for c in range(CH):
                act.wait_ge(s_pe0, 25 + c)
                nc.scalar.activation(chunk(tmpB, c), ps[:, c, 0:CW], ACT.Ln, bias=eps_ww[:, :]).then_inc(s_ev0, 1)
            act.wait_ge(s_ev0, 28)
            nc.scalar.activation(tmpB[:, :], tmpB[:, :], ACT.Exp, scale=-0.5).then_inc(s_act0, 1)
            act.wait_ge(s_dve0, 4)
            act.wait_ge(s_w1, NW1)
            for c in range(CH):
                act.wait_ge(s_pe0, 29 + c)
                nc.scalar.activation(chunk(fcT, c), ps[:, 4 + c, 0:CW], ACT.Identity, bias=delta[:, :]).then_inc(s_ev0, 1)
            act.wait_ge(s_ev0, 32)
            nc.scalar.activation(tmpA[:, :], fcT[:, :], ACT.Abs).then_inc(s_act0, 1)
            act.wait_ge(s_act0, 2)
            nc.scalar.activation(tmpA[:, :], tmpA[:, :], ACT.Exp, scale=-1.0).then_inc(s_act0, 1)
            act.wait_ge(s_act0, 3)
            nc.scalar.activation(tmpA[:, :], tmpA[:, :], ACT.Ln, bias=1.0).then_inc(s_act0, 1)

            for k in range(NK):
                W = T8 * (k + 1)
                act.wait_ge(s_sub, k + 1)
                e = E[:, k, :].rearrange("p (b j) -> p b j", j=NS)[:, :, 0:W]
                nc.scalar.activation(e, e, ACT.Exp).then_inc(s_exp, 1)

            def body_a(i, u):
                if live(i, NT):
                    act.wait_ge(a_tr, i + 1)
                    if past(i, 2):
                        act.wait_ge(a_pv, i - 1)
                    nc.scalar.copy(paT[0:TP, u % 2, :],
                                   ps[0:TP, 2 * (u % 2):2 * (u % 2) + 2, :].rearrange("p b n -> p (b n)")[:, 0:NK * 128])\
                        .then_inc(a_pt, 1)
                j = i - 1
                if live(j, NT):
                    act.wait_ge(a_pv, j + 1)
                    if past(j, 2):
                        act.wait_ge(a_wo, j - 1)
                    nc.scalar.copy(oTa[:, (u - 1) % 2, :], ps[:, 4 + (u - 1) % 2, 0:TP]).then_inc(a_o, 1)
                j = i - 3
                if live(j, NT):
                    act.wait_ge(a_xt, j + 1)
                    nc.scalar.copy(xT[:, bass.ts(j, TP)], ps[:, 7, 0:TP]).then_inc(a_xe, 1)

            pipeline(act, NT, 3, 8, 4, body_a)

            for c in range(CH):
                act.wait_ge(b_qx, c + 1)
                nc.scalar.activation(chunk(qx, c), ps[:, c, 0:CW], ACT.Identity, bias=BQ).then_inc(b_qxe, 1)

            def body_b(i, u):
                if live(i, NT):
                    act.wait_ge(b_qt, i + 1)
                    if past(i, 2):
                        act.wait_ge(b_sc, i - 1)
                    nc.scalar.copy(qts[:, u % 2, :], ps[:, 7, 0:TP]).then_inc(b_qte, 1)
                for q in (0, 2, 4):
                    if live(i, NT):
                        act.wait_ge(b_ct, 6 * i + q + 1)
                        b, t = q // 3, q % 3
                        nc.scalar.copy(cT[:, u % 2, b * NCTX + t * 4 * CR:b * NCTX + (t + 1) * 4 * CR],
                                       ps[:, 3, 0:4 * CR]).then_inc(b_cta, 1)
                    j = i - 4
                    if q == 2 and live(j, NT):
                        act.wait_ge(b_ont, j + 1)
                        if past(j, 2):
                            act.wait_ge(b_wv, j - 1)
                        nc.scalar.copy(oxT[:, u % 2, :].rearrange("p (b n) -> p b n", b=2),
                                       ps[:, 7, 128:256].rearrange("p (b n) -> p b n", b=2)[:, :, 0:NS]).then_inc(b_one, 1)
                j = i - 2
                if live(j, NT):
                    for r in range(2):
                        act.wait_ge(b_ptr, 3 * j + r + 1)
                        if r == 0 and past(j, 2):
                            act.wait_ge(b_pv, j - 1)
                        nc.scalar.copy(pxT[0:CR, u % 2, r * 4 * QP:(r + 1) * 4 * QP], ps[0:CR, 5, 0:4 * QP]).then_inc(b_pta, 1)
                j = i - 5
                if live(j, NT):
                    act.wait_ge(s_w2, NW2)
                    act.wait_ge(b_ht, j + 1)
                    nc.scalar.activation(xT[:, bass.ts(j, TP)], ps[:, 7, 384:384 + TP], ACT.Identity, bias=B1,
                                         scale=G1).then_inc(b_hte, 1)
                j = i - 1
                if live(j, NT):
                    act.wait_ge(b_nb, j + 1)
                    if past(j, 2):
                        act.wait_ge(b_ptr, 3 * (j - 1))
                    nc.scalar.activation(px[0:QP, (u - 1) % 2, :].rearrange("p (t n) -> p t n", t=3), ps[0:QP, 0:3, 0:4 * CR],
                                         ACT.Exp, bias=stat(u - 1, NBI, 1, QP), scale=SCALE_D,
                                         accum_out=stat(u - 1, DEN, 1, QP)).then_inc(b_exp, 1)

            pipeline(act, NT, 5, 8, 4, body_b)

            def upper_act(e, u):
                act.wait_ge(s_prep_ev, 4)
                if past(e, 2):
                    act.wait_ge(m_relu, CH * FC * (e - 1))
                nc.scalar.copy(b1e[:, u, :], b1T[:, bass.ds(e * FC, FC)]).then_inc(m_b1, 1)
                act.wait_ge(m_wm, e + 1)
                if past(e, 2):
                    act.wait_ge(m_hid, CH * FC * (e - 1))
                else:
                    act.wait_ge(c_hs, NT)
                nc.scalar.copy(w1h[:, u, :], w1m[:, u, :]).then_inc(m_wh, 1)

            def hidden_act(e, u, c):
                n = e * CH + c
                for f in range(FC):
                    if f == 0:
                        act.wait_ge(m_b1, e + 1)
                        if past(n, 2):
                            act.wait_ge(m_out, n - 1)
                    act.wait_ge(m_hid, n * FC + f + 1)
                    nc.scalar.activation(hid[:, c % 2, f, :], ps[:, 1 + f, 0:CW], ACT.Relu,
                                         bias=b1e[:, u, f:f + 1]).then_inc(m_relu, 1)

            def body_c(i, u):
                if live(i, NT):
                    act.wait_ge(c_qkv, i + 1)
                    if past(i, 2):
                        act.wait_ge(c_sc, i - 1)
                    nc.scalar.activation(qs[:, u % 2, :], ps[:, 0, 0:TP], ACT.Identity, bias=FQ).then_inc(c_q, 1)
                j = i - 5
                if live(j, NT):
                    act.wait_ge(c_ht, j + 1)
                    if past(j, 4):
                        act.wait_ge(c_gt, j - 3)
                        act.wait_ge(c_xl, j - 3)
                    nc.scalar.activation(h2s[:, (u - 5) % 4, :], ps[:, 0, 0:TP], ACT.Identity, bias=B2,
                                         scale=G2).then_inc(c_hte, 1)
                j = i - 2
                if live(j, NT):
                    act.wait_ge(c_ptr, j + 1)
                    if past(j, 2):
                        act.wait_ge(c_pv, j - 1)
                    nc.scalar.copy(pfT[0:TP, u % 2, :].rearrange("p (k n) -> p k n", k=2), ps[0:TP, 5:7, 0:4 * QP]).then_inc(c_pte, 1)
                j = i - 1
                if live(j, NT):
                    act.wait_ge(c_sub, j + 1)
                    p = pf[0:QP, (u - 1) % 2, :]
                    nc.scalar.activation(p, p, ACT.Exp, scale=SCALE_HD).then_inc(c_exp, 1)
                j = i - 3
                if live(j, NT):
                    act.wait_ge(c_pv, j + 1)
                    if past(j, 2):
                        act.wait_ge(c_wo, j - 1)
                    nc.scalar.activation(ofT[:, (u - 3) % 2, :], ps[:, 7, 0:TP], ACT.Identity, bias=FV).then_inc(c_o, 1)
                j = i - 6
                if live(j, NT):
                    act.wait_ge(c_xm, j + 1)
                    nc.scalar.copy(xh[:, bass.ts(j, TP)], xm[:, u % 2, :]).then_inc(c_xh, 1)
                if at(i, NT):
                    upper_act(0, 0)
                if at(i, NT + 2):
                    hidden_act(0, 0, 0)
                if at(i, NT + 4):
                    hidden_act(0, 0, 1)

            pipeline(act, NT, 6, 8, 4, body_c)

            hidden_act(0, 0, 2)
            act.wait_ge(m_link, 12)
            nc.scalar.activation(gs[:, 4, :], gs[:, 4, :], ACT.Exp).then_inc(m_e, 1)
            hidden_act(0, 0, 3)
            upper_act(1, 1)
            for c in range(CH):
                hidden_act(1, 1, c)
            with act.Fori(1, NE // 2, 1) as r:
                for u in range(2):
                    upper_act(r * 2 + u, u)
                    for c in range(CH):
                        hidden_act(r * 2 + u, u, c)

        @block.vector
        def _(dve):
            K, Wv, BW = tok(kT), tok(wT), tok(bwT)
            dve.wait_ge(s_w1, NW1)
            dve.tensor_copy(wb_rep[:, :].rearrange("p (h d) -> p h d", d=HD),
                            wbf[:, 0:H].unsqueeze(2).broadcast_to([D, H, HD])).then_inc(s_rep, 1)
            dve.tensor_copy(wf_rep[:, :].rearrange("p (h d) -> p h d", d=HD),
                            wbf[:, H:].unsqueeze(2).broadcast_to([D, H, HD])).then_inc(s_rep, 1)
            dve.wait_ge(s_ev0, 24)
            dve.tensor_scalar(bwT[:, :], bwT[:, :], 1.0, None, ALU.add).then_inc(s_dve0, 1)
            dve.wait_ge(s_dve0, 1)
            dve.reciprocal(bwT[:, :], bwT[:, :]).then_inc(s_dve0, 1)
            dve.wait_ge(s_act0, 1)
            dve.tensor_tensor(wT[:, :], wT[:, :], tmpB[:, :], ALU.mult).then_inc(s_dve0, 1)
            dve.wait_ge(s_dve0, 3)
            dve.scalar_tensor_tensor(bwT[:, :], bwT[:, :], 2.0, wT[:, :], ALU.mult, ALU.mult).then_inc(s_dve0, 1)
            dve.wait_ge(s_dve0, 4)
            dve.memset(tmpB[:, :], 1.0).then_inc(s_dve0, 1)
            dve.wait_ge(s_dve0, 5)
            dve.memset(tmpB[:, 0:NTOK:NS], 0.0).then_inc(s_dve0, 1)
            dve.wait_ge(s_act0, 4)
            dve.scalar_tensor_tensor(tmpA[:, :], fcT[:, :], 0.0, tmpA[:, :], ALU.min, ALU.subtract).then_inc(s_dve0, 1)
            dve.wait_ge(s_dve0, 7)
            dve.tensor_tensor_scan(fcT[:, :], tmpB[:, :], tmpA[:, :], 0.0, ALU.mult, ALU.add).then_inc(s_dve0, 1)
            for j in range(2):
                dve.wait_ge(s_v, j + 1)
                dve.tensor_copy(v_nat[:, 8 * j:8 * j + 8, :].rearrange("p (c i) d -> p c (i d)", c=2),
                                ps[0:TP, 2 * j:2 * j + 2, :]).then_inc(s_vev, 1)
            dve.wait_ge(s_prep, 1)
            dve.tensor_copy(xwqT[:, :], ps[:, 4, 0:D]).then_inc(s_prep_ev, 1)
            dve.tensor_copy(xwvT[:, :], ps[:, 4, D:2 * D]).then_inc(s_prep_ev, 1)
            dve.tensor_copy(b1T[:, :], ps[:, 4, 2 * D:2 * D + NE * FC]).then_inc(s_prep_ev, 1)
            dve.tensor_copy(rows_b[:, :], ps[0:TP, 5, 0:2 * D + NE]).then_inc(s_prep_ev, 1)
            dve.wait_ge(s_fct, 1)
            dve.tensor_copy(fct8[:, :, :], ps[:, 7, 0:NB * NK].rearrange("p (b k) -> p b k", k=NK)).then_inc(s_fct8, 1)

            def step_T(t, half):
                bs = slice(half * HB, (half + 1) * HB)
                if t >= 2:
                    dve.wait_ge(s_K, 2 * (t - 2) + half + 1)
                dve.tensor_tensor(Tw[:, half, 0:HB * t].rearrange("p (b j) -> p b j", j=t), K[:, bs, 0:t],
                                  Wv[:, bs, t:t + 1].broadcast_to([128, HB, t]), ALU.mult).then_inc(s_T, 1)

            def softmax_logits(k):
                W = T8 * (k + 1)
                e = E[:, k, :].rearrange("p (b j) -> p b j", j=NS)
                if k == 0:
                    dve.wait_ge(s_const, 3)
                    dve.wait_ge(s_fct8, 1)
                dve.wait_ge(s_S, 2 * T8 * (k + 1))
                dve.tensor_tensor(e[:, :, 0:W].rearrange("p (c b) j -> p c b j", c=CH),
                                  ps[:, 4:8, 0:GB * W].rearrange("p c (b j) -> p c b j", j=W),
                                  fct8[:, :, k:k + 1].rearrange("p (c b) k -> p c b k", c=CH).broadcast_to([128, CH, GB, W]),
                                  ALU.add).then_inc(s_Sev, 1)
                dve.wait_ge(s_Sev, k + 1)
                d = e[:, :, T8 * k:W]
                dve.tensor_tensor(d, d, causal8[:, :].unsqueeze(1).broadcast_to([128, NB, T8]), ALU.add).then_inc(s_msk, 1)
                dve.wait_ge(s_msk, k + 1)
                dve.tensor_reduce(rowmax[:, k % 2, :], e[:, :, 0:W], AX.X, ALU.max).then_inc(s_max, 1)
                dve.wait_ge(s_max, k + 1)
                dve.tensor_tensor(e[:, :, 0:W], e[:, :, 0:W],
                                  rowmax[:, k % 2, :].unsqueeze(2).broadcast_to([128, NB, W]), ALU.subtract).then_inc(s_sub, 1)

            def softmax_sum(k):
                W = T8 * (k + 1)
                e = E[:, k, :].rearrange("p (b j) -> p b j", j=NS)
                dve.wait_ge(s_exp, k + 1)
                dve.tensor_reduce(rowsum[:, k, :], e[:, :, 0:W], AX.X, ALU.add).then_inc(s_sum, 1)
                dve.wait_ge(s_sum, k + 1)
                dve.reciprocal(rinv[:, k, :], rowsum[:, k, :]).then_inc(s_rinv, 1)

            for half in range(2):
                step_T(1, half)
            for t in range(1, NS):
                for half in range(2):
                    bs = slice(half * HB, (half + 1) * HB)
                    x = Xw[:, half, 0:HB * t]
                    dve.wait_ge(s_U, 2 * (t - 1) + half + 1)
                    dve.tensor_tensor(x.rearrange("p (c b j) -> p c b j", c=2, j=t),
                                      ps[:, 2 * half:2 * half + 2, 0:GB * t].rearrange("p c (b j) -> p c b j", j=t),
                                      BW[:, bs, t:t + 1].rearrange("p (c b) n -> p c b n", c=2).broadcast_to([128, 2, GB, t]),
                                      ALU.mult).then_inc(s_X, 1)
                    dve.wait_ge(s_X, 2 * (t - 1) + half + 1)
                    dve.wait_ge(s_Tq, 2 * (t - 1) + half + 1)
                    dve.tensor_tensor(K[:, bs, 0:t], K[:, bs, 0:t], x.rearrange("p (b j) -> p b j", j=t),
                                      ALU.subtract).then_inc(s_K, 1)
                    if t + 1 < NS:
                        step_T(t + 1, half)
                if t % T8 == 0:
                    softmax_logits(t // T8 - 1)
                if t % T8 == 2 and t > T8:
                    softmax_sum(t // T8 - 1)
            softmax_logits(NK - 1)
            softmax_sum(NK - 1)

            dve.wait_ge(s_S, 2 * NS)
            dve.wait_ge(s_rinv, NK)

            def body_a(i, u):
                if live(i, NT):
                    if past(i, 2):
                        dve.wait_ge(a_tr, i - 1)
                    dve.tensor_tensor(pa[:, u % 2, :].rearrange("p (k b j) -> p k b j", k=NK, b=2),
                                      E[:, :, bass.ts(i, TP)].rearrange("p k (b j) -> p k b j", b=2),
                                      rinv[:, :, bass.ts(i, 2)].unsqueeze(3).broadcast_to([128, NK, 2, NS]),
                                      ALU.mult).then_inc(a_ps, 1)
                j = i - 2
                if live(j, NT):
                    y, x1 = stage[0:TP, (u - 2) % 4, 0, :], stage[0:TP, (u - 2) % 4, 1, :]
                    dve.wait_ge(a_wo, j + 1)
                    dve.tensor_tensor(y, ps[0:TP, 6, 0:D], res[:, bass.ds(j, 1), :].rearrange("p i d -> p (i d)"), ALU.add).then_inc(a_y, 1)
                    dve.wait_ge(a_y, j + 1)
                    dve.bn_stats(stat(u - 2, ST1, 6), y).then_inc(a_st, 1)
                    dve.wait_ge(s_vev, 2)
                    dve.wait_ge(a_st, j + 1)
                    dve.bn_aggr(stat(u - 2, MV1, 2), stat(u - 2, ST1, 6)).then_inc(a_mv, 1)
                    dve.wait_ge(a_rs, j + 1)
                    if past(j, 4):
                        dve.wait_ge(a_rb, j - 3)
                    dve.tensor_scalar(x1, y, stat(u - 2, MV1), stat(u - 2, RS1), ALU.subtract, ALU.mult).then_inc(a_x1, 1)

            pipeline(dve, NT, 3, 8, 4, body_a)

            def normalise(i, u):
                j = i - 3
                if live(j, NT):
                    dve.wait_ge(b_exp, j + 1)
                    dve.reciprocal(stat(u - 3, RDN, 1, QP), stat(u - 3, DEN, 1, QP)).then_inc(b_rd, 1)
                    dve.wait_ge(b_rd, j + 1)
                    dve.wait_ge(b_pv, j + 1)
                    if past(j, 2):
                        dve.wait_ge(b_ont, j - 1)
                    dve.tensor_scalar(onx[:, (u - 3) % 2, :], ps[0:QP, 6, 0:D], stat(u - 3, RDN, 1, QP), None,
                                      ALU.mult).then_inc(b_on, 1)

            def residual(i, u, y):
                j = i - 4
                if live(j, NT):
                    dve.wait_ge(b_wv, j + 1)
                    dve.tensor_tensor(y, ps[0:TP, 7, 256:384], res[:, bass.ds(j, 1), :].rearrange("p i d -> p (i d)"), ALU.add).then_inc(b_y, 1)
                    dve.wait_ge(b_y, j + 1)
                    dve.bn_stats(stat(u, ST1, 6), y).then_inc(b_st, 1)
                    dve.wait_ge(s_vev, 2)
                    dve.wait_ge(b_st, j + 1)
                    dve.bn_aggr(stat(u, MV1, 2), stat(u, ST1, 6)).then_inc(b_mv, 1)

            def body_b(i, u):
                y, x2, h = (stage[0:TP, u % 4, k, :] for k in range(3))
                if live(i, NT):
                    dve.wait_ge(b_qte, i + 1)
                    dve.tensor_copy(stat(u, QB, 1, QP), ps[0:QP, 7, TP:TP + 1]).then_inc(b_qb, 1)
                for q in (1, 3, 5):
                    if live(i, NT):
                        dve.wait_ge(b_ct, 6 * i + q + 1)
                        if q == 1 and past(i, 2):
                            dve.wait_ge(b_sc, i - 1)
                        b, t = q // 3, q % 3
                        dve.tensor_copy(cT[:, u % 2, b * NCTX + t * 4 * CR:b * NCTX + (t + 1) * 4 * CR],
                                        ps[:, 4, 0:4 * CR]).then_inc(b_ctd, 1)
                    if q == 3:
                        normalise(i, u)
                        residual(i, u, y)

                j = i - 1
                if live(j, NT):
                    dve.wait_ge(b_sc, j + 1)
                    dve.tensor_reduce(stat(u - 1, MX, 1, QP), ps[0:QP, 0:3, 0:4 * CR], AX.XY, ALU.max).then_inc(b_mx, 1)
                    dve.wait_ge(b_mx, j + 1)
                    dve.tensor_scalar(stat(u - 1, M2, 1, QP), stat(u - 1, MX, 1, QP), stat(u - 1, QB, 1, QP), None,
                                      ALU.add).then_inc(b_m2, 1)
                    dve.wait_ge(b_m2, j + 1)
                    dve.tensor_scalar(stat(u - 1, NBI, 1, QP), stat(u - 1, M2, 1, QP), stat(u - 1, QB, 1, QP), -SCALE_D,
                                      ALU.subtract, ALU.mult).then_inc(b_nb, 1)
                j = i - 2
                if live(j, NT):
                    dve.wait_ge(b_ptr, 3 * j + 3)
                    if past(j, 2):
                        dve.wait_ge(b_pv, j - 1)
                    dve.tensor_copy(pxT[0:CR, u % 2, 2 * 4 * QP:], ps[0:CR, 5, 0:4 * QP]).then_inc(b_ptd, 1)
                j = i - 4
                if live(j, NT):
                    dve.wait_ge(b_rs, j + 1)
                    if past(j, 4):
                        dve.wait_ge(b_rb, 2 * (j - 3))
                    dve.tensor_scalar(x2, y, stat(u, MV1), stat(u, RS1), ALU.subtract, ALU.mult).then_inc(b_x2, 1)
                    dve.wait_ge(b_x2, j + 1)
                    dve.bn_stats(stat(u, ST2, 6), x2).then_inc(b_st2, 1)
                    dve.wait_ge(s_vev, 2)
                    dve.wait_ge(b_st2, j + 1)
                    dve.bn_aggr(stat(u, MV2, 2), stat(u, ST2, 6)).then_inc(b_mv2, 1)
                    dve.wait_ge(b_rs2, j + 1)
                    if past(j, 4):
                        dve.wait_ge(b_ht, j - 3)
                    dve.tensor_scalar(h, x2, stat(u, MV2), stat(u, RS2), ALU.subtract, ALU.mult).then_inc(b_h, 1)

            pipeline(dve, NT, 5, 8, 4, body_b)

            def upper(e, u):
                dve.wait_ge(m_w[u], 16 * (e - u) + 32)
                if past(e, 2):
                    dve.wait_ge(m_wh, e - 1)
                    dve.wait_ge(m_wl, e - 1)
                dve.tensor_scalar(w1m[:, u, :].bitcast(I32), w1r[:, u, :].bitcast(I32), UPPER, None,
                                  ALU.bitwise_and).then_inc(m_wm, 1)

            dve.wait_ge(c_zero, 1)
            dve.wait_ge(b_rb, 2 * NT)

            def body_c(i, u):
                if live(i, NT):
                    dve.wait_ge(c_q, i + 1)
                    if past(i, 2):
                        dve.wait_ge(c_sc, i - 1)
                    dve.scalar_tensor_tensor(km[:, u % 2, :, :], ps[:, 0, TP:2 * TP].unsqueeze(1).broadcast_to([128, 4, TP]), FK,
                                             quad_mask[:, :].unsqueeze(2).broadcast_to([128, 4, TP]), ALU.add, ALU.mult)\
                        .then_inc(c_km, 1)
                    if past(i, 4):
                        dve.wait_ge(c_pv, i - 3)
                    dve.tensor_tensor(vpf[0:TP, u % 4, :, :].rearrange("p b (k c) -> p b k c", c=48)[:, :, :, 0:2 * HD],
                                      ps[0:TP, 0, 2 * TP:2 * TP + 2 * D].rearrange("p (b k c) -> p b k c", b=2, c=2 * HD),
                                      half_mask[:, :].unsqueeze(1).unsqueeze(1).broadcast_to([TP, 2, 8, 2 * HD]),
                                      ALU.mult).then_inc(c_vp, 1)
                j = i - 4
                y, h = stage[0:TP, u % 4, 0, :], stage[0:TP, u % 4, 2, :]
                if live(j, NT):
                    dve.wait_ge(c_wo, j + 1)
                    if past(j, 4):
                        dve.wait_ge(c_acc, j - 3)
                    dve.tensor_tensor(y, ps[0:TP, 7, 128:256], res[:, bass.ds(j, 1), :].rearrange("p i d -> p (i d)"), ALU.add).then_inc(c_y, 1)
                    dve.wait_ge(c_y, j + 1)
                    dve.bn_stats(stat(u, ST1, 6), y).then_inc(c_st, 1)
                    dve.wait_ge(s_vev, 2)
                    dve.wait_ge(c_st, j + 1)
                    dve.bn_aggr(stat(u, MV1, 2), stat(u, ST1, 6)).then_inc(c_mv, 1)
                j = i - 6
                if live(j, NT):
                    dve.wait_ge(c_hte, j + 1)
                    if past(j, 2):
                        dve.wait_ge(c_xl, j - 1)
                        dve.wait_ge(c_xh, j - 1)
                    dve.tensor_scalar(xm[:, u % 2, :].bitcast(I32), h2s[:, (u - 6) % 4, :].bitcast(I32), UPPER, None,
                                      ALU.bitwise_and).then_inc(c_xm, 1)
                j = i - 1
                p = pf[0:QP, (u - 1) % 2, :]
                if live(j, NT):
                    sc = ps[0:QP, 1:5, 0:4 * NS].rearrange("p g (h j) -> p g h j", j=NS)
                    dve.wait_ge(c_sc, j + 1)
                    dve.tensor_reduce(stat(u - 1, HMX, H, QP).rearrange("p (g h) -> p g h", g=4), sc, AX.X, ALU.max).then_inc(c_mx, 1)
                    dve.wait_ge(c_mx, j + 1)
                    if past(j, 2):
                        dve.wait_ge(c_ptr, j - 1)
                    dve.tensor_tensor(p.rearrange("p (g h j) -> p g h j", g=4, j=NS), sc,
                                      stat(u - 1, HMX, H, QP).rearrange("p (g h) -> p g h", g=4).unsqueeze(3)
                                      .broadcast_to([QP, 4, 4, NS]), ALU.subtract).then_inc(c_sub, 1)
                j = i - 4
                if live(j, NT):
                    dve.wait_ge(c_rs, j + 1)
                    if past(j, 4):
                        dve.wait_ge(c_ht, j - 3)
                    dve.tensor_scalar(h, y, stat(u, MV1), stat(u, RS1), ALU.subtract, ALU.mult).then_inc(c_h, 1)
                j = i - 6
                if live(j, NT):
                    dve.wait_ge(c_gt, j + 1)
                    dve.tensor_tensor(lg[:, bass.ds(j, 1), :].rearrange("p i d -> p (i d)"), ps[0:TP, 0, 480:480 + NE], GBR, ALU.add).then_inc(c_lg, 1)
                j = i - 1
                if live(j, NT):
                    dve.wait_ge(c_exp, j + 1)
                    dve.tensor_reduce(stat(u - 1, HSM, H, QP), p.rearrange("p (h j) -> p h j", j=NS), AX.X, ALU.add).then_inc(c_sum, 1)
                    dve.wait_ge(c_sum, j + 1)
                    dve.reciprocal(stat(u - 1, HRI, H, QP), stat(u - 1, HSM, H, QP)).then_inc(c_ri, 1)

            for i in range(8):
                body_c(i, i % 4)
            for e in range(2):
                upper(e, e)
            with dve.Fori(8 // 4, NT // 4, 1) as r:
                for u in range(4):
                    body_c(r * 4 + u, u)
            for i in range(NT, NT + 6):
                body_c(i, i % 4)

            links = [0]

            def link(ins):
                links[0] += 1
                ins.then_inc(m_link, 1)
                dve.wait_ge(m_link, links[0])

            dve.wait_ge(c_lg, NT)

            def wide(x):
                return x.unsqueeze(2).broadcast_to([TP, NT, NE])

            iota_w = iota8[:, :].unsqueeze(1).broadcast_to([TP, NT, NE])
            eq, val, one1, l2, one2 = (gt[:, k, :, :] for k in range(5))

            def largest(logits, top, one):
                link(dve.tensor_reduce(top, logits, AX.X, ALU.max))
                link(dve.tensor_tensor(eq, logits, wide(top), ALU.is_equal))
                link(dve.scalar_tensor_tensor(val, eq, -float(NE), iota_w, ALU.mult, ALU.add))
                link(dve.tensor_reduce(gs[:, 5, :], val, AX.X, ALU.min))
                link(dve.tensor_tensor(one, val, wide(gs[:, 5, :]), ALU.is_equal))

            largest(lg[:, :, :], gs[:, 0, :], one1)
            link(dve.scalar_tensor_tensor(l2, one1, NEG, lg[:, :, :], ALU.mult, ALU.add))
            largest(l2, gs[:, 1, :], one2)
            link(dve.tensor_tensor(gs[:, 4, :], gs[:, 1, :], gs[:, 0, :], ALU.subtract))
            dve.wait_ge(m_e, 1)
            link(dve.tensor_scalar(gs[:, 2, :], gs[:, 4, :], 1.0, None, ALU.add))
            link(dve.reciprocal(gs[:, 3, :], gs[:, 2, :]))
            link(dve.tensor_tensor(gs[:, 2, :], gs[:, 4, :], gs[:, 3, :], ALU.mult))
            link(dve.tensor_tensor(one1, one1, wide(gs[:, 3, :]), ALU.mult))
            link(dve.tensor_tensor(one2, one2, wide(gs[:, 2, :]), ALU.mult))
            dve.tensor_tensor(ew[:, :, :], one1, one2, ALU.add).then_inc(m_ew, 1)
            stats = gt[:, 2:4, :, :].rearrange("p k i e -> p (k i e)")

            def last_norm(c):
                four = range(4 * c, 4 * c + 4)
                for i in four:
                    dve.wait_ge(m_acc, 4 * ((NE - 1) * CH + c + 1))
                    dve.bn_stats(stats[:, 6 * i:6 * i + 6], acc[:, i, :]).then_inc(f_st, 1)
                for i in four:
                    dve.wait_ge(f_st, i + 1)
                    dve.bn_aggr(gt[:, 1, i, 0:2], stats[:, 6 * i:6 * i + 6]).then_inc(f_mv, 1)
                for i in four:
                    dve.wait_ge(f_mv, i + 1)
                    dve.wait_ge(f_rs, c + 1)
                    dve.tensor_scalar(acc[:, i, :], acc[:, i, :], gt[:, 1, i, 0:1], gs[:, 2, i:i + 1],
                                      ALU.subtract, ALU.mult).then_inc(f_y, 1)

            def weigh(e, c):
                n = e * CH + c
                dve.wait_ge(m_out, n + 1)
                if past(n, CH):
                    dve.wait_ge(m_acc, 4 * (n - 3))
                for k in range(4):
                    t = acc[:, 4 * c + k, :]
                    dve.scalar_tensor_tensor(t, ps[0:TP, 5 + c % 2, k * D:(k + 1) * D],
                                             ew[:, 4 * c + k, bass.ds(e, 1)], t, ALU.mult, ALU.add).then_inc(m_acc, 1)

            def spread(c):
                dve.wait_ge(m_ewt, c + 1)
                dve.tensor_copy(ewT[:, c * CW:(c + 1) * CW], ps[0:NE, 7 * (1 - c % 2), 0:CW]).then_inc(m_ewe, 1)

            def second_bias(c):
                dve.wait_ge(m_b2, c + 1)
                dve.wait_ge(m_acc, 4 * (c + 1))
                t = acc[:, 4 * c:4 * c + 4, :]
                dve.tensor_tensor(t, t, ps[0:TP, 7 * (1 - c % 2), :].rearrange("p (i d) -> p i d", d=D), ALU.add).then_inc(m_acc0, 1)

            dve.wait_ge(c_acc, NT)
            dve.wait_ge(m_ew, 1)
            weigh(0, 0)
            spread(0); spread(1)
            weigh(0, 1)
            spread(2); spread(3)
            weigh(0, 2)
            weigh(0, 3)
            second_bias(0); second_bias(1)
            upper(2, 0)
            dve.wait_ge(m_acc0, 1)
            weigh(1, 0)
            second_bias(2); second_bias(3)
            for c in range(1, CH):
                dve.wait_ge(m_acc0, c + 1)
                weigh(1, c)
            for u in range(2):
                upper(3 + u, 1 - u)
                for c in range(CH):
                    weigh(2 + u, c)
            with dve.Fori(2, NE // 2 - 1, 1) as r:
                for u in range(2):
                    upper(r * 2 + u + 1, 1 - u)
                    for c in range(CH):
                        weigh(r * 2 + u, c)
            upper(NE - 1, 1)
            for e in range(NE - 2, NE):
                for c in range(CH):
                    weigh(e, c)
                    if e == NE - 1:
                        last_norm(c)

        @block.tensor
        def _(pe):
            pe.wait_ge(s_const, 1)
            pe.wait_ge(s_x, 16)
            for c in range(CH):
                for i in range(4):
                    last = pe.transpose(ps[:, c, i * TP:(i + 1) * TP], res[:, 4 * c + i, :], ident[0:TP, 0:TP])
                last.then_inc(s_pe0, 1)

            def project(first, w, src, bank, need):
                for c in range(CH):
                    pe.wait_ge(s_ev0, need + c)
                    pe.matmul(ps[0:w.shape[1], bank + c, 0:CW], w, src[0:w.shape[0], c * CW:(c + 1) * CW],
                              start=True, stop=True).then_inc(s_pe0, 1)

            pe.wait_ge(s_w1, NW1)
            pe.wait_ge(s_rep, 2)
            project(5, wq[:, :], xT, 4, 1)
            project(9, wk[:, :], xT, 0, 1)
            project(13, ww1[:, :], xT, 4, 5)
            project(17, ww2[:, :], tmpA, 0, 13)
            project(21, wb_rep[:, :], xT, 4, 13)
            pe.wait_ge(s_const, 2)
            project(25, blockones[:, :], tmpB, 0, 17)
            project(29, wf_rep[:, :], xT, 4, 21)
            pe.wait_ge(s_ev0, 28)
            for i in range(NT):
                mm = pe.matmul(ps[0:TP, i // 4, (i % 4) * D:(i % 4 + 1) * D], xT[:, i * TP:(i + 1) * TP], wv[:, :],
                               start=True, stop=True)
                if i % 8 == 7:
                    mm.then_inc(s_v, 1)
            pe.wait_ge(s_dve0, 8)
            pe.wait_ge(s_ev0, 32)
            pe.wait_ge(s_w2, NW2)
            pe.transpose(ps[:, 4, 0:D], xw[:, 0, :], ident[:, :])
            pe.transpose(ps[:, 4, D:2 * D], xw[:, 1, :], ident[:, :])
            pe.transpose(ps[:, 4, 2 * D:2 * D + NE * FC], b1_nat[:, :], ident[0:NE * FC, 0:NE * FC])
            pe.matmul(ps[0:TP, 5, 0:2 * D + NE], ones_row[:, :], rows[:, :], start=True, stop=True).then_inc(s_prep, 1)
            F = fcT[:, :].rearrange("p (b k t) -> p b k t", k=NK, t=T8)
            for t in range(T8):
                mm = pe.matmul(ps[:, 7, 0:NB * NK], fc_win[:, (7 - t) * H:(15 - t) * H], F[:, :, :, t],
                               start=(t == 0), stop=(t == T8 - 1))
            mm.then_inc(s_fct, 1)
            pe.wait_ge(s_fct8, 1)
            pe.wait_ge(s_prep_ev, 4)
            pe.wait_ge(s_vev, 2)

            def reduce_U(t, half):
                pe.wait_ge(s_T, 2 * (t - 1) + half + 1)
                for c in range(2):
                    mm = pe.matmul(ps[:, 2 * half + c, 0:GB * t], blockones[:, :],
                                   Tw[:, half, c * GB * t:(c + 1) * GB * t], start=True, stop=True)
                mm.then_inc(s_U, 1)

            def reduce_S(t, half):
                k, W = t // T8, T8 * (t // T8 + 1)
                if t % T8 == 0:
                    if k > 0:
                        pe.wait_ge(s_Sev, k)
                    for c in range(2 * half, 2 * half + 2):
                        pe.matmul(ps[:, 4 + c, 0:GB * W], fc_neg[:, :], tok(fcT)[:, c * GB:(c + 1) * GB, 0:W],
                                  start=True, stop=False)
                pe.wait_ge(s_Tq, 2 * t + half + 1)
                for c in range(2):
                    mm = pe.matmul(ps[:, 4 + 2 * half + c, 0:GB * W], head_win[:, (7 - t % T8) * H:(15 - t % T8) * H],
                                   Tq[:, half, t % 2, c * GB * W:(c + 1) * GB * W],
                                   start=False, stop=(t % T8 == T8 - 1))
                mm.then_inc(s_S, 1)

            for t in range(NS):
                for half in range(2):
                    if t + 1 < NS:
                        reduce_U(t + 1, half)
                    reduce_S(t, half)

            def body_a(i, u):
                if live(i, NT):
                    pe.wait_ge(a_ps, i + 1)
                    if past(i, 2):
                        pe.wait_ge(a_pt, i - 1)
                    for k in range(NK):
                        mm = pe.transpose(ps[0:TP, 2 * (u % 2) + k // 4, (k % 4) * 128:(k % 4 + 1) * 128],
                                          pa[:, u % 2, k * TP:(k + 1) * TP], ident[:, :])
                    mm.then_inc(a_tr, 1)
                j = i - 2
                if live(j, NT):
                    pe.wait_ge(a_o, j + 1)
                    if past(j, 1):
                        pe.wait_ge(a_y, j)
                    pe.matmul(ps[0:TP, 6, 0:D], oTa[:, u % 2, :], wo[:, :], start=True, stop=True).then_inc(a_wo, 1)
                j = i - 3
                if live(j, NT):
                    pe.wait_ge(a_x1, j + 1)
                    if past(j, 1):
                        pe.wait_ge(a_xe, j)
                    pe.transpose(ps[:, 7, 0:TP], stage[0:TP, (u - 3) % 4, 1, :], ident[0:TP, 0:TP]).then_inc(a_xt, 1)
                j = i - 1
                if live(j, NT):
                    v = (u - 1) % 2
                    pe.wait_ge(a_pt, j + 1)
                    pe.wait_ge(a_vp, 2 * (j + 1))
                    if past(j, 2):
                        pe.wait_ge(a_o, j - 1)
                    for b in range(2):
                        for hh in range(4):
                            for g in range(4):
                                h = 4 * g + hh
                                mm = pe.matmul(ps[32 * g:32 * g + 32, 4 + v, b * NS:(b + 1) * NS],
                                               vpa[0:TP, v, b, g * 160 + hh * 32:g * 160 + hh * 32 + 32],
                                               paT[0:TP, v, h:NK * 128:H], start=(hh == 0), stop=(hh == 3),
                                               tile_position=(0, 32 * g))
                    mm.then_inc(a_pv, 1)

            pipeline(pe, NT, 3, 8, 4, body_a)

            pe.wait_ge(a_xe, NT)
            pe.wait_ge(a_pt, NT)
            for c in range(CH):
                pe.matmul(ps[:, c, 0:CW], xwqT[:, :], xT[:, c * CW:(c + 1) * CW], start=True, stop=True).then_inc(b_qx, 1)
            pe.wait_ge(b_qxe, CH)

            def outputs_b(j, uj, q):
                if live(j, NT):
                    w = uj % 2
                    if q < 2:
                        pe.wait_ge(b_pta, 2 * j + q + 1)
                    else:
                        pe.wait_ge(b_ptd, j + 1)
                    if q == 0 and past(j, 1):
                        pe.wait_ge(b_on, j)
                    for c in range(4 * q, 4 * q + 4):
                        for b in range(2):
                            mm = pe.matmul(ps[64 * b:64 * b + NS, 6, 0:D], pxT[0:CR, w, c * QP + 64 * b:c * QP + 64 * b + NS],
                                           ctxr[0:CR, uj % 4, b, c * D:(c + 1) * D],
                                           start=(c == 0), stop=(c == NCC - 1))
                    if q == 2:
                        mm.then_inc(b_pv, 1)

            def body_b(i, u):
                v = u % 2
                if live(i, NT):
                    pe.wait_ge(b_qxs, i + 1)
                    if not isinstance(i, int) or i >= 6:
                        pe.wait_ge(b_hte, i - 5)
                    if live(i - 5, NT):
                        pe.wait_ge(b_y, i - 4)
                    pe.matmul(ps[:, 7, 0:TP], xw[:, 2, :], qxs[:, v, :], start=True, stop=True)
                    for b in range(2):
                        mm = pe.matmul(ps[64 * b:64 * b + NS, 7, TP:TP + 1], qxs[:, v, b * NS:(b + 1) * NS], BK,
                                       start=True, stop=True)
                    mm.then_inc(b_qt, 1)
                for q in range(6):
                    b, t = q // 3, q % 3
                    if live(i, NT):
                        if q == 0:
                            pe.wait_ge(b_ctx[u], 4 * (i - u) + 16)
                        evacuated = b_ctd if q % 2 else b_cta
                        if q >= 2 or past(i, 1):
                            pe.wait_ge(evacuated, 3 * i + q // 2)
                        for k in range(4):
                            c = 4 * t + k
                            mm = pe.transpose(ps[:, 3 + q % 2, k * CR:(k + 1) * CR], ctxr[0:CR, u, b, c * D:(c + 1) * D],
                                              ident[0:CR, 0:CR])
                        mm.then_inc(b_ct, 1)
                    j = i - 1
                    if live(j, NT):
                        if q == 0:
                            pe.wait_ge(b_cta, 3 * (j + 1))
                            pe.wait_ge(b_ctd, 3 * (j + 1))
                            pe.wait_ge(b_qte, j + 1)
                            if past(j, 1):
                                pe.wait_ge(b_exp, j)
                        w = (u - 1) % 2
                        mm = pe.matmul(ps[64 * b:64 * b + NS, t, 0:4 * CR], qts[:, w, b * NS:(b + 1) * NS],
                                       cT[:, w, b * NCTX + t * 4 * CR:b * NCTX + (t + 1) * 4 * CR], start=True, stop=True)
                        if q == 5:
                            mm.then_inc(b_sc, 1)
                    j = i - 4
                    if q == 2 and live(j, NT):
                        pe.wait_ge(b_on, j + 1)
                        if live(i, NT):
                            pe.wait_ge(b_qte, i + 1)
                            pe.wait_ge(b_qb, i + 1)
                        else:
                            pe.wait_ge(b_hte, i - 5)
                        pe.transpose(ps[:, 7, 128:128 + QP], onx[:, v, :], ident[0:QP, 0:QP]).then_inc(b_ont, 1)
                    if q == 2:
                        outputs_b(i - 3, u - 3, 2)
                    if q == 4 and live(j, NT):
                        pe.wait_ge(b_one, j + 1)
                        pe.matmul(ps[0:TP, 7, 256:384], oxT[:, v, :], xwvT[:, :], start=True, stop=True).then_inc(b_wv, 1)
                for r in range(3):
                    j = i - 2
                    if live(j, NT):
                        pe.wait_ge(b_exp, j + 1)
                        if r > 0:
                            pe.wait_ge(b_pta, 2 * j + r)
                        elif past(j, 1):
                            pe.wait_ge(b_ptd, j)
                        for k in range(4):
                            c = 4 * r + k
                            mm = pe.transpose(ps[0:CR, 5, k * QP:(k + 1) * QP], px[0:QP, v, c * CR:(c + 1) * CR],
                                              ident[0:QP, 0:QP])
                        mm.then_inc(b_ptr, 1)
                    if r > 0:
                        outputs_b(i - 2, u - 2, r - 1)
                    j = i - 5
                    if r == 0 and live(j, NT):
                        pe.wait_ge(b_h, j + 1)
                        if live(i - 4, NT):
                            pe.wait_ge(b_y, i - 3)
                        elif past(j, 1):
                            pe.wait_ge(b_hte, j)
                        pe.transpose(ps[:, 7, 384:384 + TP], stage[0:TP, (u - 5) % 4, 2, :], ident[0:TP, 0:TP]).then_inc(b_ht, 1)

            pipeline(pe, NT, 5, 8, 4, body_b)

            def hidden(e, u, c):
                n = e * CH + c
                if c == 0:
                    pe.wait_ge(m_wl, e + 1)
                    pe.wait_ge(m_wh, e + 1)
                for f in range(FC):
                    if past(n, 1):
                        pe.wait_ge(m_relu, FC * (n - 1) + f + 1)
                    for part, (w, x) in enumerate(((w1h, xh), (w1h, xl), (w1l, xh))):
                        mm = pe.matmul(ps[:, 1 + f, 0:CW], w[:, u, f * 128:(f + 1) * 128],
                                       x[:, c * CW:(c + 1) * CW], start=(part == 0), stop=(part == 2))
                    mm.then_inc(m_hid, 1)

            def outputs(e, u, c):
                n = e * CH + c
                if c == 0:
                    pe.wait_ge(m_w[u], 16 * (e - u) + 32)
                pe.wait_ge(m_relu, FC * (n + 1))
                if past(n, 2):
                    pe.wait_ge(m_acc, 4 * (n - 1))
                for k in range(4):
                    for f in range(FC):
                        mm = pe.matmul(ps[0:TP, 5 + c % 2, k * D:(k + 1) * D], hid[:, c % 2, f, k * TP:(k + 1) * TP],
                                       w2r[:, u, f, :], start=(f == 0), stop=(f == FC - 1))
                mm.then_inc(m_out, 1)

            def scores_c(j, u, b):
                for g in range(4):
                    rs = slice(32 * g, 32 * g + 32)
                    mm = pe.matmul(ps[64 * b:64 * b + NS, 1 + g, 0:4 * NS], qs[rs, u % 2, b * NS:(b + 1) * NS],
                                   km[rs, u % 2, :, b * NS:(b + 1) * NS], start=True, stop=True,
                                   tile_position=(32 * g, 64 * b))
                if b == 1:
                    mm.then_inc(c_sc, 1)

            def body_c(i, u):
                v = u % 2
                if live(i, NT):
                    pe.wait_ge(c_hs, i + 1)
                    if past(i, 1):
                        pe.wait_ge(c_q, i)
                        pe.wait_ge(c_km, i)
                        pe.wait_ge(c_vp, i)
                    if live(i - 6, NT):
                        pe.wait_ge(c_hte, i - 5)
                    if live(i - 7, NT):
                        pe.wait_ge(c_lg, i - 6)
                    h1 = hs[:, u % 4, :, 0:NS]
                    pe.matmul(ps[:, 0, 0:TP], wqkv[:, 0:D], h1, start=True, stop=True)
                    pe.matmul(ps[:, 0, TP:2 * TP], wqkv[:, D:2 * D], h1, start=True, stop=True)
                    for b in range(2):
                        mm = pe.matmul(ps[0:TP, 0, 2 * TP + b * D:2 * TP + (b + 1) * D], hs[:, u % 4, b, :], wqkv[:, 2 * D:3 * D],
                                       start=True, stop=True)
                    mm.then_inc(c_qkv, 1)
                j = i - 1
                if live(j, NT):
                    pe.wait_ge(c_q, j + 1)
                    pe.wait_ge(c_km, j + 1)
                    if past(j, 1):
                        pe.wait_ge(c_sub, j)
                    scores_c(j, u - 1, 0)
                j = i - 4
                if live(j, NT):
                    pe.wait_ge(c_o, j + 1)
                    pe.matmul(ps[0:TP, 7, 128:256], ofT[:, v, :], w_o[:, :], start=True, stop=True).then_inc(c_wo, 1)
                j = i - 1
                if live(j, NT):
                    scores_c(j, u - 1, 1)
                j = i - 5
                if live(j, NT):
                    pe.wait_ge(c_h, j + 1)
                    if live(i, NT):
                        pe.wait_ge(c_vp, i + 1)
                        pe.wait_ge(c_q, i + 1)
                        pe.wait_ge(c_km, i + 1)
                    elif past(j, 2):
                        pe.wait_ge(c_lg, j - 1)
                    pe.transpose(ps[:, 0, 0:TP], stage[0:TP, (u - 5) % 4, 2, :], ident[0:TP, 0:TP]).then_inc(c_ht, 1)
                j = i - 2
                if live(j, NT):
                    pe.wait_ge(c_nrm, j + 1)
                    if past(j, 1):
                        pe.wait_ge(c_pte, j)
                    for k in range(8):
                        mm = pe.transpose(ps[0:TP, 5 + k // 4, (k % 4) * QP:(k % 4 + 1) * QP], pf[0:QP, v, k * TP:(k + 1) * TP],
                                          ident[0:QP, 0:QP])
                    mm.then_inc(c_ptr, 1)
                j = i - 6
                if live(j, NT):
                    pe.wait_ge(c_hte, j + 1)
                    if live(i - 5, NT):
                        pe.wait_ge(c_hte, i - 4)
                    elif past(j, 1):
                        pe.wait_ge(c_lg, j)
                    pe.matmul(ps[0:TP, 0, 480:480 + NE], h2s[:, (u - 6) % 4, :], gate_w[:, :], start=True, stop=True).then_inc(c_gt, 1)
                j = i - 3
                if live(j, NT):
                    w = (u - 3) % 2
                    pe.wait_ge(c_pte, j + 1)
                    pe.wait_ge(c_vp, j + 1)
                    if live(i - 4, NT):
                        pe.wait_ge(c_y, i - 3)
                    for b in range(2):
                        for s in range(2):
                            for g in range(4):
                                k = 2 * g + s
                                mm = pe.matmul(ps[32 * g:32 * g + 32, 7, b * NS:(b + 1) * NS],
                                               vpf[0:TP, (u - 3) % 4, b, g * 96 + s * 32:g * 96 + s * 32 + 32],
                                               pfT[0:TP, w, k * QP + 64 * b:k * QP + 64 * b + NS],
                                               start=(s == 0), stop=(s == 1), tile_position=(0, 32 * g))
                    mm.then_inc(c_pv, 1)

                if at(i, NT + 2):
                    pe.wait_ge(c_sub, NT)
                    pe.wait_ge(c_xh, 4)
                    pe.wait_ge(c_xl, 4)
                    hidden(0, 0, 0)
                if at(i, NT + 4):
                    pe.wait_ge(c_xh, 8)
                    pe.wait_ge(c_xl, 8)
                    hidden(0, 0, 1)
                    pe.wait_ge(c_pte, NT)
                    outputs(0, 0, 0)

            pipeline(pe, NT, 6, 8, 4, body_c)

            def spread_pe(c):
                for i in range(4):
                    mm = pe.transpose(ps[0:NE, 7 * (1 - c % 2), i * TP:(i + 1) * TP], ew[:, 4 * c + i, :], ident[0:TP, 0:TP])
                mm.then_inc(m_ewt, 1)

            def second_bias_pe(c):
                for i in range(4):
                    t = 4 * c + i
                    mm = pe.matmul(ps[0:TP, 7 * (1 - c % 2), i * D:(i + 1) * D], ewT[:, t * TP:(t + 1) * TP], b2_nat[:, :],
                                   start=True, stop=True)
                mm.then_inc(m_b2, 1)

            pe.wait_ge(c_xh, NT)
            pe.wait_ge(c_xl, NT)
            pe.wait_ge(c_lg, NT)
            pe.wait_ge(c_y, NT)
            hidden(0, 0, 2)
            outputs(0, 0, 1)
            pe.wait_ge(m_ew, 1)
            spread_pe(0)
            spread_pe(1)
            hidden(0, 0, 3)
            for c in range(2, CH):
                pe.wait_ge(m_ewe, c - 1)
                spread_pe(c)
            outputs(0, 0, 2)
            hidden(1, 1, 0)
            outputs(0, 0, 3)
            pe.wait_ge(m_ewe, CH)
            second_bias_pe(0)
            second_bias_pe(1)
            hidden(1, 1, 1)
            outputs(1, 1, 0)
            for c in range(2, CH):
                pe.wait_ge(m_acc0, c - 1)
                second_bias_pe(c)
            for c in range(2, CH):
                hidden(1, 1, c)
                outputs(1, 1, c - 1)
            with pe.Fori(1, NE // 2, 1) as r:
                for u in range(2):
                    for c in range(CH):
                        hidden(r * 2 + u, u, c)
                        if c == 0:
                            outputs(r * 2 + u - 1, 1 - u, CH - 1)
                        else:
                            outputs(r * 2 + u, u, c - 1)
            outputs(NE - 1, 1, CH - 1)


_INS = ["x", "ctx_1024"] + ["L0_attn_" + n for n in ("Wq", "Wk", "Wv", "Wo", "Ww1", "Ww2", "Wb", "Wf", "delta")] + \
    ["L0_xattn_" + n for n in ("Wq", "bq", "Wk", "bk", "Wv", "bv")] + \
    ["L0_ffn_" + n for n in ("ln1_g", "ln1_b", "w_qkv", "b_qkv", "w_o", "b_o", "ln2_g", "ln2_b", "gate_w", "gate_b",
                             "W1", "b1", "W2", "b2")]


def kernel(**inputs):
    import numpy as _np
    import concourse.bacc as _bacc
    from concourse import mybir as _mybir
    from concourse.bass_utils import run_bass_kernel_spmd as _run

    nc = _bacc.Bacc("TRN2", target_bir_lowering=False, num_devices=1)
    arrays, args = {}, {}
    for name in _INS:
        v = _np.ascontiguousarray(inputs[name])
        arrays["in_" + name] = v
        args[name] = nc.dram_tensor("in_" + name, v.shape, _mybir.dt.from_np(v.dtype), kind="ExternalInput").ap()
    o = nc.dram_tensor("out_0", (NB, NS, D), _mybir.dt.float32, kind="ExternalOutput").ap()
    build(nc, args, o)
    r = _run(nc, [arrays], core_ids=[0])
    return r.results[0]["out_0"]
```

```python
from contextlib import ExitStack

import concourse.bass as bass
from concourse import mybir

F32 = mybir.dt.float32
F32R = mybir.dt.float32r
I32 = mybir.dt.int32
ALU = mybir.AluOpType
ACT = mybir.ActivationFunctionType
AX = mybir.AxisListType

NB, NS, D, H = 32, 56, 128, 16
HD = D // H
NT = NB // 2
TP = 2 * NS
NTOK = NB * NS
CH = 4
CW = NTOK // CH
T8 = 8
NK = NS // T8
GB = NB // CH
HB = NB // 2
NCTX = 1500
NCC = 12
CR = NCTX // NCC
QP = 120
NE, FF = 8, 4 * D
FC = FF // 128
NEG = -1.0e30
EPS = 1e-05
FILL = 4
UPPER = -(1 << 12)
SCALE_HD = float(HD) ** -0.5
SCALE_D = float(D) ** -0.5


def live(j, n):
    return not isinstance(j, int) or 0 <= j < n


def past(j, r):
    return not isinstance(j, int) or j >= r


def at(i, n):
    return isinstance(i, int) and i == n


def pipeline(eng, n, skew, lo, unroll, body, first=0, following=None):
    for i in range(first, lo):
        body(i, i % unroll)
    with eng.Fori(lo // unroll, n // unroll, 1) as r:
        for u in range(unroll):
            body(r * unroll + u, u)
    for i in range(n, n + skew):
        body(i, i % unroll)
        if following and 0 <= i - n - 1 < FILL:
            following(i - n - 1)


def build(nc, a, out):
    ctx = ExitStack()
    with ctx:
        def sb(name, shape, dtype=F32):
            return ctx.enter_context(nc.sbuf_tensor(name, shape, dtype))

        def sem(name):
            return ctx.enter_context(nc.semaphore(name))

        ps = ctx.enter_context(nc.psum_tensor("ps", [128, 8, 512], F32))

        ident = sb("ident", [128, 128])
        blockones = sb("blockones", [128, 128])
        head_win = sb("head_win", [128, 15 * H])
        fc_win = sb("fc_win", [128, 15 * H])
        fc_neg = sb("fc_neg", [128, T8 * H])
        causal8 = sb("causal8", [128, T8])
        half_mask = sb("half_mask", [TP, 2 * HD])
        quad_mask = sb("quad_mask", [128, 4])
        ones_row = sb("ones_row", [1, TP])

        wq = sb("wq", [D, D]); wk = sb("wk", [D, D]); wv = sb("wv", [D, D]); wo = sb("wo", [D, D])
        ww1 = sb("ww1", [D, HD]); ww2 = sb("ww2", [HD, D])
        wbf = sb("wbf", [D, 2 * H]); wb_rep = sb("wb_rep", [D, D]); wf_rep = sb("wf_rep", [D, D])
        delta = sb("delta", [D, 1])
        eps_ww = sb("eps_ww", [128, 1]); eps_ln = sb("eps_ln", [128, 1]); minus_half = sb("minus_half", [128, 1])
        xw = sb("xw", [D, 3, D])
        xwqT = sb("xwqT", [D, D]); xwvT = sb("xwvT", [D, D])
        wqkv = sb("wqkv", [D, 3 * D]); w_o = sb("w_o", [D, D]); gate_w = sb("gate_w", [D, NE])
        cols = sb("cols", [D, 9])
        BQ, BK, G1, B1, FQ, FK, FV, G2, B2 = (cols[:, i:i + 1] for i in range(9))
        rows = sb("rows", [1, 2 * D + NE])
        rows_b = sb("rows_b", [TP, 2 * D + NE])
        BVR, BOR, GBR = rows_b[:, 0:D], rows_b[:, D:2 * D], rows_b[:, 2 * D:]
        b1_nat = sb("b1_nat", [NE * FC, 128]); b1T = sb("b1T", [128, NE * FC]); b1e = sb("b1e", [128, 2, FC])
        b2_nat = sb("b2_nat", [NE, D])
        w1r = sb("w1r", [D, 2, FF]); w2r = sb("w2r", [128, 2, FC, D])

        with nc.sbuf_tensor("early", [128, 2 * NTOK], F32) as early:
            pass
        xh = sb("xh", [D, NTOK], F32R); xl = sb("xl", [D, NTOK], F32R)
        with nc.sbuf_tensor("xT", [D, 4 * FF], F32) as xT:
            pass
        w1h = sb("w1h", [D, 2, FF], F32R); w1l = sb("w1l", [D, 2, FF], F32R)

        res = sb("res", [TP, NT, D])
        v_nat = sb("v_nat", [TP, NT, D])
        acc = v_nat
        x2n = sb("x2n", [TP, NT, D])
        small = sb("small", [128, 4, 80])
        stage = sb("stage", [128, 4, 3, D])
        lg = sb("lg", [TP, NT, NE]); ew = sb("ew", [TP, NT, NE]); gt = sb("gt", [TP, 6, NT, NE])
        gs = sb("gs", [TP, 6, NT]); iota8 = sb("iota8", [TP, NE])

        class Region:
            def __init__(self, name, size):
                self.t, self.size = sb(name, [128, size]), size
                self.at = 0

            def take(self, n):
                self.at += n
                assert self.at <= self.size, (self.at, self.size)
                return self.t[:, self.at - n:self.at]

            def restart(self, at=0):
                self.at = at

        R1 = Region("R1", 7 * NTOK + 2 * NTOK)
        R2 = Region("R2", NK * NB * NS)
        qT, kT, wT, bwT, fcT, tmpA, tmpB = (R1.take(NTOK) for _ in range(7))
        halves = R1.at
        Tw = R1.take(2 * HB * NS).rearrange("p (h n) -> p h n", h=2)
        Xw = R1.take(2 * HB * NS).rearrange("p (h n) -> p h n", h=2)
        Tq = early[:, :].rearrange("p (h r n) -> p h r n", h=2, r=2)
        E = R2.take(NK * NB * NS).rearrange("p (k n) -> p k n", k=NK)
        R1.restart(halves)
        pa = R1.take(2 * NK * TP).rearrange("p (r n) -> p r n", r=2)
        paT = R1.take(2 * NK * 128).rearrange("p (r n) -> p r n", r=2)
        vpa = early[:, 0:4 * 640].rearrange("p (r b n) -> p r b n", r=2, b=2)
        oTa = R1.take(2 * TP).rearrange("p (r n) -> p r n", r=2)
        R1.restart(); R2.restart()
        ctxr = R1.take(4 * 2 * NCC * D).rearrange("p (r b n) -> p r b n", r=4, b=2)
        ctx_end = R1.at
        cT = R2.take(2 * 2 * NCTX).rearrange("p (r n) -> p r n", r=2)
        px = R2.take(2 * NCTX).rearrange("p (r n) -> p r n", r=2)
        pxT = R2.take(2 * NCC * QP).rearrange("p (r n) -> p r n", r=2)
        qx = sb("qx", [D, NTOK]); onx = sb("onx", [QP, 2, D])
        ewT = qx[0:NE, :]
        qxs = sb("qxs", [D, 2, TP]); qts = sb("qts", [D, 2, TP]); oxT = sb("oxT", [D, 2, TP])
        R1.restart()
        hs = R1.take(4 * 2 * TP).rearrange("p (r b n) -> p r b n", r=4, b=2)
        qs = R1.take(2 * TP).rearrange("p (r n) -> p r n", r=2)
        km = R1.take(2 * 4 * TP).rearrange("p (r f n) -> p r f n", r=2, f=4)
        pf = R1.take(2 * H * NS).rearrange("p (r n) -> p r n", r=2)
        pfT = R1.take(2 * 8 * QP).rearrange("p (r n) -> p r n", r=2)
        vpf = R1.take(4 * 2 * 384).rearrange("p (r b n) -> p r b n", r=4, b=2)
        ofT = R1.take(2 * TP).rearrange("p (r n) -> p r n", r=2)
        h2s = R1.take(4 * TP).rearrange("p (r n) -> p r n", r=4)
        xm = R1.take(2 * TP).rearrange("p (r n) -> p r n", r=2)
        w1m = R1.take(2 * FF).rearrange("p (r n) -> p r n", r=2)
        R2.restart()
        hid = R2.take(2 * FC * CW).rearrange("p (r f n) -> p r f n", r=2, f=FC)

        fct8 = sb("fct8", [128, NB, NK])
        rowmax = sb("rowmax", [128, NB]); rowsum = sb("rowsum", [128, NK, NB]); rinv = sb("rinv", [128, NK, NB])

        s_const = sem("s_const"); s_link = sem("s_link")
        s_x = sem("s_x"); s_w1 = sem("s_w1")
        s_rep = sem("s_rep")
        s_pe0 = sem("s_pe0"); s_ev0 = sem("s_ev0"); s_wk = sem("s_wk"); s_sq = sem("s_sq"); s_act0 = sem("s_act0"); s_dve0 = sem("s_dve0")
        s_T = sem("s_T"); s_U = sem("s_U"); s_X = sem("s_X"); s_K = sem("s_K"); s_Tq = sem("s_Tq"); s_S = sem("s_S")
        s_shift = sem("s_shift"); s_max = sem("s_max"); s_sub = sem("s_sub"); s_exp = sem("s_exp")
        s_sum = sem("s_sum"); s_rinv = sem("s_rinv"); s_fct = sem("s_fct"); s_fct8 = sem("s_fct8")
        s_first = sem("s_first"); s_v = sem("s_v"); s_vev = sem("s_vev")
        s_out = sem("s_out"); s_w2 = sem("s_w2"); s_prep = sem("s_prep"); s_prep_ev = sem("s_prep_ev")
        a_zero = sem("a_zero"); a_ps = sem("a_ps"); a_tr = sem("a_tr"); a_pt = sem("a_pt"); a_vp = sem("a_vp")
        a_pv = sem("a_pv"); a_o = sem("a_o"); a_wo = sem("a_wo"); a_y = sem("a_y"); a_st = sem("a_st"); a_mv = sem("a_mv")
        a_ln = sem("a_ln"); a_rs = sem("a_rs"); a_x1 = sem("a_x1"); a_xt = sem("a_xt"); a_xe = sem("a_xe"); a_rb = sem("a_rb")
        b_ctx = [sem(f"b_ctx{u}") for u in range(4)]
        b_qx = sem("b_qx"); b_qxe = sem("b_qxe"); b_qxs = sem("b_qxs"); b_qt = sem("b_qt"); b_qte = sem("b_qte"); b_qb = sem("b_qb")
        b_ct = sem("b_ct"); b_cta = sem("b_cta"); b_ctd = sem("b_ctd"); b_sc = sem("b_sc"); b_mx = sem("b_mx"); b_m2 = sem("b_m2")
        b_nb = sem("b_nb"); b_exp = sem("b_exp"); b_ptr = sem("b_ptr"); b_pta = sem("b_pta"); b_ptd = sem("b_ptd"); b_pv = sem("b_pv")
        b_rd = sem("b_rd"); b_on = sem("b_on"); b_ont = sem("b_ont"); b_one = sem("b_one"); b_wv = sem("b_wv"); b_y = sem("b_y")
        b_st = sem("b_st"); b_mv = sem("b_mv"); b_ln = sem("b_ln"); b_rs = sem("b_rs"); b_x2 = sem("b_x2"); b_st2 = sem("b_st2")
        b_mv2 = sem("b_mv2"); b_ln2 = sem("b_ln2"); b_rs2 = sem("b_rs2"); b_h = sem("b_h"); b_ht = sem("b_ht"); b_hte = sem("b_hte")
        b_rb = sem("b_rb")
        c_zero = sem("c_zero"); c_hs = sem("c_hs"); c_qkv = sem("c_qkv"); c_q = sem("c_q"); c_km = sem("c_km"); c_vp = sem("c_vp")
        c_sc = sem("c_sc"); c_mx = sem("c_mx"); c_sub = sem("c_sub"); c_exp = sem("c_exp"); c_sum = sem("c_sum"); c_ri = sem("c_ri")
        c_nrm = sem("c_nrm"); c_ptr = sem("c_ptr"); c_pte = sem("c_pte"); c_pv = sem("c_pv"); c_o = sem("c_o"); c_wo = sem("c_wo")
        c_y = sem("c_y"); c_st = sem("c_st"); c_mv = sem("c_mv"); c_ln = sem("c_ln"); c_rs = sem("c_rs"); c_h = sem("c_h")
        c_ht = sem("c_ht"); c_hte = sem("c_hte"); c_xm = sem("c_xm"); c_xh = sem("c_xh"); c_xl = sem("c_xl"); c_gt = sem("c_gt"); c_lg = sem("c_lg"); c_acc = sem("c_acc")
        m_link = sem("m_link"); m_e = sem("m_e"); m_ew = sem("m_ew"); m_ewt = sem("m_ewt"); m_ewe = sem("m_ewe"); m_b2 = sem("m_b2")
        m_b1 = sem("m_b1"); m_acc0 = sem("m_acc0"); m_w = [sem(f"m_w{u}") for u in range(2)]; m_hid = sem("m_hid"); m_relu = sem("m_relu")
        m_out = sem("m_out"); m_acc = sem("m_acc"); m_wm = sem("m_wm"); m_wh = sem("m_wh"); m_wl = sem("m_wl"); f_st = sem("f_st"); f_mv = sem("f_mv"); f_ln = sem("f_ln"); f_rs = sem("f_rs")
        f_y = sem("f_y")

        xflat = a["x"].rearrange("b n d -> (b n) d").rearrange("(i p) d -> p i d", p=TP)

        def tok(t):
            return t[:, 0:NTOK].rearrange("p (b n) -> p b n", n=NS)

        GATES_T, FCT_T = 3, 6
        FCT0 = 512 - NB * NK
        ROW0 = 512 - (2 * D + NE)
        PREP_T = 20
        assert GB * FCT_T <= FCT0 and GB * PREP_T <= min(ROW0, 2 * D)

        block = ctx.enter_context(nc.Block())

        @block.sync
        def _(sp):
            sp.dma_start(res[:, :, :], xflat).then_inc(s_x, 16)
            for t, n in ((wq, "Wq"), (wk, "Wk"), (ww1, "Ww1"), (ww2, "Ww2"), (wv, "Wv"), (wo, "Wo")):
                sp.dma_start(t[:, :], a["L0_attn_" + n]).then_inc(s_w1, 16)
            sp.dma_start(wbf[:, 0:H], a["L0_attn_Wb"]).then_inc(s_w1, 16)
            sp.dma_start(wbf[:, H:2 * H], a["L0_attn_Wf"]).then_inc(s_w1, 16)
            sp.dma_start(delta[:, :], a["L0_attn_delta"].rearrange("(h o) -> h o", o=1).broadcast_to([H, HD]).rearrange("h (d o) -> h d o", o=1)).then_inc(s_w1, 16)
            X, F = "L0_xattn_", "L0_ffn_"
            for t, n in ((xw[:, 0, :], X + "Wq"), (xw[:, 1, :], X + "Wv"), (xw[:, 2, :], X + "Wk"), (wqkv[:, :], F + "w_qkv"),
                         (w_o[:, :], F + "w_o"), (gate_w[:, :], F + "gate_w"), (b2_nat[:, :], F + "b2")):
                sp.dma_start(t, a[n]).then_inc(s_w2, 16)
            sp.dma_start(b1_nat[:, :], a[F + "b1"].rearrange("e (c f) -> (e c) f", f=128)).then_inc(s_w2, 16)
            bqkv = a[F + "b_qkv"].rearrange("(s d o) -> s d o", s=3, o=1)
            for t, v in ((BQ, a[X + "bq"]), (BK, a[X + "bk"]), (G1, a[F + "ln1_g"]), (B1, a[F + "ln1_b"]), (FQ, bqkv[0]),
                         (FK, bqkv[1]), (FV, bqkv[2]), (G2, a[F + "ln2_g"]), (B2, a[F + "ln2_b"])):
                sp.dma_start(t, v if len(v.shape) == 2 else v.rearrange("(d o) -> d o", o=1)).then_inc(s_w2, 16)
            for lo, v in ((0, a[X + "bv"]), (D, a[F + "b_o"]), (2 * D, a[F + "gate_b"])):
                sp.dma_start(rows[:, lo:lo + v.shape[0]], v.rearrange("(o d) -> o d", o=1)).then_inc(s_w2, 16)
            ctx_v = a["ctx_1024"].rearrange("(i two) (p c) d -> i p two (c d)", two=2, c=NCC)
            sp.wait_ge(s_S, 2 * NS)
            sp.wait_ge(s_K, 2 * (NS - 1))
            for i in range(4):
                sp.dma_start(ctxr[0:CR, i], ctx_v[i]).then_inc(b_ctx[i], 16)
            with sp.Fori(1, NT // 4, 1) as r:
                for u in range(4):
                    sp.wait_ge(b_pv, r * 4 + u - 3)
                    sp.wait_ge(s_S, 2 * NS)
                    sp.dma_start(ctxr[0:CR, u], ctx_v[r * 4 + u]).then_inc(b_ctx[u], 16)

            w1_v = a[F + "W1"]
            w2_v = a[F + "W2"].rearrange("e (c f) d -> e f c d", f=128)

            def expert(e, u):
                sp.dma_start(w1r[:, u, :], w1_v[e]).then_inc(m_w[u], 16)
                sp.dma_start(w2r[:, u], w2_v[e]).then_inc(m_w[u], 16)

            expert(0, 0)
            expert(1, 1)
            with sp.Fori(1, NE // 2, 1) as r:
                for u in range(2):
                    e = r * 2 + u
                    sp.wait_ge(m_w[u], 32)
                    sp.wait_ge(m_out, (e - 1) * CH)
                    expert(e, u)
            oflat = out.rearrange("b n d -> (b n) d").rearrange("(i p) d -> p i d", p=TP)
            for c in range(CH):
                sp.wait_ge(f_y, 4 * (c + 1))
                sp.dma_start(oflat[:, 4 * c:4 * c + 4, :], acc[:, 4 * c:4 * c + 4, :]).then_inc(s_out, 16)
            sp.wait_ge(s_out, 16 * CH)

        NW1 = 9 * 16
        NW2 = 20 * 16

        def stat(u, lo, n=1, rows=TP):
            return small[0:rows, u % 4, lo:lo + n]

        ST1, MV1, LN1, RS1, ST2, MV2, LN2, RS2 = 0, 6, 8, 9, 10, 16, 18, 19
        MX, QB, M2, NBI, DEN, RDN, HMX, HSM, HRI = 20, 21, 22, 23, 24, 25, 26, 42, 58

        @block.gpsimd
        def _(pool):
            links = [0]

            def link(ins):
                links[0] += 1
                ins.then_inc(s_link, 1)
                pool.wait_ge(s_link, links[0])

            pool.memset(eps_ww[:, :], 1e-6)
            pool.memset(eps_ln[:, :], EPS)
            pool.memset(minus_half[:, :], -0.5)
            link(pool.memset(ident[:, :], 0.0))
            pool.affine_select(out=ident[:, :], in_=ident[:, :], compare_op=ALU.not_equal, fill=1.0,
                               base=0, pattern=[[-1, 128]], channel_multiplier=1).then_inc(s_const, 1)
            bo = blockones[:, :].rearrange("p (g d) -> p g d", d=HD)
            link(pool.memset(blockones[:, :], 1.0))
            link(pool.affine_select(out=bo, in_=bo, compare_op=ALU.is_ge, fill=0.0,
                                    base=0, pattern=[[-HD, H], [0, HD]], channel_multiplier=1))
            link(pool.affine_select(out=bo, in_=bo, compare_op=ALU.is_ge, fill=0.0,
                                    base=HD - 1, pattern=[[HD, H], [0, HD]], channel_multiplier=-1))
            link(pool.memset(head_win[:, :], 0.0))
            mid = slice(7 * H, 8 * H)
            link(pool.tensor_copy(head_win[:, mid], blockones[:, 0:D:HD]))
            link(pool.memset(fc_win[:, :], 0.0))
            link(pool.affine_select(out=fc_win[:, mid], in_=fc_win[:, mid], compare_op=ALU.not_equal, fill=1.0,
                                    base=0, pattern=[[-HD, H]], channel_multiplier=1))
            fn = fc_neg[:, :].rearrange("p (t h) -> p t h", t=T8)
            link(pool.memset(fc_neg[:, :], 0.0))
            link(pool.affine_select(out=fn, in_=fn, compare_op=ALU.not_equal, fill=-1.0,
                                    base=0, pattern=[[0, T8], [-HD, H]], channel_multiplier=1))
            link(pool.memset(causal8[:, :], 0.0))
            link(pool.affine_select(out=causal8[:, :], in_=causal8[:, :], compare_op=ALU.is_ge, fill=NEG,
                                    base=0, pattern=[[-H, T8]], channel_multiplier=1))
            link(pool.memset(half_mask[:, :], 1.0))
            link(pool.affine_select(out=half_mask[:, 0:HD], in_=half_mask[:, 0:HD], compare_op=ALU.is_ge, fill=0.0,
                                    base=NS - 1, pattern=[[0, HD]], channel_multiplier=-1))
            link(pool.affine_select(out=half_mask[:, HD:], in_=half_mask[:, HD:], compare_op=ALU.is_ge, fill=0.0,
                                    base=-NS, pattern=[[0, HD]], channel_multiplier=1))
            link(pool.tensor_copy(quad_mask[:, :], blockones[:, 0:4 * HD:HD]))
            for g in range(1, 4):
                link(pool.tensor_tensor(quad_mask[:, :], quad_mask[:, :], blockones[:, 4 * HD * g:4 * HD * (g + 1):HD], ALU.add))
            link(pool.iota(iota8[:, :], pattern=[[1, NE]], base=0, channel_multiplier=0, allow_small_or_imprecise_dtypes=True))
            pool.memset(ones_row[:, :], 1.0).then_inc(s_const, 1)
            pool.memset(E[:, :, :], 0.0).then_inc(s_const, 1)
            pool.wait_ge(s_dve0, 1)
            link(pool.memset(tmpB[:, :], 1.0))
            pool.memset(tmpB[:, 0:NTOK:NS], 0.0).then_inc(s_first, 1)
            K, Q = tok(kT), tok(qT)
            pool.wait_ge(s_wk, 8)
            pool.wait_ge(s_ev0, 20)
            for t in range(NS):
                W = T8 * (t // T8 + 1)
                for half in range(2):
                    bs = slice(half * HB, (half + 1) * HB)
                    if t > 0:
                        pool.wait_ge(s_K, 2 * (t - 1) + half + 1)
                    if t >= 2:
                        pool.wait_ge(s_S, 2 * (t - 2) + half + 1)
                    o = Tq[:, half, t % 2, 0:HB * W].rearrange("p (b j) -> p b j", j=W)
                    nc.gpsimd.tensor_tensor(o, K[:, bs, 0:W], Q[:, bs, t:t + 1].broadcast_to([128, HB, W]),
                                            ALU.mult).then_inc(s_Tq, 1)

            def rstd(var, eps_sum, out, mv, ln, rs, j):
                pool.wait_ge(mv, j + 1)
                nc.gpsimd.tensor_tensor(eps_sum, var, eps_ln[0:TP, :], ALU.add).then_inc(ln, 1)
                pool.wait_ge(ln, j + 1)
                nc.gpsimd.tensor_tensor(out, eps_sum, minus_half[0:TP, :], ALU.pow).then_inc(rs, 1)

            pool.wait_ge(s_S, 2 * NS)
            pool.wait_ge(s_K, 2 * (NS - 1))
            pool.memset(vpa, 0.0).then_inc(a_zero, 1)
            pool.wait_ge(a_zero, 1)
            pool.wait_ge(s_vev, 2)
            pool.wait_ge(s_prep_ev, 4)

            def body_a(i, u):
                if live(i, NT):
                    if past(i, 2):
                        pool.wait_ge(a_pv, i - 1)
                    for b in range(2):
                        nc.gpsimd.tensor_tensor(
                            vpa[0:TP, u % 2, b, :].rearrange("p (h c) -> p h c", c=5 * HD)[:, :, 0:HD],
                            v_nat[:, bass.ds(i, 1), :].rearrange("p i (h d) -> p (i h) d", d=HD),
                            half_mask[:, b * HD:(b + 1) * HD].unsqueeze(1).broadcast_to([TP, H, HD]),
                            ALU.mult).then_inc(a_vp, 1)
                j = i - 3
                if live(j, NT):
                    rstd(stat(u - 3, MV1 + 1), stat(u - 3, LN1), stat(u - 3, RS1), a_mv, a_ln, a_rs, j)
                j = i - 4
                if live(j, NT):
                    pool.wait_ge(a_x1, j + 1)
                    nc.gpsimd.tensor_tensor(res[:, bass.ds(j, 1), :].rearrange("p i d -> p (i d)"), stage[0:TP, (u - 4) % 4, 1, :], BVR,
                                            ALU.add).then_inc(a_rb, 1)

            pipeline(pool, NT, 4, 8, 4, body_a)

            def body_b(i, u):
                if live(i, NT):
                    pool.wait_ge(b_qxe, NT)
                    if past(i, 2):
                        pool.wait_ge(b_qt, i - 1)
                    nc.gpsimd.tensor_copy(qxs[:, u % 2, :], qx[:, bass.ts(i, TP)]).then_inc(b_qxs, 1)
                j, v = i - 5, u - 5
                if live(j, NT):
                    x2 = stage[0:TP, v % 4, 1, :]
                    rstd(stat(v, MV1 + 1), stat(v, LN1), stat(v, RS1), b_mv, b_ln, b_rs, j)
                    rstd(stat(v, MV2 + 1), stat(v, LN2), stat(v, RS2), b_mv2, b_ln2, b_rs2, j)
                    pool.wait_ge(b_x2, j + 1)
                    nc.gpsimd.tensor_tensor(res[:, bass.ds(j, 1), :].rearrange("p i d -> p (i d)"), x2, BOR, ALU.add).then_inc(b_rb, 1)
                    nc.gpsimd.tensor_copy(x2n[:, bass.ds(j, 1), :].rearrange("p i d -> p (i d)"), x2).then_inc(b_rb, 1)


            def lower(e, u):
                pool.wait_ge(m_wm, e + 1)
                if past(e, 2):
                    pool.wait_ge(m_hid, CH * FC * (e - 1))
                else:
                    pool.wait_ge(c_hs, NT)
                nc.gpsimd.tensor_tensor(w1l[:, u, :], w1r[:, u, :], w1m[:, u, :], ALU.subtract).then_inc(m_wl, 1)

            def body_c(i, u):
                if at(i, 0):
                    pool.wait_ge(b_pv, NT - 1)
                    pool.memset(vpf, 0.0).then_inc(c_zero, 1)
                if live(i, NT):
                    pool.wait_ge(b_hte, i + 1)
                    if past(i, 4):
                        pool.wait_ge(c_qkv, i - 3)
                    nc.gpsimd.tensor_copy(hs[:, u % 4, :, :].rearrange("p b (r n) -> p b r n", r=2),
                                          xT[:, bass.ts(i, TP)].rearrange("p (b n) -> p b n", b=2).unsqueeze(2)
                                          .broadcast_to([128, 2, 2, NS])).then_inc(c_hs, 1)
                j = i - 5
                if live(j, NT):
                    rstd(stat(u - 5, MV1 + 1), stat(u - 5, LN1), stat(u - 5, RS1), c_mv, c_ln, c_rs, j)
                    pool.wait_ge(c_y, j + 1)
                    pool.wait_ge(b_rb, 2 * NT)
                    nc.gpsimd.tensor_tensor(acc[:, bass.ds(j, 1), :].rearrange("p i d -> p (i d)"), stage[0:TP, (u - 5) % 4, 0, :],
                                            x2n[:, bass.ds(j, 1), :].rearrange("p i d -> p (i d)"), ALU.add).then_inc(c_acc, 1)
                j = i - 2
                if live(j, NT):
                    pool.wait_ge(c_ri, j + 1)
                    p = pf[0:QP, u % 2, :].rearrange("p (h j) -> p h j", h=H)
                    nc.gpsimd.tensor_tensor(p, p, stat(u - 2, HRI, H, QP).unsqueeze(2).broadcast_to([QP, H, NS]),
                                            ALU.mult).then_inc(c_nrm, 1)
                j = i - 6
                if live(j, NT):
                    pool.wait_ge(c_xm, j + 1)
                    nc.gpsimd.tensor_tensor(xl[:, bass.ts(j, TP)], h2s[:, (u - 6) % 4, :], xm[:, u % 2, :],
                                            ALU.subtract).then_inc(c_xl, 1)
                if at(i, NT):
                    lower(0, 0)
                if at(i, NT + 2):
                    lower(1, 1)

            pipeline(pool, NT, 6, 8, 4, body_b, following=lambda k: body_c(k, k))
            pipeline(pool, NT, 7, 8, 4, body_c, first=FILL)

            with pool.Fori(1, NE // 2, 1) as r:
                for u in range(2):
                    lower(r * 2 + u, u)

            for c in range(CH):
                four = slice(4 * c, 4 * c + 4)
                pool.wait_ge(f_mv, 4 * (c + 1))
                nc.gpsimd.tensor_tensor(gs[:, 1, four], gt[:, 1, four, 1], eps_ln[0:TP, :].broadcast_to([TP, 4]), ALU.add).then_inc(f_ln, 1)
                pool.wait_ge(f_ln, c + 1)
                nc.gpsimd.tensor_tensor(gs[:, 2, four], gs[:, 1, four], minus_half[0:TP, :].broadcast_to([TP, 4]), ALU.pow).then_inc(f_rs, 1)

        @block.scalar
        def _(act):
            def chunk(t, c):
                return t[:, c * CW:(c + 1) * CW]

            for c in range(CH):
                act.wait_ge(s_pe0, 1 + c)
                nc.scalar.copy(chunk(xT, c), ps[:, c, 0:CW]).then_inc(s_ev0, 1)
            for c in range(CH):
                act.wait_ge(s_pe0, 5 + c)
                nc.scalar.copy(tmpA[0:HD, c * CW:(c + 1) * CW], ps[0:HD, 4 + c, 0:CW]).then_inc(s_ev0, 1)
            for c in range(CH):
                act.wait_ge(s_pe0, 13 + c)
                nc.scalar.activation(chunk(bwT, c), ps[:, 4 + c, 0:CW], ACT.Exp, scale=-1.0).then_inc(s_ev0, 1)
            act.wait_ge(s_ev0, 12)
            nc.scalar.activation(bwT[:, :], bwT[:, :], ACT.Ln, bias=1.0).then_inc(s_act0, 1)
            act.wait_ge(s_const, 1)
            for c in range(CH):
                act.wait_ge(s_pe0, 17 + c)
                nc.scalar.activation(chunk(tmpB, c), ps[:, c, 0:CW], ACT.Ln, bias=eps_ww[:, :]).then_inc(s_ev0, 1)
            act.wait_ge(s_ev0, 16)
            nc.scalar.activation(tmpB[:, :], tmpB[:, :], ACT.Exp, scale=-0.5).then_inc(s_act0, 1)
            act.wait_ge(s_act0, 1)
            nc.scalar.activation(bwT[:, :], bwT[:, :], ACT.Exp, scale=-1.0).then_inc(s_act0, 1)
            for c in range(CH):
                act.wait_ge(s_pe0, 25 + c)
                nc.scalar.mul(chunk(qT, c), ps[:, c, 0:CW], SCALE_HD).then_inc(s_ev0, 1)
            act.wait_ge(s_w1, NW1)
            for c in range(CH):
                act.wait_ge(s_pe0, 29 + c)
                nc.scalar.activation(chunk(fcT, c), ps[:, 4 + c, 0:CW], ACT.Identity, bias=delta[:, :]).then_inc(s_ev0, 1)
            act.wait_ge(s_ev0, 24)
            nc.scalar.activation(tmpA[:, :], fcT[:, :], ACT.Abs).then_inc(s_act0, 1)
            act.wait_ge(s_act0, 4)
            nc.scalar.activation(tmpA[:, :], tmpA[:, :], ACT.Exp, scale=-1.0).then_inc(s_act0, 1)
            act.wait_ge(s_act0, 5)
            nc.scalar.activation(tmpA[:, :], tmpA[:, :], ACT.Ln, bias=1.0).then_inc(s_act0, 1)

            for k in range(NK - 1):
                if k == (PREP_T - 1) // T8:
                    act.wait_ge(s_prep, 1)
                    nc.scalar.copy(xwqT[:, :], ps[:, 1, 2 * D:3 * D]).then_inc(s_prep_ev, 1)
                    nc.scalar.copy(xwvT[:, :], ps[:, 1, 3 * D:4 * D]).then_inc(s_prep_ev, 1)
                    act.wait_ge(s_prep, 2)
                    nc.scalar.copy(b1T[:, :], ps[:, 2, 2 * D:2 * D + NE * FC]).then_inc(s_prep_ev, 1)
                    nc.scalar.copy(rows_b[:, :], ps[0:TP, 3, ROW0:]).then_inc(s_prep_ev, 1)
                W = T8 * (k + 1)
                act.wait_ge(s_sub, k + 1)
                e = E[:, k, :].rearrange("p (b j) -> p b j", j=NS)[:, :, 0:W]
                nc.scalar.activation(e, e, ACT.Exp).then_inc(s_exp, 1)

            def last_exponentials(c):
                act.wait_ge(s_sub, NK + c)
                e = E[:, NK - 1, c * CW:(c + 1) * CW]
                nc.scalar.activation(e, e, ACT.Exp).then_inc(s_exp, 1)

            for j in range(2):
                act.wait_ge(s_v, j + 1)
                nc.scalar.copy(v_nat[:, 8 * j:8 * j + 8, :].rearrange("p (c i) d -> p c (i d)", c=2),
                               ps[0:TP, 2 * j:2 * j + 2, :]).then_inc(s_vev, 1)
            last_exponentials(0)

            def body_a(i, u):
                for c in range(1, CH):
                    if at(i, 3 * (c - 1)):
                        last_exponentials(c)
                if live(i, NT):
                    act.wait_ge(a_tr, i + 1)
                    if past(i, 2):
                        act.wait_ge(a_pv, i - 1)
                    nc.scalar.copy(paT[0:TP, u % 2, :],
                                   ps[0:TP, 2 * (u % 2):2 * (u % 2) + 2, :].rearrange("p b n -> p (b n)")[:, 0:NK * 128])\
                        .then_inc(a_pt, 1)
                j = i - 5
                if live(j, NT):
                    act.wait_ge(s_w2, NW2)
                    act.wait_ge(b_qx, j + 1)
                    nc.scalar.activation(qx[:, bass.ts(j, TP)], ps[:, 7, 128:128 + TP], ACT.Identity, bias=BQ).then_inc(b_qxe, 1)
                j = i - 1
                if live(j, NT):
                    act.wait_ge(a_pv, j + 1)
                    if past(j, 2):
                        act.wait_ge(a_wo, j - 1)
                    nc.scalar.copy(oTa[:, (u - 1) % 2, :], ps[:, 4 + (u - 1) % 2, 0:TP]).then_inc(a_o, 1)
                j = i - 4
                if live(j, NT):
                    act.wait_ge(a_xt, j + 1)
                    nc.scalar.copy(xT[:, bass.ts(j, TP)], ps[:, 7, 0:TP]).then_inc(a_xe, 1)

            pipeline(act, NT, 5, 8, 4, body_a)

            def body_b(i, u):
                if live(i, NT):
                    act.wait_ge(b_qt, i + 1)
                    if past(i, 2):
                        act.wait_ge(b_sc, i - 1)
                    nc.scalar.copy(qts[:, u % 2, :], ps[:, 7, 0:TP]).then_inc(b_qte, 1)
                for q in (0, 2, 4):
                    if live(i, NT):
                        act.wait_ge(b_ct, 6 * i + q + 1)
                        b, t = q // 3, q % 3
                        nc.scalar.copy(cT[:, u % 2, b * NCTX + t * 4 * CR:b * NCTX + (t + 1) * 4 * CR],
                                       ps[:, 3, 0:4 * CR]).then_inc(b_cta, 1)
                    j = i - 4
                    if q == 2 and live(j, NT):
                        act.wait_ge(b_ont, j + 1)
                        if past(j, 2):
                            act.wait_ge(b_wv, j - 1)
                        nc.scalar.copy(oxT[:, u % 2, :].rearrange("p (b n) -> p b n", b=2),
                                       ps[:, 7, 128:256].rearrange("p (b n) -> p b n", b=2)[:, :, 0:NS]).then_inc(b_one, 1)
                j = i - 2
                if live(j, NT):
                    for r in range(2):
                        act.wait_ge(b_ptr, 3 * j + r + 1)
                        if r == 0 and past(j, 2):
                            act.wait_ge(b_pv, j - 1)
                        nc.scalar.copy(pxT[0:CR, u % 2, r * 4 * QP:(r + 1) * 4 * QP], ps[0:CR, 5, 0:4 * QP]).then_inc(b_pta, 1)
                j = i - 5
                if live(j, NT):
                    act.wait_ge(s_w2, NW2)
                    act.wait_ge(b_ht, j + 1)
                    nc.scalar.activation(xT[:, bass.ts(j, TP)], ps[:, 7, 384:384 + TP], ACT.Identity, bias=B1,
                                         scale=G1).then_inc(b_hte, 1)
                j = i - 1
                if live(j, NT):
                    act.wait_ge(b_nb, j + 1)
                    if past(j, 2):
                        act.wait_ge(b_ptr, 3 * (j - 1))
                    nc.scalar.activation(px[0:QP, (u - 1) % 2, :].rearrange("p (t n) -> p t n", t=3), ps[0:QP, 0:3, 0:4 * CR],
                                         ACT.Exp, bias=stat(u - 1, NBI, 1, QP), scale=SCALE_D,
                                         accum_out=stat(u - 1, DEN, 1, QP)).then_inc(b_exp, 1)

            def upper_act(e, u):
                act.wait_ge(s_prep_ev, 4)
                if past(e, 2):
                    act.wait_ge(m_relu, CH * FC * (e - 1))
                nc.scalar.copy(b1e[:, u, :], b1T[:, bass.ds(e * FC, FC)]).then_inc(m_b1, 1)
                act.wait_ge(m_wm, e + 1)
                if past(e, 2):
                    act.wait_ge(m_hid, CH * FC * (e - 1))
                else:
                    act.wait_ge(c_hs, NT)
                nc.scalar.copy(w1h[:, u, :], w1m[:, u, :]).then_inc(m_wh, 1)

            def hidden_act(e, u, c):
                n = e * CH + c
                for f in range(FC):
                    if f == 0:
                        act.wait_ge(m_b1, e + 1)
                        if past(n, 2):
                            act.wait_ge(m_out, n - 1)
                    act.wait_ge(m_hid, n * FC + f + 1)
                    nc.scalar.activation(hid[:, c % 2, f, :], ps[:, 1 + f, 0:CW], ACT.Relu,
                                         bias=b1e[:, u, f:f + 1]).then_inc(m_relu, 1)

            def body_c(i, u):
                if live(i, NT):
                    act.wait_ge(c_qkv, i + 1)
                    if past(i, 2):
                        act.wait_ge(c_sc, i - 1)
                    nc.scalar.activation(qs[:, u % 2, :], ps[:, 0, 0:TP], ACT.Identity, bias=FQ).then_inc(c_q, 1)
                j = i - 5
                if live(j, NT):
                    act.wait_ge(c_ht, j + 1)
                    if past(j, 4):
                        act.wait_ge(c_gt, j - 3)
                        act.wait_ge(c_xl, j - 3)
                    nc.scalar.activation(h2s[:, (u - 5) % 4, :], ps[:, 0, 0:TP], ACT.Identity, bias=B2,
                                         scale=G2).then_inc(c_hte, 1)
                j = i - 2
                if live(j, NT):
                    act.wait_ge(c_ptr, j + 1)
                    if past(j, 2):
                        act.wait_ge(c_pv, j - 1)
                    nc.scalar.copy(pfT[0:TP, u % 2, :].rearrange("p (k n) -> p k n", k=2), ps[0:TP, 5:7, 0:4 * QP]).then_inc(c_pte, 1)
                j = i - 1
                if live(j, NT):
                    act.wait_ge(c_sub, j + 1)
                    p = pf[0:QP, (u - 1) % 2, :]
                    nc.scalar.activation(p, p, ACT.Exp, scale=SCALE_HD).then_inc(c_exp, 1)
                j = i - 3
                if live(j, NT):
                    act.wait_ge(c_pv, j + 1)
                    if past(j, 2):
                        act.wait_ge(c_wo, j - 1)
                    nc.scalar.activation(ofT[:, (u - 3) % 2, :], ps[:, 7, 0:TP], ACT.Identity, bias=FV).then_inc(c_o, 1)
                j = i - 6
                if live(j, NT):
                    act.wait_ge(c_xm, j + 1)
                    nc.scalar.copy(xh[:, bass.ts(j, TP)], xm[:, u % 2, :]).then_inc(c_xh, 1)
                if at(i, NT):
                    upper_act(0, 0)
                if at(i, NT + 2):
                    hidden_act(0, 0, 0)
                if at(i, NT + 4):
                    hidden_act(0, 0, 1)

            pipeline(act, NT, 5, 8, 4, body_b, following=lambda k: body_c(k, k))
            pipeline(act, NT, 6, 8, 4, body_c, first=FILL)

            hidden_act(0, 0, 2)
            act.wait_ge(m_link, 12)
            nc.scalar.activation(gs[:, 4, :], gs[:, 4, :], ACT.Exp).then_inc(m_e, 1)
            hidden_act(0, 0, 3)
            upper_act(1, 1)
            for c in range(CH):
                hidden_act(1, 1, c)
            with act.Fori(1, NE // 2, 1) as r:
                for u in range(2):
                    upper_act(r * 2 + u, u)
                    for c in range(CH):
                        hidden_act(r * 2 + u, u, c)

        @block.vector
        def _(dve):
            K, Wv, BW = tok(kT), tok(wT), tok(bwT)
            dve.wait_ge(s_w1, NW1)
            dve.tensor_copy(wb_rep[:, :].rearrange("p (h d) -> p h d", d=HD),
                            wbf[:, 0:H].unsqueeze(2).broadcast_to([D, H, HD])).then_inc(s_rep, 1)
            dve.tensor_copy(wf_rep[:, :].rearrange("p (h d) -> p h d", d=HD),
                            wbf[:, H:].unsqueeze(2).broadcast_to([D, H, HD])).then_inc(s_rep, 1)
            def cols_of(t, c):
                return t[:, c * CW:(c + 1) * CW]

            for c in range(CH):
                dve.wait_ge(s_pe0, 9 + c)
                dve.tensor_copy(cols_of(wT, c), ps[:, c, 0:CW]).then_inc(s_wk, 1)
                dve.wait_ge(s_wk, c + 1)
                dve.tensor_tensor(cols_of(tmpB, c), cols_of(wT, c), cols_of(wT, c), ALU.mult).then_inc(s_sq, 1)
            for c in range(CH):
                dve.wait_ge(s_pe0, 21 + c)
                dve.tensor_copy(cols_of(kT, c), ps[:, 4 + c, 0:CW]).then_inc(s_wk, 1)
            dve.wait_ge(s_wk, 8)
            dve.wait_ge(s_act0, 2)
            dve.tensor_tensor(wT[:, :], wT[:, :], tmpB[:, :], ALU.mult).then_inc(s_dve0, 1)
            dve.wait_ge(s_dve0, 1)

            def beta_w():
                dve.wait_ge(s_act0, 3)
                dve.scalar_tensor_tensor(bwT[:, :], bwT[:, :], 2.0, wT[:, :], ALU.mult, ALU.mult).then_inc(s_dve0, 1)
                dve.wait_ge(s_dve0, 2)

            def gates():
                dve.wait_ge(s_act0, 6)
                dve.scalar_tensor_tensor(tmpA[:, :], fcT[:, :], 0.0, tmpA[:, :], ALU.min, ALU.subtract).then_inc(s_dve0, 1)
                dve.wait_ge(s_dve0, 3)
                dve.wait_ge(s_first, 1)
                dve.tensor_tensor_scan(fcT[:, :], tmpB[:, :], tmpA[:, :], 0.0, ALU.mult, ALU.add).then_inc(s_dve0, 1)

            def gates_by_query():
                dve.wait_ge(s_fct, 1)
                dve.tensor_copy(fct8[:, :, :], ps[:, 0, FCT0:].rearrange("p (b k) -> p b k", k=NK)).then_inc(s_fct8, 1)

            def step_T(t, half):
                bs = slice(half * HB, (half + 1) * HB)
                if t >= 2:
                    dve.wait_ge(s_K, 2 * (t - 2) + half + 1)
                dve.tensor_tensor(Tw[:, half, 0:HB * t].rearrange("p (b j) -> p b j", j=t), K[:, bs, 0:t],
                                  Wv[:, bs, t:t + 1].broadcast_to([128, HB, t]), ALU.mult).then_inc(s_T, 1)

            def shift(k, bs, n):
                m, f = rowmax[:, bs], fct8[:, bs, k:k + 1].rearrange("p b k -> p (b k)")
                dve.tensor_tensor(m, m, f, ALU.add).then_inc(s_shift, 1)
                dve.wait_ge(s_shift, 2 * n + 1)
                dve.tensor_tensor(m, m, f, ALU.subtract).then_inc(s_shift, 1)
                dve.wait_ge(s_shift, 2 * n + 2)

            def softmax_logits(k):
                W = T8 * (k + 1)
                e = E[:, k, :].rearrange("p (b j) -> p b j", j=NS)
                if k == 0:
                    dve.wait_ge(s_const, 3)
                    dve.wait_ge(s_fct8, 1)
                dve.wait_ge(s_S, 2 * T8 * (k + 1))
                if k == NK - 1:
                    return
                S = ps[:, 4:8, 0:GB * W].rearrange("p c (b j) -> p c b j", j=W)
                dve.tensor_reduce(rowmax[:, :].rearrange("p (c b) -> p c b", c=CH), S, AX.X, ALU.max).then_inc(s_max, 1)
                dve.wait_ge(s_max, k + 1)
                shift(k, slice(0, NB), k)
                dve.tensor_tensor(e[:, :, 0:W].rearrange("p (c b) j -> p c b j", c=CH), S,
                                  rowmax[:, :].rearrange("p (c b) -> p c b", c=CH).unsqueeze(3).broadcast_to([128, CH, GB, W]),
                                  ALU.subtract).then_inc(s_sub, 1)

            def last_part(c, part):
                k, bs = NK - 1, slice(c * GB, (c + 1) * GB)
                e = E[:, k, c * CW:(c + 1) * CW].rearrange("p (b j) -> p b j", j=NS)
                if part == 0:
                    S = ps[:, 4 + c, 0:CW].rearrange("p (b j) -> p b j", j=NS)
                    dve.tensor_reduce(rowmax[:, bs], S, AX.X, ALU.max).then_inc(s_max, 1)
                    dve.wait_ge(s_max, NK + c)
                    shift(k, bs, k + c)
                    dve.tensor_tensor(e, S, rowmax[:, bs].unsqueeze(2).broadcast_to([128, GB, NS]),
                                      ALU.subtract).then_inc(s_sub, 1)
                else:
                    dve.wait_ge(s_exp, NK + c)
                    dve.tensor_reduce(rowsum[:, k, bs], e, AX.X, ALU.add).then_inc(s_sum, 1)
                    dve.wait_ge(s_sum, NK + c)
                    dve.reciprocal(rinv[:, k, bs], rowsum[:, k, bs]).then_inc(s_rinv, 1)

            def softmax_sum(k):
                W = T8 * (k + 1)
                e = E[:, k, :].rearrange("p (b j) -> p b j", j=NS)
                dve.wait_ge(s_exp, k + 1)
                dve.tensor_reduce(rowsum[:, k, :], e[:, :, 0:W], AX.X, ALU.add).then_inc(s_sum, 1)
                dve.wait_ge(s_sum, k + 1)
                dve.reciprocal(rinv[:, k, :], rowsum[:, k, :]).then_inc(s_rinv, 1)

            for half in range(2):
                step_T(1, half)
            beta_w()
            for t in range(1, NS):
                if t == GATES_T:
                    gates()
                if t == FCT_T:
                    gates_by_query()
                for half in range(2):
                    bs = slice(half * HB, (half + 1) * HB)
                    x = Xw[:, half, 0:HB * t]
                    dve.wait_ge(s_U, 2 * (t - 1) + half + 1)
                    dve.tensor_tensor(x.rearrange("p (c b j) -> p c b j", c=2, j=t),
                                      ps[:, 2 * half:2 * half + 2, 0:GB * t].rearrange("p c (b j) -> p c b j", j=t),
                                      BW[:, bs, t:t + 1].rearrange("p (c b) n -> p c b n", c=2).broadcast_to([128, 2, GB, t]),
                                      ALU.mult).then_inc(s_X, 1)
                    dve.wait_ge(s_X, 2 * (t - 1) + half + 1)
                    dve.wait_ge(s_Tq, 2 * (t - 1) + half + 1)
                    dve.tensor_tensor(K[:, bs, 0:t], K[:, bs, 0:t], x.rearrange("p (b j) -> p b j", j=t),
                                      ALU.subtract).then_inc(s_K, 1)
                    if t + 1 < NS:
                        step_T(t + 1, half)
                if t % T8 == 0:
                    softmax_logits(t // T8 - 1)
                if t % T8 == 2 and t > T8:
                    softmax_sum(t // T8 - 1)
            softmax_logits(NK - 1)
            last_part(0, 0)
            last_part(1, 0)
            last_part(0, 1)
            last_part(2, 0)
            last_part(3, 0)

            dve.wait_ge(s_S, 2 * NS)

            def body_a(i, u):
                for c in range(1, CH):
                    if at(i, 3 * (c - 1) + 1):
                        last_part(c, 1)
                if live(i, NT):
                    if not isinstance(i, int):
                        dve.wait_ge(s_rinv, NK + CH - 1)
                    elif i % 4 == 0:
                        dve.wait_ge(s_rinv, NK + i // 4)
                    if past(i, 2):
                        dve.wait_ge(a_tr, i - 1)
                    dve.tensor_tensor(pa[:, u % 2, :].rearrange("p (k b j) -> p k b j", k=NK, b=2),
                                      E[:, :, bass.ts(i, TP)].rearrange("p k (b j) -> p k b j", b=2),
                                      rinv[:, :, bass.ts(i, 2)].unsqueeze(3).broadcast_to([128, NK, 2, NS]),
                                      ALU.mult).then_inc(a_ps, 1)
                j = i - 4
                if live(j, NT):
                    y, x1 = stage[0:TP, (u - 4) % 4, 0, :], stage[0:TP, (u - 4) % 4, 1, :]
                    dve.wait_ge(a_rs, j + 1)
                    if past(j, 4):
                        dve.wait_ge(a_rb, j - 3)
                    dve.tensor_scalar(x1, y, stat(u - 4, MV1), stat(u - 4, RS1), ALU.subtract, ALU.mult).then_inc(a_x1, 1)
                j = i - 3
                if live(j, NT):
                    y = stage[0:TP, (u - 3) % 4, 0, :]
                    dve.wait_ge(a_wo, j + 1)
                    dve.tensor_tensor(y, ps[0:TP, 6, 0:D], res[:, bass.ds(j, 1), :].rearrange("p i d -> p (i d)"), ALU.add).then_inc(a_y, 1)
                    dve.wait_ge(a_y, j + 1)
                    dve.bn_stats(stat(u - 3, ST1, 6), y).then_inc(a_st, 1)
                    dve.wait_ge(s_vev, 2)
                    dve.wait_ge(a_st, j + 1)
                    dve.bn_aggr(stat(u - 3, MV1, 2), stat(u - 3, ST1, 6)).then_inc(a_mv, 1)

            pipeline(dve, NT, 4, 8, 4, body_a)

            def normalise(i, u):
                j = i - 3
                if live(j, NT):
                    dve.wait_ge(b_exp, j + 1)
                    dve.reciprocal(stat(u - 3, RDN, 1, QP), stat(u - 3, DEN, 1, QP)).then_inc(b_rd, 1)
                    dve.wait_ge(b_rd, j + 1)
                    dve.wait_ge(b_pv, j + 1)
                    if past(j, 2):
                        dve.wait_ge(b_ont, j - 1)
                    dve.tensor_scalar(onx[:, (u - 3) % 2, :], ps[0:QP, 6, 0:D], stat(u - 3, RDN, 1, QP), None,
                                      ALU.mult).then_inc(b_on, 1)

            def residual(i, u, y):
                j = i - 4
                if live(j, NT):
                    dve.wait_ge(b_wv, j + 1)
                    dve.tensor_tensor(y, ps[0:TP, 7, 256:384], res[:, bass.ds(j, 1), :].rearrange("p i d -> p (i d)"), ALU.add).then_inc(b_y, 1)
                    dve.wait_ge(b_y, j + 1)
                    dve.bn_stats(stat(u, ST1, 6), y).then_inc(b_st, 1)
                    dve.wait_ge(s_vev, 2)
                    dve.wait_ge(b_st, j + 1)
                    dve.bn_aggr(stat(u, MV1, 2), stat(u, ST1, 6)).then_inc(b_mv, 1)

            def body_b(i, u):
                y, x2, h = (stage[0:TP, u % 4, k, :] for k in range(3))
                if live(i, NT):
                    dve.wait_ge(b_qte, i + 1)
                    dve.tensor_copy(stat(u, QB, 1, QP), ps[0:QP, 7, TP:TP + 1]).then_inc(b_qb, 1)
                for q in (1, 3, 5):
                    if live(i, NT):
                        dve.wait_ge(b_ct, 6 * i + q + 1)
                        if q == 1 and past(i, 2):
                            dve.wait_ge(b_sc, i - 1)
                        b, t = q // 3, q % 3
                        dve.tensor_copy(cT[:, u % 2, b * NCTX + t * 4 * CR:b * NCTX + (t + 1) * 4 * CR],
                                        ps[:, 4, 0:4 * CR]).then_inc(b_ctd, 1)
                    if q == 3:
                        normalise(i, u)
                        residual(i, u, y)

                j = i - 1
                if live(j, NT):
                    dve.wait_ge(b_sc, j + 1)
                    dve.tensor_reduce(stat(u - 1, MX, 1, QP), ps[0:QP, 0:3, 0:4 * CR], AX.XY, ALU.max).then_inc(b_mx, 1)
                    dve.wait_ge(b_mx, j + 1)
                    dve.tensor_scalar(stat(u - 1, M2, 1, QP), stat(u - 1, MX, 1, QP), stat(u - 1, QB, 1, QP), None,
                                      ALU.add).then_inc(b_m2, 1)
                    dve.wait_ge(b_m2, j + 1)
                    dve.tensor_scalar(stat(u - 1, NBI, 1, QP), stat(u - 1, M2, 1, QP), stat(u - 1, QB, 1, QP), -SCALE_D,
                                      ALU.subtract, ALU.mult).then_inc(b_nb, 1)
                j = i - 2
                if live(j, NT):
                    dve.wait_ge(b_ptr, 3 * j + 3)
                    if past(j, 2):
                        dve.wait_ge(b_pv, j - 1)
                    dve.tensor_copy(pxT[0:CR, u % 2, 2 * 4 * QP:], ps[0:CR, 5, 0:4 * QP]).then_inc(b_ptd, 1)
                j = i - 4
                if live(j, NT):
                    dve.wait_ge(b_rs, j + 1)
                    if past(j, 4):
                        dve.wait_ge(b_rb, 2 * (j - 3))
                    dve.tensor_scalar(x2, y, stat(u, MV1), stat(u, RS1), ALU.subtract, ALU.mult).then_inc(b_x2, 1)
                    dve.wait_ge(b_x2, j + 1)
                    dve.bn_stats(stat(u, ST2, 6), x2).then_inc(b_st2, 1)
                    dve.wait_ge(s_vev, 2)
                    dve.wait_ge(b_st2, j + 1)
                    dve.bn_aggr(stat(u, MV2, 2), stat(u, ST2, 6)).then_inc(b_mv2, 1)
                    dve.wait_ge(b_rs2, j + 1)
                    if past(j, 4):
                        dve.wait_ge(b_ht, j - 3)
                    dve.tensor_scalar(h, x2, stat(u, MV2), stat(u, RS2), ALU.subtract, ALU.mult).then_inc(b_h, 1)

            def upper(e, u):
                dve.wait_ge(m_w[u], 16 * (e - u) + 32)
                if past(e, 2):
                    dve.wait_ge(m_wh, e - 1)
                    dve.wait_ge(m_wl, e - 1)
                dve.tensor_scalar(w1m[:, u, :].bitcast(I32), w1r[:, u, :].bitcast(I32), UPPER, None,
                                  ALU.bitwise_and).then_inc(m_wm, 1)

            def body_c(i, u):
                if live(i, NT):
                    dve.wait_ge(c_q, i + 1)
                    if past(i, 2):
                        dve.wait_ge(c_sc, i - 1)
                    dve.scalar_tensor_tensor(km[:, u % 2, :, :], ps[:, 0, TP:2 * TP].unsqueeze(1).broadcast_to([128, 4, TP]), FK,
                                             quad_mask[:, :].unsqueeze(2).broadcast_to([128, 4, TP]), ALU.add, ALU.mult)\
                        .then_inc(c_km, 1)
                    if past(i, 4):
                        dve.wait_ge(c_pv, i - 3)
                    if at(i, 0):
                        dve.wait_ge(c_zero, 1)
                    dve.tensor_tensor(vpf[0:TP, u % 4, :, :].rearrange("p b (k c) -> p b k c", c=48)[:, :, :, 0:2 * HD],
                                      ps[0:TP, 0, 2 * TP:2 * TP + 2 * D].rearrange("p (b k c) -> p b k c", b=2, c=2 * HD),
                                      half_mask[:, :].unsqueeze(1).unsqueeze(1).broadcast_to([TP, 2, 8, 2 * HD]),
                                      ALU.mult).then_inc(c_vp, 1)
                j = i - 4
                y, h = stage[0:TP, u % 4, 0, :], stage[0:TP, u % 4, 2, :]
                if live(j, NT):
                    dve.wait_ge(b_rb, 2 * NT)
                    dve.wait_ge(c_wo, j + 1)
                    if past(j, 4):
                        dve.wait_ge(c_acc, j - 3)
                    dve.tensor_tensor(y, ps[0:TP, 7, 128:256], res[:, bass.ds(j, 1), :].rearrange("p i d -> p (i d)"), ALU.add).then_inc(c_y, 1)
                    dve.wait_ge(c_y, j + 1)
                    dve.bn_stats(stat(u, ST1, 6), y).then_inc(c_st, 1)
                    dve.wait_ge(s_vev, 2)
                    dve.wait_ge(c_st, j + 1)
                    dve.bn_aggr(stat(u, MV1, 2), stat(u, ST1, 6)).then_inc(c_mv, 1)
                j = i - 6
                if live(j, NT):
                    dve.wait_ge(c_hte, j + 1)
                    if past(j, 2):
                        dve.wait_ge(c_xl, j - 1)
                        dve.wait_ge(c_xh, j - 1)
                    dve.tensor_scalar(xm[:, u % 2, :].bitcast(I32), h2s[:, (u - 6) % 4, :].bitcast(I32), UPPER, None,
                                      ALU.bitwise_and).then_inc(c_xm, 1)
                j = i - 1
                p = pf[0:QP, (u - 1) % 2, :]
                if live(j, NT):
                    sc = ps[0:QP, 1:5, 0:4 * NS].rearrange("p g (h j) -> p g h j", j=NS)
                    dve.wait_ge(c_sc, j + 1)
                    dve.tensor_reduce(stat(u - 1, HMX, H, QP).rearrange("p (g h) -> p g h", g=4), sc, AX.X, ALU.max).then_inc(c_mx, 1)
                    dve.wait_ge(c_mx, j + 1)
                    if past(j, 2):
                        dve.wait_ge(c_ptr, j - 1)
                    dve.tensor_tensor(p.rearrange("p (g h j) -> p g h j", g=4, j=NS), sc,
                                      stat(u - 1, HMX, H, QP).rearrange("p (g h) -> p g h", g=4).unsqueeze(3)
                                      .broadcast_to([QP, 4, 4, NS]), ALU.subtract).then_inc(c_sub, 1)
                j = i - 6
                if live(j, NT):
                    dve.wait_ge(c_gt, j + 1)
                    dve.tensor_tensor(lg[:, bass.ds(j, 1), :].rearrange("p i d -> p (i d)"), ps[0:TP, 0, 480:480 + NE], GBR, ALU.add).then_inc(c_lg, 1)
                j = i - 4
                if live(j, NT):
                    dve.wait_ge(c_rs, j + 1)
                    if past(j, 4):
                        dve.wait_ge(c_ht, j - 3)
                    dve.tensor_scalar(h, y, stat(u, MV1), stat(u, RS1), ALU.subtract, ALU.mult).then_inc(c_h, 1)
                j = i - 1
                if live(j, NT):
                    dve.wait_ge(c_exp, j + 1)
                    dve.tensor_reduce(stat(u - 1, HSM, H, QP), p.rearrange("p (h j) -> p h j", j=NS), AX.X, ALU.add).then_inc(c_sum, 1)
                    dve.wait_ge(c_sum, j + 1)
                    dve.reciprocal(stat(u - 1, HRI, H, QP), stat(u - 1, HSM, H, QP)).then_inc(c_ri, 1)

            pipeline(dve, NT, 5, 8, 4, body_b, following=lambda k: body_c(k, k))
            dve.wait_ge(b_pv, NT)
            for e in range(2):
                upper(e, e)
            pipeline(dve, NT, 6, 8, 4, body_c, first=FILL)

            links = [0]

            def link(ins):
                links[0] += 1
                ins.then_inc(m_link, 1)
                dve.wait_ge(m_link, links[0])

            dve.wait_ge(c_lg, NT)

            def wide(x):
                return x.unsqueeze(2).broadcast_to([TP, NT, NE])

            iota_w = iota8[:, :].unsqueeze(1).broadcast_to([TP, NT, NE])
            eq, val, one1, l2, one2 = (gt[:, k, :, :] for k in range(5))

            def largest(logits, top, one):
                link(dve.tensor_reduce(top, logits, AX.X, ALU.max))
                link(dve.tensor_tensor(eq, logits, wide(top), ALU.is_equal))
                link(dve.scalar_tensor_tensor(val, eq, -float(NE), iota_w, ALU.mult, ALU.add))
                link(dve.tensor_reduce(gs[:, 5, :], val, AX.X, ALU.min))
                link(dve.tensor_tensor(one, val, wide(gs[:, 5, :]), ALU.is_equal))

            largest(lg[:, :, :], gs[:, 0, :], one1)
            link(dve.scalar_tensor_tensor(l2, one1, NEG, lg[:, :, :], ALU.mult, ALU.add))
            largest(l2, gs[:, 1, :], one2)
            link(dve.tensor_tensor(gs[:, 4, :], gs[:, 1, :], gs[:, 0, :], ALU.subtract))
            dve.wait_ge(m_e, 1)
            link(dve.tensor_scalar(gs[:, 2, :], gs[:, 4, :], 1.0, None, ALU.add))
            link(dve.reciprocal(gs[:, 3, :], gs[:, 2, :]))
            link(dve.tensor_tensor(gs[:, 2, :], gs[:, 4, :], gs[:, 3, :], ALU.mult))
            link(dve.tensor_tensor(one1, one1, wide(gs[:, 3, :]), ALU.mult))
            link(dve.tensor_tensor(one2, one2, wide(gs[:, 2, :]), ALU.mult))
            dve.tensor_tensor(ew[:, :, :], one1, one2, ALU.add).then_inc(m_ew, 1)
            stats = gt[:, 2:4, :, :].rearrange("p k i e -> p (k i e)")

            def last_norm(c):
                four = range(4 * c, 4 * c + 4)
                for i in four:
                    dve.wait_ge(m_acc, 4 * ((NE - 1) * CH + c + 1))
                    dve.bn_stats(stats[:, 6 * i:6 * i + 6], acc[:, i, :]).then_inc(f_st, 1)
                for i in four:
                    dve.wait_ge(f_st, i + 1)
                    dve.bn_aggr(gt[:, 1, i, 0:2], stats[:, 6 * i:6 * i + 6]).then_inc(f_mv, 1)
                for i in four:
                    dve.wait_ge(f_mv, i + 1)
                    dve.wait_ge(f_rs, c + 1)
                    dve.tensor_scalar(acc[:, i, :], acc[:, i, :], gt[:, 1, i, 0:1], gs[:, 2, i:i + 1],
                                      ALU.subtract, ALU.mult).then_inc(f_y, 1)

            def weigh(e, c):
                n = e * CH + c
                dve.wait_ge(m_out, n + 1)
                if past(n, CH):
                    dve.wait_ge(m_acc, 4 * (n - 3))
                for k in range(4):
                    t = acc[:, 4 * c + k, :]
                    dve.scalar_tensor_tensor(t, ps[0:TP, 5 + c % 2, k * D:(k + 1) * D],
                                             ew[:, 4 * c + k, bass.ds(e, 1)], t, ALU.mult, ALU.add).then_inc(m_acc, 1)

            def spread(c):
                dve.wait_ge(m_ewt, c + 1)
                dve.tensor_copy(ewT[:, c * CW:(c + 1) * CW], ps[0:NE, 7 * (1 - c % 2), 0:CW]).then_inc(m_ewe, 1)

            def second_bias(c):
                dve.wait_ge(m_b2, c + 1)
                dve.wait_ge(m_acc, 4 * (c + 1))
                t = acc[:, 4 * c:4 * c + 4, :]
                dve.tensor_tensor(t, t, ps[0:TP, 7 * (1 - c % 2), :].rearrange("p (i d) -> p i d", d=D), ALU.add).then_inc(m_acc0, 1)

            dve.wait_ge(c_acc, NT)
            dve.wait_ge(m_ew, 1)
            weigh(0, 0)
            spread(0); spread(1)
            weigh(0, 1)
            spread(2); spread(3)
            weigh(0, 2)
            weigh(0, 3)
            second_bias(0); second_bias(1)
            upper(2, 0)
            dve.wait_ge(m_acc0, 1)
            weigh(1, 0)
            second_bias(2); second_bias(3)
            for c in range(1, CH):
                dve.wait_ge(m_acc0, c + 1)
                weigh(1, c)
            for u in range(2):
                upper(3 + u, 1 - u)
                for c in range(CH):
                    weigh(2 + u, c)
            with dve.Fori(2, NE // 2 - 1, 1) as r:
                for u in range(2):
                    upper(r * 2 + u + 1, 1 - u)
                    for c in range(CH):
                        weigh(r * 2 + u, c)
            upper(NE - 1, 1)
            for e in range(NE - 2, NE):
                for c in range(CH):
                    weigh(e, c)
                    if e == NE - 1:
                        last_norm(c)

        @block.tensor
        def _(pe):
            pe.wait_ge(s_const, 1)
            pe.wait_ge(s_x, 16)
            for c in range(CH):
                for i in range(4):
                    last = pe.transpose(ps[:, c, i * TP:(i + 1) * TP], res[:, 4 * c + i, :], ident[0:TP, 0:TP])
                last.then_inc(s_pe0, 1)

            def project(w, src, bank, evacuated, need):
                for c in range(CH):
                    pe.wait_ge(evacuated, need + c)
                    pe.matmul(ps[0:w.shape[1], bank + c, 0:CW], w, src[0:w.shape[0], c * CW:(c + 1) * CW],
                              start=True, stop=True).then_inc(s_pe0, 1)

            pe.wait_ge(s_w1, NW1)
            project(ww1[:, :], xT, 4, s_ev0, 1)
            project(ww2[:, :], tmpA, 0, s_ev0, 5)
            pe.wait_ge(s_rep, 2)
            project(wb_rep[:, :], xT, 4, s_ev0, 5)
            pe.wait_ge(s_const, 2)
            project(blockones[:, :], tmpB, 0, s_sq, 1)
            project(wk[:, :], xT, 4, s_ev0, 9)
            project(wq[:, :], xT, 0, s_ev0, 13)
            project(wf_rep[:, :], xT, 4, s_wk, 5)
            pe.wait_ge(s_ev0, 24)

            def gates_by_query_pe():
                pe.wait_ge(s_dve0, 4)
                F = fcT[:, :].rearrange("p (b k t) -> p b k t", k=NK, t=T8)
                for t in range(T8):
                    mm = pe.matmul(ps[:, 0, FCT0:], fc_win[:, (7 - t) * H:(15 - t) * H], F[:, :, :, t],
                                   start=(t == 0), stop=(t == T8 - 1))
                mm.then_inc(s_fct, 1)
                pe.wait_ge(s_fct8, 1)

            def weights_pe():
                pe.wait_ge(s_w2, NW2)
                pe.transpose(ps[:, 1, 2 * D:3 * D], xw[:, 0, :], ident[:, :])
                pe.transpose(ps[:, 1, 3 * D:4 * D], xw[:, 1, :], ident[:, :]).then_inc(s_prep, 1)
                pe.wait_ge(s_prep_ev, 2)

            def rows_pe():
                pe.transpose(ps[:, 2, 2 * D:2 * D + NE * FC], b1_nat[:, :], ident[0:NE * FC, 0:NE * FC])
                pe.matmul(ps[0:TP, 3, ROW0:], ones_row[:, :], rows[:, :], start=True, stop=True).then_inc(s_prep, 1)
                pe.wait_ge(s_prep_ev, 4)

            def reduce_U(t, half):
                pe.wait_ge(s_T, 2 * (t - 1) + half + 1)
                if t == FCT_T and half == 0:
                    gates_by_query_pe()
                if t == PREP_T:
                    rows_pe() if half else weights_pe()
                for c in range(2):
                    mm = pe.matmul(ps[:, 2 * half + c, 0:GB * t], blockones[:, :],
                                   Tw[:, half, c * GB * t:(c + 1) * GB * t], start=True, stop=True)
                mm.then_inc(s_U, 1)

            def reduce_S(t, half):
                k, W = t // T8, T8 * (t // T8 + 1)
                if t % T8 == 0 and k > 0:
                    pe.wait_ge(s_sub, k)
                pe.wait_ge(s_Tq, 2 * t + half + 1)
                for c in range(2):
                    mm = pe.matmul(ps[:, 4 + 2 * half + c, 0:GB * W], head_win[:, (7 - t % T8) * H:(15 - t % T8) * H],
                                   Tq[:, half, t % 2, c * GB * W:(c + 1) * GB * W],
                                   start=(t % T8 == 0), stop=False)
                if t % T8 == T8 - 1:
                    for c in range(2 * half, 2 * half + 2):
                        pe.matmul(ps[:, 4 + c, 0:GB * W], fc_neg[:, :], tok(fcT)[:, c * GB:(c + 1) * GB, 0:W],
                                  start=False, stop=False)
                        mm = pe.matmul(ps[:, 4 + c, 0:GB * W].rearrange("p (b j) -> p b j", j=W)[:, :, T8 * k:W], ident[:, :],
                                       causal8[:, :].unsqueeze(1).broadcast_to([128, GB, T8]), start=False, stop=True)
                mm.then_inc(s_S, 1)

            for t in range(NS):
                for half in range(2):
                    if t + 1 < NS:
                        reduce_U(t + 1, half)
                    reduce_S(t, half)

            pe.wait_ge(s_X, 2 * (NS - 1))
            for i in range(NT):
                mm = pe.matmul(ps[0:TP, i // 4, (i % 4) * D:(i % 4 + 1) * D], xT[:, i * TP:(i + 1) * TP], wv[:, :],
                               start=True, stop=True)
                if i % 8 == 7:
                    mm.then_inc(s_v, 1)
            pe.wait_ge(s_sub, NK + CH - 1)
            pe.wait_ge(s_vev, 2)

            def body_a(i, u):
                if live(i, NT):
                    pe.wait_ge(a_ps, i + 1)
                    if past(i, 2):
                        pe.wait_ge(a_pt, i - 1)
                    for k in range(NK):
                        mm = pe.transpose(ps[0:TP, 2 * (u % 2) + k // 4, (k % 4) * 128:(k % 4 + 1) * 128],
                                          pa[:, u % 2, k * TP:(k + 1) * TP], ident[:, :])
                    mm.then_inc(a_tr, 1)
                j = i - 2
                if live(j, NT):
                    pe.wait_ge(a_o, j + 1)
                    if past(j, 1):
                        pe.wait_ge(a_y, j)
                    pe.matmul(ps[0:TP, 6, 0:D], oTa[:, u % 2, :], wo[:, :], start=True, stop=True).then_inc(a_wo, 1)
                j = i - 5
                if live(j, NT):
                    pe.wait_ge(a_xe, j + 1)
                    pe.matmul(ps[:, 7, 128:128 + TP], xwqT[:, :], xT[:, bass.ts(j, TP)], start=True, stop=True).then_inc(b_qx, 1)
                j = i - 1
                if live(j, NT):
                    v = (u - 1) % 2
                    pe.wait_ge(a_pt, j + 1)
                    pe.wait_ge(a_vp, 2 * (j + 1))
                    if past(j, 2):
                        pe.wait_ge(a_o, j - 1)
                    for b in range(2):
                        for hh in range(4):
                            for g in range(4):
                                h = 4 * g + hh
                                mm = pe.matmul(ps[32 * g:32 * g + 32, 4 + v, b * NS:(b + 1) * NS],
                                               vpa[0:TP, v, b, g * 160 + hh * 32:g * 160 + hh * 32 + 32],
                                               paT[0:TP, v, h:NK * 128:H], start=(hh == 0), stop=(hh == 3),
                                               tile_position=(0, 32 * g))
                    mm.then_inc(a_pv, 1)

                j = i - 4
                if live(j, NT):
                    pe.wait_ge(a_x1, j + 1)
                    if past(j, 1):
                        pe.wait_ge(b_qxe, j)
                    pe.transpose(ps[:, 7, 0:TP], stage[0:TP, (u - 4) % 4, 1, :], ident[0:TP, 0:TP]).then_inc(a_xt, 1)

            pipeline(pe, NT, 5, 8, 4, body_a)

            pe.wait_ge(a_pt, NT)
            pe.wait_ge(a_o, NT)
            pe.wait_ge(a_y, NT)
            pe.wait_ge(b_qxe, NT)

            def outputs_b(j, uj, q):
                if live(j, NT):
                    w = uj % 2
                    if q < 2:
                        pe.wait_ge(b_pta, 2 * j + q + 1)
                    else:
                        pe.wait_ge(b_ptd, j + 1)
                    if q == 0 and past(j, 1):
                        pe.wait_ge(b_on, j)
                    for c in range(4 * q, 4 * q + 4):
                        for b in range(2):
                            mm = pe.matmul(ps[64 * b:64 * b + NS, 6, 0:D], pxT[0:CR, w, c * QP + 64 * b:c * QP + 64 * b + NS],
                                           ctxr[0:CR, uj % 4, b, c * D:(c + 1) * D],
                                           start=(c == 0), stop=(c == NCC - 1))
                    if q == 2:
                        mm.then_inc(b_pv, 1)

            def probs_b(j, v, r):
                if live(j, NT):
                    pe.wait_ge(b_exp, j + 1)
                    if r > 0:
                        pe.wait_ge(b_pta, 2 * j + r)
                    elif past(j, 1):
                        pe.wait_ge(b_ptd, j)
                    for k in range(4):
                        c = 4 * r + k
                        mm = pe.transpose(ps[0:CR, 5, k * QP:(k + 1) * QP], px[0:QP, v, c * CR:(c + 1) * CR],
                                          ident[0:QP, 0:QP])
                    mm.then_inc(b_ptr, 1)

            def body_b(i, u):
                v = u % 2
                if live(i, NT):
                    pe.wait_ge(b_qxs, i + 1)
                    if not isinstance(i, int) or i >= 6:
                        pe.wait_ge(b_hte, i - 5)
                    if live(i - 5, NT):
                        pe.wait_ge(b_y, i - 4)
                    pe.matmul(ps[:, 7, 0:TP], xw[:, 2, :], qxs[:, v, :], start=True, stop=True)
                    for b in range(2):
                        mm = pe.matmul(ps[64 * b:64 * b + NS, 7, TP:TP + 1], qxs[:, v, b * NS:(b + 1) * NS], BK,
                                       start=True, stop=True)
                    mm.then_inc(b_qt, 1)
                for q in range(6):
                    b, t = q // 3, q % 3
                    if live(i, NT):
                        if q == 0:
                            pe.wait_ge(b_ctx[u], 4 * (i - u) + 16)
                        evacuated = b_ctd if q % 2 else b_cta
                        if q >= 2 or past(i, 1):
                            pe.wait_ge(evacuated, 3 * i + q // 2)
                        for k in range(4):
                            c = 4 * t + k
                            mm = pe.transpose(ps[:, 3 + q % 2, k * CR:(k + 1) * CR], ctxr[0:CR, u, b, c * D:(c + 1) * D],
                                              ident[0:CR, 0:CR])
                        mm.then_inc(b_ct, 1)
                    if q == 5:
                        probs_b(i - 2, v, 0)
                    j = i - 1
                    if q % 2 == 1 and live(j, NT):
                        if q == 1:
                            pe.wait_ge(b_cta, 3 * (j + 1))
                            pe.wait_ge(b_ctd, 3 * (j + 1))
                            pe.wait_ge(b_qte, j + 1)
                            if past(j, 1):
                                pe.wait_ge(b_exp, j)
                        w, t = (u - 1) % 2, q // 2
                        for b in range(2):
                            mm = pe.matmul(ps[64 * b:64 * b + NS, t, 0:4 * CR], qts[:, w, b * NS:(b + 1) * NS],
                                           cT[:, w, b * NCTX + t * 4 * CR:b * NCTX + (t + 1) * 4 * CR], start=True, stop=True)
                        if q == 5:
                            mm.then_inc(b_sc, 1)
                    j = i - 4
                    if q == 2 and live(j, NT):
                        pe.wait_ge(b_on, j + 1)
                        if live(i, NT):
                            pe.wait_ge(b_qte, i + 1)
                            pe.wait_ge(b_qb, i + 1)
                        else:
                            pe.wait_ge(b_hte, i - 5)
                        pe.transpose(ps[:, 7, 128:128 + QP], onx[:, v, :], ident[0:QP, 0:QP]).then_inc(b_ont, 1)
                    if q == 2:
                        outputs_b(i - 3, u - 3, 2)
                    if q == 4 and live(j, NT):
                        pe.wait_ge(b_one, j + 1)
                        pe.matmul(ps[0:TP, 7, 256:384], oxT[:, v, :], xwvT[:, :], start=True, stop=True).then_inc(b_wv, 1)
                j = i - 5
                if live(j, NT):
                    pe.wait_ge(b_h, j + 1)
                    if live(i - 4, NT):
                        pe.wait_ge(b_y, i - 3)
                    elif past(j, 1):
                        pe.wait_ge(b_hte, j)
                    pe.transpose(ps[:, 7, 384:384 + TP], stage[0:TP, (u - 5) % 4, 2, :], ident[0:TP, 0:TP]).then_inc(b_ht, 1)
                for r in range(1, 3):
                    probs_b(i - 2, v, r)
                    outputs_b(i - 2, u - 2, r - 1)

            def hidden(e, u, c):
                n = e * CH + c
                if c == 0:
                    pe.wait_ge(m_wl, e + 1)
                    pe.wait_ge(m_wh, e + 1)
                for f in range(FC):
                    if past(n, 1):
                        pe.wait_ge(m_relu, FC * (n - 1) + f + 1)
                    for part, (w, x) in enumerate(((w1h, xh), (w1h, xl), (w1l, xh))):
                        mm = pe.matmul(ps[:, 1 + f, 0:CW], w[:, u, f * 128:(f + 1) * 128],
                                       x[:, c * CW:(c + 1) * CW], start=(part == 0), stop=(part == 2))
                    mm.then_inc(m_hid, 1)

            def outputs(e, u, c):
                n = e * CH + c
                if c == 0:
                    pe.wait_ge(m_w[u], 16 * (e - u) + 32)
                pe.wait_ge(m_relu, FC * (n + 1))
                if past(n, 2):
                    pe.wait_ge(m_acc, 4 * (n - 1))
                for k in range(4):
                    for f in range(FC):
                        mm = pe.matmul(ps[0:TP, 5 + c % 2, k * D:(k + 1) * D], hid[:, c % 2, f, k * TP:(k + 1) * TP],
                                       w2r[:, u, f, :], start=(f == 0), stop=(f == FC - 1))
                mm.then_inc(m_out, 1)

            def scores_c(j, u, b):
                for g in range(4):
                    rs = slice(32 * g, 32 * g + 32)
                    mm = pe.matmul(ps[64 * b:64 * b + NS, 1 + g, 0:4 * NS], qs[rs, u % 2, b * NS:(b + 1) * NS],
                                   km[rs, u % 2, :, b * NS:(b + 1) * NS], start=True, stop=True,
                                   tile_position=(32 * g, 64 * b))
                if b == 1:
                    mm.then_inc(c_sc, 1)

            def body_c(i, u):
                v = u % 2
                if at(i, 0):
                    pe.wait_ge(b_exp, NT)
                if at(i, 2):
                    pe.wait_ge(b_ptd, NT)
                    pe.wait_ge(b_on, NT)
                if at(i, 3):
                    pe.wait_ge(b_hte, NT)
                    pe.wait_ge(b_y, NT)
                if live(i, NT):
                    pe.wait_ge(c_hs, i + 1)
                    if past(i, 1):
                        pe.wait_ge(c_q, i)
                        pe.wait_ge(c_km, i)
                        pe.wait_ge(c_vp, i)
                    if live(i - 6, NT):
                        pe.wait_ge(c_hte, i - 5)
                    if live(i - 7, NT):
                        pe.wait_ge(c_lg, i - 6)
                    h1 = hs[:, u % 4, :, 0:NS]
                    pe.matmul(ps[:, 0, 0:TP], wqkv[:, 0:D], h1, start=True, stop=True)
                    pe.matmul(ps[:, 0, TP:2 * TP], wqkv[:, D:2 * D], h1, start=True, stop=True)
                    for b in range(2):
                        mm = pe.matmul(ps[0:TP, 0, 2 * TP + b * D:2 * TP + (b + 1) * D], hs[:, u % 4, b, :], wqkv[:, 2 * D:3 * D],
                                       start=True, stop=True)
                    mm.then_inc(c_qkv, 1)
                j = i - 1
                if live(j, NT):
                    pe.wait_ge(c_q, j + 1)
                    pe.wait_ge(c_km, j + 1)
                    if past(j, 1):
                        pe.wait_ge(c_sub, j)
                    scores_c(j, u - 1, 0)
                j = i - 4
                if live(j, NT):
                    pe.wait_ge(c_o, j + 1)
                    pe.matmul(ps[0:TP, 7, 128:256], ofT[:, v, :], w_o[:, :], start=True, stop=True).then_inc(c_wo, 1)
                j = i - 1
                if live(j, NT):
                    scores_c(j, u - 1, 1)
                j = i - 5
                if live(j, NT):
                    pe.wait_ge(c_h, j + 1)
                    if live(i, NT):
                        pe.wait_ge(c_vp, i + 1)
                        pe.wait_ge(c_q, i + 1)
                        pe.wait_ge(c_km, i + 1)
                    elif past(j, 2):
                        pe.wait_ge(c_lg, j - 1)
                    pe.transpose(ps[:, 0, 0:TP], stage[0:TP, (u - 5) % 4, 2, :], ident[0:TP, 0:TP]).then_inc(c_ht, 1)
                j = i - 2
                if live(j, NT):
                    pe.wait_ge(c_nrm, j + 1)
                    if past(j, 1):
                        pe.wait_ge(c_pte, j)
                    for k in range(8):
                        mm = pe.transpose(ps[0:TP, 5 + k // 4, (k % 4) * QP:(k % 4 + 1) * QP], pf[0:QP, v, k * TP:(k + 1) * TP],
                                          ident[0:QP, 0:QP])
                    mm.then_inc(c_ptr, 1)
                j = i - 6
                if live(j, NT):
                    pe.wait_ge(c_hte, j + 1)
                    if live(i - 5, NT):
                        pe.wait_ge(c_hte, i - 4)
                    elif past(j, 1):
                        pe.wait_ge(c_lg, j)
                    pe.matmul(ps[0:TP, 0, 480:480 + NE], h2s[:, (u - 6) % 4, :], gate_w[:, :], start=True, stop=True).then_inc(c_gt, 1)
                j = i - 3
                if live(j, NT):
                    w = (u - 3) % 2
                    pe.wait_ge(c_pte, j + 1)
                    pe.wait_ge(c_vp, j + 1)
                    if live(i - 4, NT):
                        pe.wait_ge(c_y, i - 3)
                    for b in range(2):
                        for s in range(2):
                            for g in range(4):
                                k = 2 * g + s
                                mm = pe.matmul(ps[32 * g:32 * g + 32, 7, b * NS:(b + 1) * NS],
                                               vpf[0:TP, (u - 3) % 4, b, g * 96 + s * 32:g * 96 + s * 32 + 32],
                                               pfT[0:TP, w, k * QP + 64 * b:k * QP + 64 * b + NS],
                                               start=(s == 0), stop=(s == 1), tile_position=(0, 32 * g))
                    mm.then_inc(c_pv, 1)

                if at(i, NT + 2):
                    pe.wait_ge(c_sub, NT)
                    pe.wait_ge(c_xh, 4)
                    pe.wait_ge(c_xl, 4)
                    hidden(0, 0, 0)
                if at(i, NT + 4):
                    pe.wait_ge(c_xh, 8)
                    pe.wait_ge(c_xl, 8)
                    hidden(0, 0, 1)
                    pe.wait_ge(c_pte, NT)
                    outputs(0, 0, 0)

            pipeline(pe, NT, 5, 8, 4, body_b, following=lambda k: body_c(k, k))
            pipeline(pe, NT, 6, 8, 4, body_c, first=FILL)

            def spread_pe(c):
                for i in range(4):
                    mm = pe.transpose(ps[0:NE, 7 * (1 - c % 2), i * TP:(i + 1) * TP], ew[:, 4 * c + i, :], ident[0:TP, 0:TP])
                mm.then_inc(m_ewt, 1)

            def second_bias_pe(c):
                for i in range(4):
                    t = 4 * c + i
                    mm = pe.matmul(ps[0:TP, 7 * (1 - c % 2), i * D:(i + 1) * D], ewT[:, t * TP:(t + 1) * TP], b2_nat[:, :],
                                   start=True, stop=True)
                mm.then_inc(m_b2, 1)

            pe.wait_ge(c_xh, NT)
            pe.wait_ge(c_xl, NT)
            pe.wait_ge(c_lg, NT)
            pe.wait_ge(c_y, NT)
            hidden(0, 0, 2)
            outputs(0, 0, 1)
            pe.wait_ge(m_ew, 1)
            spread_pe(0)
            spread_pe(1)
            hidden(0, 0, 3)
            for c in range(2, CH):
                pe.wait_ge(m_ewe, c - 1)
                spread_pe(c)
            outputs(0, 0, 2)
            hidden(1, 1, 0)
            outputs(0, 0, 3)
            pe.wait_ge(m_ewe, CH)
            second_bias_pe(0)
            second_bias_pe(1)
            hidden(1, 1, 1)
            outputs(1, 1, 0)
            for c in range(2, CH):
                pe.wait_ge(m_acc0, c - 1)
                second_bias_pe(c)
            for c in range(2, CH):
                hidden(1, 1, c)
                outputs(1, 1, c - 1)
            with pe.Fori(1, NE // 2, 1) as r:
                for u in range(2):
                    for c in range(CH):
                        hidden(r * 2 + u, u, c)
                        if c == 0:
                            outputs(r * 2 + u - 1, 1 - u, CH - 1)
                        else:
                            outputs(r * 2 + u, u, c - 1)
            outputs(NE - 1, 1, CH - 1)


_INS = ["x", "ctx_1024"] + ["L0_attn_" + n for n in ("Wq", "Wk", "Wv", "Wo", "Ww1", "Ww2", "Wb", "Wf", "delta")] + \
    ["L0_xattn_" + n for n in ("Wq", "bq", "Wk", "bk", "Wv", "bv")] + \
    ["L0_ffn_" + n for n in ("ln1_g", "ln1_b", "w_qkv", "b_qkv", "w_o", "b_o", "ln2_g", "ln2_b", "gate_w", "gate_b",
                             "W1", "b1", "W2", "b2")]


def kernel(**inputs):
    import numpy as _np
    import concourse.bacc as _bacc
    from concourse import mybir as _mybir
    from concourse.bass_utils import run_bass_kernel_spmd as _run

    nc = _bacc.Bacc("TRN2", target_bir_lowering=False, num_devices=1)
    arrays, args = {}, {}
    for name in _INS:
        v = _np.ascontiguousarray(inputs[name])
        arrays["in_" + name] = v
        args[name] = nc.dram_tensor("in_" + name, v.shape, _mybir.dt.from_np(v.dtype), kind="ExternalInput").ap()
    o = nc.dram_tensor("out_0", (NB, NS, D), _mybir.dt.float32, kind="ExternalOutput").ap()
    build(nc, args, o)
    r = _run(nc, [arrays], core_ids=[0])
    return r.results[0]["out_0"]
```
